# Optimizing a Trainium2 kernel written in Bass

```python
import numpy as np
import jax
import jax.numpy as jnp

def _softmax(x, axis=-1):
    return jax.nn.softmax(x, axis=axis)

def _gelu(x):
    return jax.nn.gelu(x, approximate=True)

def _silu(x):
    return jax.nn.silu(x)

def _sigmoid(x):
    return jax.nn.sigmoid(x)

def _layernorm(x, axis=-1, eps=1e-05):
    m = jnp.mean(x, axis=axis, keepdims=True)
    v = jnp.var(x, axis=axis, keepdims=True)
    return (x - m) / jnp.sqrt(v + eps)

def _scatter_add(tgt, idx, src, axis=0):
    return tgt.at[idx].add(src)

def _segment_sum(src, seg, n):
    return jax.ops.segment_sum(src, seg, n)
kernel_name = 'mk_lm_tower_d1_tok_ids256_r4_29ecfe'

def setup_inputs(seed: int=0):
    np.random.seed(seed)
    _w = jnp.asarray

    def _rec_inputs():
        import jax
        import jax.numpy as jnp
        _rk = jax.random.key(seed)
        x = jax.random.randint(jax.random.fold_in(_rk, 1), (32, 128), 0, 25000, jnp.int32)
        fside_BS_outcomes = jax.random.uniform(jax.random.fold_in(_rk, 21), (32, 128), jnp.float32, 0.0, 0.999994)
        fside_BS_timestamps = -0.0064186 + 0.999588 * jax.random.normal(jax.random.fold_in(_rk, 22), (32, 128), jnp.float32)
        return (x, fside_BS_outcomes, fside_BS_timestamps)
    x, fside_BS_outcomes, fside_BS_timestamps = _rec_inputs()

    def _L0_tok_setup():
        import jax, jax.numpy as jnp
        import numpy as np
        N_Q = 25000
        D = 64
        B, L = (32, 512)
        LN_EPS = 1e-05
        key = jax.random.key(seed)
        ks = jax.random.split(key, 6)
        q_idx = jax.random.randint(ks[0], (B, L), 0, N_Q, dtype=jnp.int64) if jax.config.jax_enable_x64 else jax.random.randint(ks[0], (B, L), 0, N_Q, dtype=jnp.int32)
        outcomes = jax.random.uniform(ks[1], (B, L), dtype=jnp.float32)
        timestamps = jax.random.normal(ks[2], (B, L), dtype=jnp.float32)
        h_q = jax.random.normal(ks[3], (N_Q, D), dtype=jnp.float32)
        bound = float(np.sqrt(6.0 / (D + 2 + D)))
        W_proj_w = jax.random.uniform(ks[4], (D, D + 2), minval=-bound, maxval=bound, dtype=jnp.float32)
        W_proj_b = jnp.zeros((D,), jnp.float32)
        return {'q_idx': q_idx, 'outcomes': outcomes, 'timestamps': timestamps, 'h_q': h_q, 'W_o': jnp.ones((1,), jnp.float32), 'W_dt': jnp.ones((1,), jnp.float32), 'W_proj_w': W_proj_w, 'W_proj_b': W_proj_b, 'ln_g': jnp.ones((D,), jnp.float32), 'ln_b': jnp.zeros((D,), jnp.float32)}
    _L0_tok_all = _L0_tok_setup()
    _L0_tok_in = {k: v for k, v in _L0_tok_all.items() if k in ('h_q', 'W_o', 'W_dt', 'W_proj_w', 'W_proj_b', 'ln_g', 'ln_b')}
    del _L0_tok_all

    def _L0_attn_setup():
        import jax, jax.numpy as jnp
        import numpy as np
        EPS = 1e-09

        def _glorot(key, shape):
            fan_in, fan_out = (shape[-2], shape[-1])
            std = (2.0 / (fan_in + fan_out)) ** 0.5
            return jax.random.normal(key, shape, dtype=jnp.float32) * std

        def _reference_tuple_inner(x, Wks, Wqs, Wvs, Wo):
            keys = jnp.einsum('bsd,hdk->hbsk', x, Wks)
            queries = jnp.einsum('bsd,hdk->hbsk', x, Wqs)
            values = jnp.einsum('bsd,hde->hbse', x, Wvs)
            keys = jax.nn.elu(keys) + 1.0
            queries = jax.nn.elu(queries) + 1.0
            att = jnp.einsum('hbsk,hbtk->hbst', queries, keys)
            S = att.shape[-1]
            causal = jnp.tril(jnp.ones((S, S), dtype=att.dtype))
            att = att * causal
            att = att / (jnp.sum(att, axis=-1, keepdims=True) + EPS)
            kv = jnp.einsum('hbsk,hbsd->hbsdk', keys, values)
            kv_cum = jnp.cumsum(kv, axis=2)
            numerator = jnp.einsum('hbsdk,hbsk->hbsd', kv_cum, queries)
            denominator = jnp.einsum('hbsk,hbsk->hbs', jnp.cumsum(keys, axis=2), queries)
            node = numerator / (denominator[..., None] + EPS)
            out = jnp.einsum('hbsd,hde->bse', node, Wo)
            return (out, att)
        key = jax.random.key(seed)
        kx, k1, k2, k3, k4 = jax.random.split(key, 5)
        B, S, D = (2, 256, 64)
        H, K = (8, 32)
        return {'x': jax.random.normal(kx, (B, S, D), dtype=jnp.float32), 'Wks': _glorot(k1, (H, D, K)), 'Wqs': _glorot(k2, (H, D, K)), 'Wvs': _glorot(k3, (H, D, D)), 'Wo': _glorot(k4, (H, D, D))}
    _L0_attn_all = _L0_attn_setup()
    _L0_attn_in = {k: v for k, v in _L0_attn_all.items() if k in ('Wks', 'Wqs', 'Wvs', 'Wo')}
    del _L0_attn_all

    def _L0_ffn_setup():
        import jax, jax.numpy as jnp
        import numpy as np
        B, N, D = (16, 1024, 64)
        NUM_EXPERTS, TOP_K, HEADS = (4, 2, 4)
        N_EDGES = 262144
        LN_EPS = 1e-05

        def _layernorm(x, g, b):
            mu = x.mean(-1, keepdims=True)
            var = ((x - mu) ** 2).mean(-1, keepdims=True)
            return (x - mu) * jax.lax.rsqrt(var + LN_EPS) * g + b

        def _forward(x, edge_index, W_gat, att_src, att_dst, b_gat, ln_gamma, ln_beta, W1, b1, W2, b2):
            Bc, Nc, Dc = x.shape
            M = Bc * Nc
            x_flat = x.reshape(M, Dc)
            h = (x_flat @ W_gat).reshape(M, HEADS, NUM_EXPERTS)
            loops = jnp.arange(M, dtype=edge_index.dtype)
            src = jnp.concatenate([edge_index[0], loops])
            dst = jnp.concatenate([edge_index[1], loops])
            a_src = (h * att_src).sum(-1)
            a_dst = (h * att_dst).sum(-1)
            e = jax.nn.leaky_relu(a_src[src] + a_dst[dst], negative_slope=0.2)
            e_max = jax.ops.segment_max(e, dst, num_segments=M)
            ee = jnp.exp(e - e_max[dst])
            denom = jax.ops.segment_sum(ee, dst, num_segments=M)
            alpha = ee / (denom[dst] + 1e-16)
            msg = h[src] * alpha[:, :, None]
            agg = jax.ops.segment_sum(msg, dst, num_segments=M).reshape(M, HEADS * NUM_EXPERTS) + b_gat
            scores = _layernorm(agg, ln_gamma, ln_beta).reshape(M, HEADS, NUM_EXPERTS).mean(1)
            scores = scores.reshape(Bc, Nc, NUM_EXPERTS)
            topk_s, topk_i = jax.lax.top_k(scores, TOP_K)
            w = jax.nn.softmax(topk_s, axis=-1)
            out = jnp.zeros_like(x)
            for ei in range(NUM_EXPERTS):
                g = jnp.where(topk_i == ei, w, 0.0).sum(-1)
                hh = jax.nn.gelu(x @ W1[ei] + b1[ei], approximate=False)
                out = out + g[..., None] * (hh @ W2[ei] + b2[ei])
            return out
        key = jax.random.key(seed)
        ks = jax.random.split(key, 8)
        s = 0.05
        return {'x': jax.random.normal(ks[0], (B, N, D), jnp.float32), 'W_gat': jax.random.normal(ks[1], (D, HEADS * NUM_EXPERTS), jnp.float32) * s, 'att_src': jax.random.normal(ks[2], (HEADS, NUM_EXPERTS), jnp.float32) * s, 'att_dst': jax.random.normal(ks[3], (HEADS, NUM_EXPERTS), jnp.float32) * s, 'b_gat': jnp.zeros((HEADS * NUM_EXPERTS,), jnp.float32), 'ln_gamma': jnp.ones((HEADS * NUM_EXPERTS,), jnp.float32), 'ln_beta': jnp.zeros((HEADS * NUM_EXPERTS,), jnp.float32), 'W1': jax.random.normal(ks[4], (NUM_EXPERTS, D, 2 * D), jnp.float32) * s, 'b1': jnp.zeros((NUM_EXPERTS, 2 * D), jnp.float32), 'W2': jax.random.normal(ks[5], (NUM_EXPERTS, 2 * D, D), jnp.float32) * s, 'b2': jnp.zeros((NUM_EXPERTS, D), jnp.float32), 'edge_index': jax.random.randint(ks[6], (2, N_EDGES), 0, B * N, jnp.int32)}
    _L0_ffn_all = _L0_ffn_setup()
    _L0_ffn_in = {k: v for k, v in _L0_ffn_all.items() if k in ('W_gat', 'att_src', 'att_dst', 'b_gat', 'ln_gamma', 'ln_beta', 'W1', 'b1', 'W2', 'b2', 'edge_index')}
    del _L0_ffn_all
    return {'x': x, 'fside_BS_outcomes': fside_BS_outcomes, 'fside_BS_timestamps': fside_BS_timestamps, 'L0_tok_h_q': _L0_tok_in['h_q'], 'L0_tok_W_o': _L0_tok_in['W_o'], 'L0_tok_W_dt': _L0_tok_in['W_dt'], 'L0_tok_W_proj_w': _L0_tok_in['W_proj_w'], 'L0_tok_W_proj_b': _L0_tok_in['W_proj_b'], 'L0_tok_ln_g': _L0_tok_in['ln_g'], 'L0_tok_ln_b': _L0_tok_in['ln_b'], 'L0_attn_Wks': _L0_attn_in['Wks'], 'L0_attn_Wqs': _L0_attn_in['Wqs'], 'L0_attn_Wvs': _L0_attn_in['Wvs'], 'L0_attn_Wo': _L0_attn_in['Wo'], 'L0_ffn_W_gat': _L0_ffn_in['W_gat'], 'L0_ffn_att_src': _L0_ffn_in['att_src'], 'L0_ffn_att_dst': _L0_ffn_in['att_dst'], 'L0_ffn_b_gat': _L0_ffn_in['b_gat'], 'L0_ffn_ln_gamma': _L0_ffn_in['ln_gamma'], 'L0_ffn_ln_beta': _L0_ffn_in['ln_beta'], 'L0_ffn_W1': _L0_ffn_in['W1'], 'L0_ffn_b1': _L0_ffn_in['b1'], 'L0_ffn_W2': _L0_ffn_in['W2'], 'L0_ffn_b2': _L0_ffn_in['b2'], 'L0_ffn_edge_index': _L0_ffn_in['edge_index']}

def reference(x, fside_BS_outcomes, fside_BS_timestamps, L0_tok_h_q, L0_tok_W_o, L0_tok_W_dt, L0_tok_W_proj_w, L0_tok_W_proj_b, L0_tok_ln_g, L0_tok_ln_b, L0_attn_Wks, L0_attn_Wqs, L0_attn_Wvs, L0_attn_Wo, L0_ffn_W_gat, L0_ffn_att_src, L0_ffn_att_dst, L0_ffn_b_gat, L0_ffn_ln_gamma, L0_ffn_ln_beta, L0_ffn_W1, L0_ffn_b1, L0_ffn_W2, L0_ffn_b2, L0_ffn_edge_index):
    import jax
    import jax.numpy as jnp

    def _L0_tok_ref(q_idx, outcomes, timestamps, h_q, W_o, W_dt, W_proj_w, W_proj_b, ln_g, ln_b):
        import jax, jax.numpy as jnp
        import numpy as np
        N_Q = 25000
        D = 64
        B, L = (32, 512)
        LN_EPS = 1e-05
        idx = jnp.clip(q_idx, 0, h_q.shape[0] - 1)
        q_emb = h_q[idx]
        o_feat = jnp.clip(outcomes[..., None] * W_o, -5.0, 5.0)
        t_feat = jnp.clip(jnp.log1p(jnp.abs(timestamps))[..., None] * W_dt, -5.0, 5.0)
        x = jnp.concatenate([q_emb, o_feat, t_feat], axis=-1)
        h = jnp.einsum('bli,oi->blo', x, W_proj_w) + W_proj_b
        mu = jnp.mean(h, axis=-1, keepdims=True)
        var = jnp.mean(jnp.square(h - mu), axis=-1, keepdims=True)
        return (h - mu) * jax.lax.rsqrt(var + LN_EPS) * ln_g + ln_b

    def _L0_attn_ref(x, Wks, Wqs, Wvs, Wo):
        import jax, jax.numpy as jnp
        import numpy as np
        EPS = 1e-09

        def _glorot(key, shape):
            fan_in, fan_out = (shape[-2], shape[-1])
            std = (2.0 / (fan_in + fan_out)) ** 0.5
            return jax.random.normal(key, shape, dtype=jnp.float32) * std

        def _reference_tuple_inner(x, Wks, Wqs, Wvs, Wo):
            keys = jnp.einsum('bsd,hdk->hbsk', x, Wks)
            queries = jnp.einsum('bsd,hdk->hbsk', x, Wqs)
            values = jnp.einsum('bsd,hde->hbse', x, Wvs)
            keys = jax.nn.elu(keys) + 1.0
            queries = jax.nn.elu(queries) + 1.0
            att = jnp.einsum('hbsk,hbtk->hbst', queries, keys)
            S = att.shape[-1]
            causal = jnp.tril(jnp.ones((S, S), dtype=att.dtype))
            att = att * causal
            att = att / (jnp.sum(att, axis=-1, keepdims=True) + EPS)
            kv = jnp.einsum('hbsk,hbsd->hbsdk', keys, values)
            kv_cum = jnp.cumsum(kv, axis=2)
            numerator = jnp.einsum('hbsdk,hbsk->hbsd', kv_cum, queries)
            denominator = jnp.einsum('hbsk,hbsk->hbs', jnp.cumsum(keys, axis=2), queries)
            node = numerator / (denominator[..., None] + EPS)
            out = jnp.einsum('hbsd,hde->bse', node, Wo)
            return (out, att)
        return _reference_tuple_inner(x, Wks, Wqs, Wvs, Wo)[0]

    def _L0_ffn_ref(x, W_gat, att_src, att_dst, b_gat, ln_gamma, ln_beta, W1, b1, W2, b2, edge_index):
        import jax, jax.numpy as jnp
        import numpy as np
        B, N, D = (16, 1024, 64)
        NUM_EXPERTS, TOP_K, HEADS = (4, 2, 4)
        N_EDGES = 262144
        LN_EPS = 1e-05

        def _layernorm(x, g, b):
            mu = x.mean(-1, keepdims=True)
            var = ((x - mu) ** 2).mean(-1, keepdims=True)
            return (x - mu) * jax.lax.rsqrt(var + LN_EPS) * g + b

        def _forward(x, edge_index, W_gat, att_src, att_dst, b_gat, ln_gamma, ln_beta, W1, b1, W2, b2):
            Bc, Nc, Dc = x.shape
            M = Bc * Nc
            x_flat = x.reshape(M, Dc)
            h = (x_flat @ W_gat).reshape(M, HEADS, NUM_EXPERTS)
            loops = jnp.arange(M, dtype=edge_index.dtype)
            src = jnp.concatenate([edge_index[0], loops])
            dst = jnp.concatenate([edge_index[1], loops])
            a_src = (h * att_src).sum(-1)
            a_dst = (h * att_dst).sum(-1)
            e = jax.nn.leaky_relu(a_src[src] + a_dst[dst], negative_slope=0.2)
            e_max = jax.ops.segment_max(e, dst, num_segments=M)
            ee = jnp.exp(e - e_max[dst])
            denom = jax.ops.segment_sum(ee, dst, num_segments=M)
            alpha = ee / (denom[dst] + 1e-16)
            msg = h[src] * alpha[:, :, None]
            agg = jax.ops.segment_sum(msg, dst, num_segments=M).reshape(M, HEADS * NUM_EXPERTS) + b_gat
            scores = _layernorm(agg, ln_gamma, ln_beta).reshape(M, HEADS, NUM_EXPERTS).mean(1)
            scores = scores.reshape(Bc, Nc, NUM_EXPERTS)
            topk_s, topk_i = jax.lax.top_k(scores, TOP_K)
            w = jax.nn.softmax(topk_s, axis=-1)
            out = jnp.zeros_like(x)
            for ei in range(NUM_EXPERTS):
                g = jnp.where(topk_i == ei, w, 0.0).sum(-1)
                hh = jax.nn.gelu(x @ W1[ei] + b1[ei], approximate=False)
                out = out + g[..., None] * (hh @ W2[ei] + b2[ei])
            return out
        return _forward(x, edge_index, W_gat, att_src, att_dst, b_gat, ln_gamma, ln_beta, W1, b1, W2, b2)
    h = _L0_tok_ref(x, fside_BS_outcomes, fside_BS_timestamps, L0_tok_h_q, L0_tok_W_o, L0_tok_W_dt, L0_tok_W_proj_w, L0_tok_W_proj_b, L0_tok_ln_g, L0_tok_ln_b)
    h = h + _L0_attn_ref(_layernorm(h, axis=-1), L0_attn_Wks, L0_attn_Wqs, L0_attn_Wvs, L0_attn_Wo)
    h = h + _L0_ffn_ref(_layernorm(h, axis=-1), L0_ffn_W_gat, L0_ffn_att_src, L0_ffn_att_dst, L0_ffn_b_gat, L0_ffn_ln_gamma, L0_ffn_ln_beta, L0_ffn_W1, L0_ffn_b1, L0_ffn_W2, L0_ffn_b2, L0_ffn_edge_index)
    return h

_drawn_inputs = setup_inputs


def setup_inputs(seed=0):
    import zlib

    import numpy as np

    out = dict(_drawn_inputs(seed))
    spreads = {'L0_tok_W_proj_b': (0.0, 0.1),
     'L0_tok_ln_g': (1.0, 0.2),
     'L0_tok_ln_b': (0.0, 0.1),
     'L0_ffn_b_gat': (0.0, 0.603),
     'L0_ffn_ln_gamma': (1.0, 0.552),
     'L0_ffn_ln_beta': (0.0, 0.8),
     'L0_ffn_b1': (0.0, 0.442),
     'L0_ffn_b2': (0.0, 0.1)}
    factors = {'L0_ffn_att_src': 64.0, 'L0_ffn_att_dst': 64.0}
    for name, (base, spread) in spreads.items():
        noise = np.random.default_rng([zlib.crc32(name.encode()), seed]).standard_normal(out[name].shape)
        drawn = base * np.exp(spread * noise) if base else spread * noise
        out[name] = jnp.asarray(drawn.astype(out[name].dtype))
    for name, factor in factors.items():
        out[name] = (out[name] * factor).astype(out[name].dtype)
    return out
```

```python
from contextlib import ExitStack

import concourse.bass as bass
from concourse import mybir

P = 128
N_TOK, D, N_Q = 4096, 64, 25000
NT = N_TOK // P
TG = 4
NG = NT // TG
GW = TG * P
H, K = 8, 32
HF = H // 4
FEATS = D + 3
NE_EXP, HEADS, HID = 4, 4, 128
N_EDGES = 262144
EC = N_EDGES // P
CW = 256
OW = 128
N_CHUNK = EC // CW
LOCAL_BITS = 11
CHUNK_BITS = 8
ALL_BITS = CHUNK_BITS + 7
CL_BASE = float(1 << 24)
BAD = float(1 << 25)
LAST = float(N_TOK - 1)
ROW = HEADS + HEADS * NE_EXP
NS = HEADS * (1 + NE_EXP)
SROW = HEADS + NS
LOW = -1e30
LN_EPS = 1e-5
ATT_EPS = 1e-9
OOB = 1e6
N_VAR = 3 * NG + 1
ACT_TURN = 4
VEC_HIST = 5
VEC_TURN = 145

F32 = mybir.dt.float32
BF16 = mybir.dt.bfloat16
I32 = mybir.dt.int32
ALU = mybir.AluOpType
ACT = mybir.ActivationFunctionType
X = mybir.AxisListType.X

C_ID, C_TRI, C_ONE, C_SIGN = 0, P, 2 * P, 3 * P
C_WIDTH = 3 * P + 8
B_G, B_B, B_SRC, B_DST, B_GAT, B_LG, B_LB, B_B2 = 0, 64, 128, 144, 160, 176, 192, 208
B_WO, B_WDT = 464, 465
B_WIDTH = 466


class Own:

    def __init__(self, eng, sem, before=0, turn=None, per_turn=0):
        self.eng, self.sem, self.n, self.before, self.turn, self.per_turn = eng, sem, 0, before, turn, per_turn

    def did(self, ins):
        ins.then_inc(self.sem, 1)
        self.n += 1

    def settle(self):
        at = self.before + self.n
        self.eng.wait_ge(self.sem, at if self.turn is None else self.turn * self.per_turn + at)


def every(turn, per_turn, n):
    return turn * per_turn + n


def build(nc, A, out):
    with ExitStack() as ctx:
        def sb(name, shape, dt=F32):
            return ctx.enter_context(nc.sbuf_tensor(name, shape, dt))

        def sem(name):
            return ctx.enter_context(nc.semaphore(name))

        const = sb("const", [P, C_WIDTH])
        par = sb("par", [P, B_WIDTH])
        ident, tri, ones = (const[:, c:c + P] for c in (C_ID, C_TRI, C_ONE))
        key_a = sb("key_a", [P, EC])
        key_b = sb("key_b", [P, EC])
        h2 = sb("h2", [P, NT, D])
        tab = sb("tab", [P, NT, ROW])
        a_dst = sb("a_dst", [P, NT, HEADS])
        y_exp = sb("y_exp", [P, NT, NE_EXP * D])
        counts = sb("counts", [P, 4])
        n_turns = sb("n_turns", [2, 2], I32)
        n_clamped = sb("n_clamped", [P, NT])
        acc_m = sb("acc_m", [P, NT, HEADS])
        acc_s = sb("acc_s", [P, NT, HEADS, 1 + NE_EXP])
        last_row = sb("last_row", [P, ROW])
        w_hid = sb("w_hid", [D + 1, NE_EXP * HID])
        w_outp = sb("w_outp", [HID, NE_EXP * D])
        w_gat = sb("w_gat", [D, HEADS * NE_EXP])

        arena = sb("arena", [P, 28 * 1024])
        used = [0]

        def cut(shape, dt=F32, rows=P):
            n = 1
            for s in shape:
                n *= s
            words = n if dt != BF16 else n // 2
            v = arena[0:rows, used[0]:used[0] + words]
            used[0] += words
            assert used[0] <= 28 * 1024, used[0]
            if dt != F32:
                v = v.bitcast(dt)
            if len(shape) > 1:
                names = "abcd"[:len(shape)]
                v = v.rearrange(f"p ({' '.join(names)}) -> p {' '.join(names)}", **dict(zip(names, shape)))
            return v

        emb = cut([NT, D])
        cat_t = cut([N_TOK], rows=FEATS)
        h1 = cut([NT, D])
        exp_kq, relu_kq = cut([4, GW]), cut([4, GW])
        kq = cut([4, GW])
        vals = cut([2, H, D + 1])
        att = cut([2, 4, 2, P])
        w_tok = cut([D], rows=FEATS)
        w_kq = cut([4 * P], rows=D)
        w_vt, w_o, w_vo = (cut([H * D], rows=D) for _ in range(3))
        x_t = cut([GW], rows=D)
        ffn_at = used[0]
        src_i, dst_i, t_a, t_b = cut([EC], I32), cut([EC], I32), cut([EC]), cut([EC])
        used[0] = ffn_at
        x2_t = cut([N_TOK], rows=D + 1)
        hid = cut([NE_EXP, GW])
        pulled = cut([NT, SROW])
        gate = cut([16, NT])
        agg, agg2 = (cut([NT, HEADS * NE_EXP]) for _ in range(2))
        used[0] = 0
        oh_p, oh_t = cut([P, OW], BF16), cut([NT, OW], BF16)
        rows = cut([CW, ROW])
        seg = cut([CW, SROW])
        ad_at = cut([CW, HEADS])
        e_ad, e_val, e_new = (cut([HEADS, CW]) for _ in range(3))
        tmp_s = arena[:, 0:CW * NS].rearrange("p (f s) -> p f s", s=NS)
        e_w, e_a = (key_b[:, c:c + HEADS * CW].rearrange("p (h f) -> p h f", h=HEADS) for c in (0, HEADS * CW))

        cen = sb("cen", [P, TG, D])
        sq = sb("sq", [P, TG, D])
        x2 = sb("x2", [P, TG, D])
        stat = sb("stat", [P, 4, TG])
        half = sb("half", [P, NT])
        feats = sb("feats", [NT, 2, P])
        q_idx = sb("q_idx", [P, NT], I32)
        q_f = sb("q_f", [P, NT])
        nv = sb("nv", [P, 2, 4, D])
        att_den = sb("att_den", [P, 2, H])
        prod = sb("prod", [P, TG, HEADS * NE_EXP])

        ck = [sb("ck0", [P, CW]), sb("ck1", [P, CW])]
        ki = sb("ki", [P, CW], I32)
        ti = sb("ti", [P, CW], I32)
        si = sb("si", [P, CW], I32)
        tb, lb = sb("tb", [P, CW], BF16), sb("lb", [P, CW], BF16)
        dst_f = sb("dst_f", [P, CW])
        same = sb("same", [P, CW])
        pen = sb("pen", [P, CW])
        hist = sb("hist", [P, NT])
        pos = sb("pos", [P, 4, NT])
        i_start, i_end = sb("i_start", [P, NT], I32), sb("i_end", [P, NT], I32)
        nonempty = sb("nonempty", [P, NT])
        i_first = sb("i_first", [P, 1], I32)
        ad_first = sb("ad_first", [P, HEADS])
        ends = sb("ends", [P, 4, NS])
        chain = sb("chain", [P, 8, P])
        carry = sb("carry", [P, 2, NS])
        new_m = sb("new_m", [P, NT, HEADS])
        fade = sb("fade", [P, 2, NT, HEADS])

        ps = ctx.enter_context(nc.psum_tensor("ps", [P, 8, 512], F32))

        d_tab = nc.dram_tensor("d_tab", [N_TOK, ROW], F32).ap()
        d_ad = nc.dram_tensor("d_ad", [P * CW, HEADS], F32).ap()
        d_adrow = nc.dram_tensor("d_adrow", [N_TOK, HEADS], F32).ap()
        d_seg = nc.dram_tensor("d_seg", [P * CW, SROW], F32).ap()

        made = {}

        def S(name):
            if name not in made:
                made[name] = sem(name)
            return made[name]

        block = ctx.enter_context(nc.Block())
        tall = lambda ap, n: ap.unsqueeze(len(ap.shape)).to_broadcast(list(ap.shape) + [n])

        def sign(k):
            return const[:, C_SIGN + k - CHUNK_BITS + 1:C_SIGN + k - CHUNK_BITS + 2]

        def early_value(eng, row):
            eng.wait_ge(S("turns_ready"), 16)
            return eng.value_load(turns_row[0:1, row:row + 1], min_val=1, max_val=N_CHUNK)

        turns_row = sb("turns_row", [1, 2], I32)

        order = ["vo", ("turn", 0), ("token", 0)]
        for g in range(NG):
            order += [("x_t", g)] + [("kq", g, m) for m in range(4)] + [("values", TG * g + k) for k in range(TG)]
            if g < NG - 1:
                order += [("turn", g + 1), ("token", g + 1)]
            if g:
                order += [("x2_t", g - 1), ("nodes", g - 1)]
        order += [("x2_t", NG - 1), ("nodes", NG - 1)]
        order += [("hidden", g, x) for g in range(NG) for x in range(NE_EXP)]
        nth = {item: n + 1 for n, item in enumerate(order)}

        @block.sync
        def _(sp):
            sp.dma_start(q_idx[:], A["idx"]).then_inc(S("idx_in"), 16)
            sp.dma_start(src_i, A["src"]).then_inc(S("src_in"), 16)
            sp.dma_start(dst_i, A["dst"]).then_inc(S("dst_in"), 16)
            sp.dma_start(const[:], A["const"]).then_inc(S("const_in"), 16)
            sp.dma_start(par[:], A["par"].to_broadcast([P, B_WIDTH])).then_inc(S("par_in"), 16)
            sp.dma_start(feats[:, 0, :], A["outcomes"]).then_inc(S("feats_in"), 16)
            sp.dma_start(feats[:, 1, :], A["times"]).then_inc(S("feats_in"), 16)
            for dst, name in ((w_tok, "w_tok"), (w_kq, "w_kq"), (w_vt, "w_vt"), (w_o, "w_o"),
                              (w_hid[:], "w_hid"), (w_outp[:], "w_outp"), (w_gat[:], "w_gat")):
                sp.dma_start(dst, A[name]).then_inc(S("weights_in"), 16)
            sp.dma_start(d_ad.rearrange("(p f) h -> p (f h)", p=P), A["zeros"].to_broadcast([P, CW * HEADS]))\
              .then_inc(S("zero_written"), 16)
            sp.wait_ge(S("feats_done"), 2)
            for r in range(2):
                sp.dma_start(cat_t[D + r:D + r + 1, :], feats[:, r, :]).then_inc(S("cat_rows"), 16)
            sp.wait_ge(S("n_turns_set"), 1)
            sp.dma_start(turns_row[:], n_turns[:, 0:1]).then_inc(S("turns_ready"), 16)
            sp.wait_ge(S("tab_ready"), NG)
            sp.dma_start(d_tab.rearrange("(t p) r -> p t r", p=P), tab[:]).then_inc(S("tab_written"), 16)
            sp.dma_start(d_adrow.rearrange("(t p) r -> p t r", p=P), a_dst[:]).then_inc(S("adrow_written"), 16)
            sp.wait_ge(S("tab_written"), 16)
            sp.dma_start(last_row[:], d_tab[N_TOK - 1:N_TOK, :].to_broadcast([P, ROW])).then_inc(S("last_row_in"), 16)
            turns = early_value(sp, 1)
            with sp.Fori(0, turns) as i:
                sp.wait_ge(S("ad_scattered"), every(i, 16 * NT, 16 * NT))
                sp.dma_start(ad_at.rearrange("p f h -> p (f h)"), d_ad.rearrange("(p f) h -> p (f h)", p=P))\
                  .then_inc(S("ad_in"), 16)
                sp.wait_ge(S("seg_ready"), every(i, 1, 1))
                sp.dma_start(d_seg.rearrange("(p f) s -> p (f s)", p=P), seg.rearrange("p f s -> p (f s)"))\
                  .then_inc(S("seg_written"), 16)
            sp.wait_ge(S("result"), 1)
            sp.dma_start(out.rearrange("b s d -> s b d"), h2[:]).then_inc(S("stored"), 16)
            sp.wait_ge(S("stored"), 16)

        @block.gpsimd
        def _(pool):
            pool.memset(half[:], -0.5).then_inc(S("half_set"), 1)
            pool.wait_ge(S("idx_ready"), 1)
            for t in range(NT):
                pool.indirect_dma_start(out=emb[:, t, :], out_offset=None, in_=A["h_q"],
                                        in_offset=bass.IndirectOffsetOnAxis(q_idx[:, t:t + 1], 0))\
                    .then_inc(S(f"emb_in{t // TG}"), 16)
            pool.wait_ge(S("half_set"), 1)
            n_pow = 0

            def rsqrt():
                nonlocal n_pow
                n_pow += 1
                pool.wait_ge(S("var_ready"), n_pow)
                pool.tensor_tensor(stat[:, 2, :], stat[:, 1, :], half[:, 0:TG], ALU.pow).then_inc(S("rstd_ready"), 1)

            def mask(b):
                pool.wait_ge(S("att_ready"), b + 1)
                v = att[:, b % 2].rearrange("p j m s -> p (j m) s")
                pool.affine_select(out=v, in_=v, compare_op=ALU.is_ge, fill=0.0, base=0,
                                   pattern=[[0, H], [1, P]], channel_multiplier=-1).then_inc(S("masked"), 1)

            rsqrt()
            rsqrt()
            for g in range(NG):
                if g:
                    rsqrt()
                for b in range(TG):
                    mask(TG * g + b)
                if g < NG - 1:
                    rsqrt()
                    rsqrt()
            rsqrt()

            turns = early_value(pool, 1)
            pool.wait_ge(S("tab_written"), 16)
            pool.wait_ge(S("adrow_written"), 16)
            pool.wait_ge(S("zero_written"), 16)
            pool.wait_ge(S("experts_done"), 1)
            with pool.Fori(0, turns) as i:
                pool.wait_ge(S("src_ready"), every(i, 1, 1))
                pool.sem_inc(S("pool_passed"), 1)
                for f in range(CW):
                    if f == 0:
                        pool.indirect_dma_start(out=ad_first[:], out_offset=None, in_=d_adrow,
                                                in_offset=bass.IndirectOffsetOnAxis(i_first[:, 0:1], 0))\
                            .then_inc(S("ad_first_in"), 16)
                    if f == CW // 2:
                        pool.wait_ge(S("pos_ready"), every(i, 1, 1))
                        pool.sem_inc(S("pool_passed"), 1)
                        for t in range(NT):
                            pool.indirect_dma_start(out=d_ad, in_=a_dst[:, t, :], in_offset=None,
                                                    out_offset=bass.IndirectOffsetOnAxis(i_start[:, t:t + 1], 0),
                                                    bounds_check=P * CW - 1, oob_is_err=False)\
                                .then_inc(S("ad_scattered"), 16)
                    pool.indirect_dma_start(out=rows[:, f, :], out_offset=None, in_=d_tab,
                                            in_offset=bass.IndirectOffsetOnAxis(si[:, f:f + 1], 0))\
                        .then_inc(S("rows_in"), 16)
                pool.wait_ge(S("seg_written"), every(i, 16, 16))
                pool.sem_inc(S("pool_passed"), 1)
                for t in range(NT):
                    pool.indirect_dma_start(out=pulled[:, t, :], out_offset=None, in_=d_seg,
                                            in_offset=bass.IndirectOffsetOnAxis(i_end[:, t:t + 1], 0))\
                        .then_inc(S("pulled_in"), 16)
                pool.wait_ge(S("turn_done"), every(i, 1, 1))
                pool.sem_inc(S("pool_passed"), 1)
            pool.wait_ge(S("var_ready"), N_VAR)
            pool.tensor_tensor(gate[:, 2, :], gate[:, 1, :], half[:], ALU.pow).then_inc(S("rstd_ready"), 1)

        @block.scalar
        def _(act):
            act.wait_ge(S("abs_ready"), 1)
            act.activation(feats[:, 1, :], feats[:, 1, :], ACT.Ln, bias=1.0).then_inc(S("logged"), 1)
            done = 0

            def evacuate(item, *jobs):
                nonlocal done
                done += 1
                assert nth[item] == done, item
                act.wait_ge(S("bank_filled"), done)
                for out_, func, view in jobs:
                    last = act.activation(out_, view(ps[:, (done - 1) % 2, :]), func)
                last.then_inc(S("bank_read"), 1)

            whole = lambda v: v
            lower = lambda v: v[0:D, :]

            def token_part(g):
                evacuate(("turn", g), (cat_t[0:D, g * GW:(g + 1) * GW], ACT.Copy, lower))
                evacuate(("token", g), (h1[:, TG * g:TG * g + TG, :], ACT.Copy,
                                        lambda v: v[:, 0:TG * D].rearrange("p (t d) -> p t d", t=TG)))

            def node_part(g):
                evacuate(("x2_t", g), (x2_t[0:D, g * GW:(g + 1) * GW], ACT.Copy, lower))
                evacuate(("nodes", g), (tab[:, TG * g:TG * g + TG, HEADS:ROW], ACT.Copy,
                                        lambda v: v[:, 0:64].rearrange("p (t c) -> p t c", t=TG)))

            evacuate("vo", (w_vo, ACT.Copy, lower))
            token_part(0)
            for g in range(NG):
                evacuate(("x_t", g), (x_t, ACT.Copy, lower))
                for m in range(4):
                    if g and m == 0:
                        act.wait_ge(S("kq_ready"), 4 * g)
                    evacuate(("kq", g, m), (relu_kq[:, m, :], ACT.Relu, whole), (exp_kq[:, m, :], ACT.Exp, whole))
                for b in range(TG * g, TG * g + TG):
                    act.wait_ge(S("att_out"), b + 1)
                    if b >= 2:
                        act.wait_ge(S("av_out"), b - 1)
                    act.activation(att[:, b % 2], ps[:, 4:8, 0:2 * P].rearrange("p j (m s) -> p j m s", m=2),
                                   ACT.Copy).then_inc(S("att_ready"), 1)
                    if b == 0:
                        act.wait_ge(S("ones_set"), 1)
                    evacuate(("values", b), (vals[:, b % 2, :, 0:D], ACT.Copy, lambda v: v.rearrange("p (h e) -> p h e", h=H)))
                if g < NG - 1:
                    token_part(g + 1)
                if g:
                    node_part(g - 1)
            node_part(NG - 1)
            for g in range(NG):
                for x in range(NE_EXP):
                    if g and x == 0:
                        act.wait_ge(S("y_out"), 2 * g)
                    evacuate(("hidden", g, x), (hid[:, x, :], ACT.Gelu, whole))
            act.wait_ge(S("fade_shift"), 1)
            act.activation(fade[:], fade[:], ACT.Exp).then_inc(S("faded"), 1)

            turns = early_value(act, 1)
            with act.Fori(0, turns) as i:
                own = Own(act, S("act_scan"), 0, i, ACT_TURN)
                act.wait_ge(S("shift_ready"), every(i, 1, 1))
                act.activation(e_a, e_a, ACT.Exp)
                own.did(act.activation(e_w, e_w, ACT.Exp))
                act.wait_ge(S("chain_shift"), every(i, 1, 1))
                own.did(act.activation(chain[0:NS, 4:6, :], chain[0:NS, 4:6, :], ACT.Exp))
                act.wait_ge(S("carry_shift"), every(i, 1, 1))
                act.activation(e_a, e_a, ACT.Exp)
                own.did(act.activation(e_w, e_w, ACT.Exp))
                act.wait_ge(S("fade_shift"), every(i, 1, 2))
                own.did(act.activation(fade[:], fade[:], ACT.Exp))
                assert own.n == ACT_TURN
            act.wait_ge(S("soft_shift"), 1)
            act.activation(gate[:, 8:12, :], gate[:, 8:12, :], ACT.Exp).then_inc(S("soft_exp"), 1)

        @block.tensor
        def _(pe):
            pe.wait_ge(S("const_in"), 16)
            pe.wait_ge(S("weights_in"), 7 * 16)
            done = 0

            def bank(item):
                nonlocal done
                done += 1
                assert nth[item] == done, item
                if done > 2:
                    pe.wait_ge(S("bank_read"), done - 2)
                return ps[:, (done - 1) % 2, :]

            def copied(item):
                pe.wait_ge(S("bank_read"), nth[item])

            to = bank("vo")
            for h in range(H):
                last = pe.matmul(to[0:D, h * D:(h + 1) * D], w_vt[:, h * D:(h + 1) * D], w_o[:, h * D:(h + 1) * D],
                                 start=True, stop=True)
            last.then_inc(S("bank_filled"), 1)
            pe.wait_ge(S("counts_ready"), 1)
            pe.transpose(ps[0:2, 2, 0:P], counts[:, 0:2], ident).then_inc(S("counts_turned"), 1)

            def turn(item, tile_of):
                to = bank(item)
                for k in range(TG):
                    last = pe.transpose(to[0:D, k * P:(k + 1) * P], tile_of(k), ident)
                last.then_inc(S("bank_filled"), 1)

            def token_part(g):
                pe.wait_ge(S(f"emb_in{g}"), 16 * TG)
                turn(("turn", g), lambda k: emb[:, TG * g + k, :])
                if g == 0:
                    pe.wait_ge(S("cat_rows"), 32)
                copied(("turn", g))
                to = bank(("token", g))
                for k in range(TG):
                    t = TG * g + k
                    last = pe.matmul(to[:, k * D:(k + 1) * D], cat_t[:, t * P:(t + 1) * P], w_tok, start=True, stop=True)
                last.then_inc(S("bank_filled"), 1)

            def node_part(g):
                pe.wait_ge(S("x2_ready"), g + 1)
                turn(("x2_t", g), lambda k: x2[:, k, :])
                copied(("x2_t", g))
                to = bank(("nodes", g))
                for k in range(TG):
                    t = TG * g + k
                    last = pe.matmul(to[:, 16 * k:16 * k + 16], x2_t[0:D, t * P:(t + 1) * P], w_gat[:], start=True, stop=True)
                last.then_inc(S("bank_filled"), 1)

            def weigh(b):
                pe.wait_ge(S("masked"), b + 1)
                copied(("values", b))
                if b:
                    pe.wait_ge(S("av_read"), b)
                for h in range(H):
                    j, m = h % 4, h // 4
                    last = pe.matmul(ps[:, 2 + m, j * (D + 1):(j + 1) * (D + 1)], att[:, b % 2, j, m, :],
                                     vals[:, b % 2, h, :], start=True, stop=True)
                last.then_inc(S("av_out"), 1)

            token_part(0)
            for g in range(NG):
                pe.wait_ge(S("xa_ready"), g + 1)
                turn(("x_t", g), lambda k: h2[:, TG * g + k, :])
                copied(("x_t", g))
                for m in range(4):
                    pe.matmul(bank(("kq", g, m)), w_kq[:, m * P:(m + 1) * P], x_t, start=True, stop=True)\
                      .then_inc(S("bank_filled"), 1)
                pe.wait_ge(S("kq_ready"), 4 * (g + 1))
                for b in range(TG * g, TG * g + TG):
                    k = b - TG * g
                    if b:
                        pe.wait_ge(S("att_ready"), b)
                    for h in range(H):
                        j, m = h % 4, h // 4
                        last = pe.matmul(ps[:, 4 + j, m * P:(m + 1) * P], kq[32 * j:32 * j + 32, m, k * P:(k + 1) * P],
                                         kq[32 * j:32 * j + 32, 2 + m, k * P:(k + 1) * P], start=True, stop=True)
                    last.then_inc(S("att_out"), 1)
                    pe.matmul(bank(("values", b)), x_t[:, k * P:(k + 1) * P], w_vo, start=True, stop=True)\
                      .then_inc(S("bank_filled"), 1)
                    if k:
                        weigh(b - 1)
                if g < NG - 1:
                    token_part(g + 1)
                if g:
                    node_part(g - 1)
                weigh(TG * g + TG - 1)
            node_part(NG - 1)
            pe.wait_ge(S("x2_ones"), 1)
            pe.wait_ge(S("av_read"), NT)
            for g in range(NG):
                for x in range(NE_EXP):
                    pe.matmul(bank(("hidden", g, x)), w_hid[:, x * HID:(x + 1) * HID], x2_t[:, g * GW:(g + 1) * GW],
                              start=True, stop=True).then_inc(S("bank_filled"), 1)
                copied(("hidden", g, NE_EXP - 1))
                for q in range(2):
                    n = 2 * g + q
                    if n >= 4:
                        pe.wait_ge(S("y_read"), n - 3)
                    for k in range(2):
                        for x in range(NE_EXP):
                            last = pe.matmul(ps[:, 4 + n % 4, k * 256 + x * D:k * 256 + (x + 1) * D],
                                             hid[:, x, (2 * q + k) * P:(2 * q + k + 1) * P],
                                             w_outp[:, x * D:(x + 1) * D], start=True, stop=True)
                    last.then_inc(S("y_out"), 1)

            def count(bank, ready, done, i, per_turn):
                for q in range(CW // OW):
                    pe.wait_ge(S(ready), every(i, per_turn, q + 1))
                    for f in range(OW):
                        last = pe.matmul(ps[:, bank, 0:NT], oh_p[:, :, f], oh_t[:, :, f],
                                         start=q == f == 0, stop=q == CW // OW - 1 and f == OW - 1)
                    last.then_inc(S(done), 1)

            turns = early_value(pe, 0)
            with pe.Fori(0, turns) as i:
                count(0, "onehots", "counted", i, 2)

            turns = early_value(pe, 1)
            with pe.Fori(0, turns) as i:
                for k in range(CHUNK_BITS + 1, ALL_BITS + 1):
                    n = k - CHUNK_BITS
                    pe.wait_ge(S("to_columns"), every(i, 7, n))
                    for q in range(2):
                        last = pe.transpose(ps[:, 0, q * P:(q + 1) * P], ck[0][:, q * P:(q + 1) * P], ident)
                    last.then_inc(S("in_columns"), 1)
                    pe.wait_ge(S("to_rows"), every(i, 7, n))
                    for q in range(2):
                        last = pe.transpose(ps[:, 1, q * P:(q + 1) * P], ck[n % 2][:, q * P:(q + 1) * P], ident)
                    last.then_inc(S("in_rows"), 1)
                count(2, "onehots2", "counted2", i, 2)
                pe.wait_ge(S("hist_ready"), every(i, 1, 1))
                pe.matmul(ps[:, 2, 64:64 + NT], tri, hist[:], start=True, stop=True)
                pe.matmul(ps[:, 2, 96:96 + NT], ones, hist[:], start=True, stop=True).then_inc(S("cum_out"), 1)
                pe.wait_ge(S("ends_ready"), every(i, 1, 1))
                for q in range(4):
                    last = pe.transpose(ps[0:NS, 3, q * P:(q + 1) * P], ends[:, q, :], ident)
                last.then_inc(S("ends_turned"), 1)
                pe.wait_ge(S("chain_ready"), every(i, 1, 1))
                for q in range(2):
                    last = pe.transpose(ps[:, 5, q * P:(q + 1) * P], chain[:, q, :], ident)
                last.then_inc(S("carry_out"), 1)

        @block.vector
        def _(dve):
            own = Own(dve, S("vec_step"))

            def then(ins):
                own.did(ins)
                own.settle()

            TT, TS, STT = dve.tensor_tensor, dve.tensor_scalar, dve.scalar_tensor_tensor
            dve.memset(cat_t[D:FEATS, :], 1.0)
            dve.memset(counts[:], 0.0)
            dve.wait_ge(S("idx_in"), 16)
            then(dve.tensor_copy(q_f[:], q_idx[:]))
            then(TS(q_f[:], q_f[:], 0.0, float(N_Q - 1), ALU.max, ALU.min))
            dve.tensor_copy(q_idx[:], q_f[:]).then_inc(S("idx_ready"), 1)
            dve.wait_ge(S("feats_in"), 32)
            STT(feats[:, 1, :], feats[:, 1, :], -1.0, feats[:, 1, :], ALU.mult, ALU.max).then_inc(S("abs_ready"), 1)
            dve.wait_ge(S("par_in"), 16)
            then(TS(feats[:, 0, :], feats[:, 0, :], par[0:NT, B_WO:B_WO + 1], -5.0, ALU.mult, ALU.max))
            TS(feats[:, 0, :], feats[:, 0, :], 5.0, None, ALU.min).then_inc(S("feats_done"), 1)
            dve.wait_ge(S("logged"), 1)
            then(TS(feats[:, 1, :], feats[:, 1, :], par[0:NT, B_WDT:B_WDT + 1], -5.0, ALU.mult, ALU.max))
            TS(feats[:, 1, :], feats[:, 1, :], 5.0, None, ALU.min).then_inc(S("feats_done"), 1)
            dve.memset(vals[:, :, :, D:D + 1], 1.0).then_inc(S("ones_set"), 1)

            dve.wait_ge(S("src_in"), 16)
            dve.wait_ge(S("dst_in"), 16)
            dve.tensor_copy(key_b[:], src_i)
            then(dve.tensor_copy(t_a, dst_i))
            then(TS(t_b, key_b[:], 0.0, float(N_TOK), ALU.is_lt, ALU.mult))
            then(TT(key_b[:], key_b[:], t_b, ALU.add))
            then(TS(key_b[:], key_b[:], 0.0, LAST, ALU.max, ALU.min))
            TS(src_i, key_b[:], LAST, None, ALU.is_ge)
            TS(t_b, t_a, LAST, None, ALU.is_gt)
            then(STT(key_a[:], t_a, float(N_TOK), key_b[:], ALU.mult, ALU.add))
            then(STT(dst_i, t_a, 0.0, t_b, ALU.is_lt, ALU.max))
            then(TS(t_a, t_a, 2.0, CL_BASE, ALU.mult, ALU.add))
            then(dve.copy_predicated(key_a[:], src_i, t_a))
            then(dve.memset(t_b, BAD))
            then(dve.copy_predicated(key_a[:], dst_i, t_b))
            TS(t_a, key_a[:], BAD, None, ALU.is_lt)
            then(TS(t_b, key_a[:], CL_BASE, None, ALU.is_lt))
            dve.tensor_reduce(counts[:, 0:1], t_a, X, ALU.add)
            dve.tensor_reduce(counts[:, 1:2], t_b, X, ALU.add).then_inc(S("counts_ready"), 1)
            dve.wait_ge(S("counts_turned"), 1)
            then(dve.tensor_reduce(counts[0:2, 2:3], ps[0:2, 2, 0:P], X, ALU.max))
            then(TS(counts[0:2, 2:3], counts[0:2, 2:3], 1.0, float(CW - 1), ALU.max, ALU.add))
            then(dve.tensor_copy(n_turns[:, 0:1], counts[0:2, 2:3]))
            TS(n_turns[:, 0:1], n_turns[:, 0:1], CHUNK_BITS, None, ALU.logical_shift_right).then_inc(S("n_turns_set"), 1)
            dve.memset(x2_t[D:D + 1, :], 1.0).then_inc(S("x2_ones"), 1)
            dve.memset(n_clamped[:], 0.0)

            def local_sort():
                sorting = Own(dve, S("sort_step"))
                src, dst = key_a, key_b
                for k in range(1, LOCAL_BITS + 1):
                    for j in range(k - 1, -1, -1):
                        d = 1 << j
                        a = src[:].rearrange("p (b w) -> p b w", w=2 * d)
                        o = dst[:].rearrange("p (b w) -> p b w", w=2 * d)
                        hi = a[:, :, 2 * d - 1:d - 1:-1] if j == k - 1 and d > 1 else a[:, :, d:2 * d]
                        if sorting.n:
                            sorting.settle()
                        TT(o[:, :, 0:d], a[:, :, 0:d], hi, ALU.min)
                        sorting.did(TT(o[:, :, d:2 * d], a[:, :, 0:d], hi, ALU.max))
                        src, dst = dst, src
                        yield
                assert src is key_a
                sorting.settle()

            steps = local_sort()

            def sort(n):
                for _ in range(n):
                    next(steps, None)

            n_var = 0

            def normalise(x, o, last=None):
                nonlocal n_var
                then(dve.tensor_reduce(stat[:, 0, :], x, X, ALU.add))
                then(TS(stat[:, 0, :], stat[:, 0, :], -1.0 / D, None, ALU.mult))
                then(TT(cen[:], x, tall(stat[:, 0, :], D), ALU.add))
                then(TT(sq[:], cen[:], cen[:], ALU.mult))
                then(dve.tensor_reduce(stat[:, 3, :], sq[:], X, ALU.add))
                TS(stat[:, 1, :], stat[:, 3, :], 1.0 / D, LN_EPS, ALU.mult, ALU.add).then_inc(S("var_ready"), 1)
                n_var += 1
                sort(1)
                dve.wait_ge(S("rstd_ready"), n_var)
                ins = TT(o, cen[:], tall(stat[:, 2, :], D), ALU.mult)
                if last:
                    ins.then_inc(S(last), 1)
                else:
                    then(ins)

            def across(c, n, mid):
                return par[:, c:c + n].unsqueeze(1).to_broadcast([P, mid, n])

            def token_part(g):
                dve.wait_ge(S("bank_read"), nth[("token", g)])
                t = slice(TG * g, TG * g + TG)
                normalise(h1[:, t, :], sq[:])
                then(TT(sq[:], sq[:], across(B_G, D, TG), ALU.mult))
                own.did(TT(h1[:, t, :], sq[:], across(B_B, D, TG), ALU.add))
                own.settle()
                normalise(h1[:, t, :], h2[:, t, :], "xa_ready")

            def features(g):
                for m in range(4):
                    dve.wait_ge(S("bank_read"), nth[("kq", g, m)])
                    STT(kq[:, m, :], exp_kq[:, m, :], 1.0, relu_kq[:, m, :], ALU.min, ALU.add).then_inc(S("kq_ready"), 1)

            def attended(b):
                dve.wait_ge(S("av_out"), b + 1)
                av = ps[:, 2:4, 0:4 * (D + 1)].rearrange("p m (j e) -> p m j e", j=4)
                d0, d1 = (att_den[:, q, :].rearrange("p (m j) -> p m j", m=2) for q in range(2))
                then(TS(d0, av[:, :, :, D], ATT_EPS, None, ALU.add))
                then(dve.reciprocal(d1, d0))
                dve.tensor_tensor(nv[:], av[:, :, :, 0:D], tall(d1, D), ALU.mult).then_inc(S("av_read"), 1)
                dve.wait_ge(S("av_read"), b + 1)
                then(dve.tensor_reduce(h2[:, b, :], nv[:].rearrange("p m j e -> p e (m j)"), X, ALU.add))
                own.did(TT(h2[:, b, :], h2[:, b, :], h1[:, b, :], ALU.add))

            def second_norm(g):
                own.settle()
                normalise(h2[:, TG * g:TG * g + TG, :], x2[:], "x2_ready")

            def node_part(g):
                t = slice(TG * g, TG * g + TG)
                dve.wait_ge(S("bank_read"), nth[("nodes", g)])
                for c, o in ((B_SRC, tab[:, t, 0:HEADS]), (B_DST, a_dst[:, t, :])):
                    then(TT(prod[:], tab[:, t, HEADS:ROW], across(c, 16, TG), ALU.mult))
                    ins = dve.tensor_reduce(o, prod[:].rearrange("p t (h e) -> p t h e", e=NE_EXP), X, ALU.add)
                    if c == B_DST:
                        ins.then_inc(S("tab_ready"), 1)
                    else:
                        then(ins)

            token_part(0)
            for g in range(NG):
                features(g)
                if g:
                    second_norm(g - 1)
                for b in range(TG * g, TG * g + 3):
                    sort(1)
                    attended(b)
                if g < NG - 1:
                    token_part(g + 1)
                if g:
                    node_part(g - 1)
                attended(TG * g + 3)
            second_norm(NG - 1)
            node_part(NG - 1)
            for n in range(2 * NG):
                sort(1)
                dve.wait_ge(S("y_out"), n + 1)
                TT(y_exp[:, 2 * n:2 * n + 2, :], ps[:, 4 + n % 4, :].rearrange("p (t c) -> p t c", t=2),
                   across(B_B2, NE_EXP * D, 2), ALU.add).then_inc(S("y_read"), 1)
            sort(LOCAL_BITS * LOCAL_BITS)
            dve.wait_ge(S("y_read"), 2 * NG)

            def one_hots(q, ready):
                for j in range(P):
                    TS(oh_p[:, j, :], lb[:, q * OW:(q + 1) * OW], float(j), None, ALU.is_equal)
                for j in range(NT):
                    last = TS(oh_t[:, j, :], tb[:, q * OW:(q + 1) * OW], float(j), None, ALU.is_equal)
                last.then_inc(S(ready), 1)

            def node_of(ints, low, high):
                then(TS(ti[:], ints[:], low, P - 1, ALU.logical_shift_right, ALU.bitwise_and))
                then(dve.tensor_copy(lb[:], ti[:]))
                then(TS(ti[:], ints[:], high, None, ALU.arith_shift_right))
                then(dve.tensor_copy(tb[:], ti[:]))

            turns = early_value(dve, 0)
            with dve.Fori(0, turns) as i:
                own = Own(dve, S("vec_hist"), 0, i, VEC_HIST)
                then(TS(ki[:], key_a[:, bass.ds(i * CW, CW)], CL_BASE, 2.0 * N_TOK, ALU.subtract, ALU.min))
                node_of(ki, 1, 8)
                one_hots(0, "onehots")
                dve.wait_ge(S("counted"), every(i, 2, 1))
                one_hots(1, "onehots")
                dve.wait_ge(S("counted"), every(i, 2, 2))
                TT(n_clamped[:], n_clamped[:], ps[:, 0, 0:NT], ALU.add).then_inc(S("clamped_added"), 1)
                dve.wait_ge(S("clamped_added"), every(i, 1, 1))
                assert own.n == VEC_HIST, own.n

            own = Own(dve, S("vec_start"))

            def leaky(o):
                then(STT(o, o, 0.2, o, ALU.mult, ALU.max))

            def masked(present):
                m, s_ = pulled[:, :, 0:HEADS], pulled[:, :, HEADS:SROW]
                then(TT(m, m, tall(present, HEADS), ALU.mult))
                then(TS(pos[:, 3, :], present, -LOW, LOW, ALU.mult, ALU.add))
                then(TT(m, m, tall(pos[:, 3, :], HEADS), ALU.add))
                then(TT(s_, s_, tall(present, NS), ALU.mult))

            s5 = lambda v: v.rearrange("p t (h c) -> p t h c", h=HEADS)

            def merge(sent, n_exp, value):
                m, s_ = pulled[:, :, 0:HEADS], s5(pulled[:, :, HEADS:SROW])
                then(TT(new_m[:], acc_m[:], m, ALU.max))
                TT(fade[:, 0], acc_m[:], new_m[:], ALU.subtract)
                TT(fade[:, 1], m, new_m[:], ALU.subtract).then_inc(S("fade_shift"), 1)
                dve.wait_ge(S(n_exp), value)
                then(dve.tensor_copy(acc_m[:], new_m[:]))
                then(TT(acc_s[:], acc_s[:], tall(fade[:, 0], 1 + NE_EXP), ALU.mult))
                then(TT(s_, s_, tall(fade[:, 1], 1 + NE_EXP), ALU.mult))
                then(TT(acc_s[:], acc_s[:], s_, ALU.add))

            then(TT(acc_m[:], tab[:, :, 0:HEADS], a_dst[:], ALU.add))
            leaky(acc_m[:])
            then(dve.memset(acc_s[:], 1.0))
            then(dve.tensor_copy(acc_s[:, :, :, 1:], s5(tab[:, :, HEADS:ROW])))
            dve.wait_ge(S("last_row_in"), 16)
            lr = lambda a, b: last_row[:, a:b].unsqueeze(1).to_broadcast([P, NT, b - a])
            then(TT(pulled[:, :, 0:HEADS], a_dst[:], lr(0, HEADS), ALU.add))
            leaky(pulled[:, :, 0:HEADS])
            p5 = s5(pulled[:, :, HEADS:SROW])
            then(dve.memset(p5[:, :, :, 0:1], 1.0))
            then(dve.tensor_copy(p5[:, :, :, 1:], s5(lr(HEADS, ROW))))
            then(TT(pulled[:, :, HEADS:SROW], pulled[:, :, HEADS:SROW], tall(n_clamped[:], NS), ALU.mult))
            then(TS(nonempty[:], n_clamped[:], 0.0, None, ALU.is_gt))
            masked(nonempty[:])
            merge("x", "faded", 1)

            then(dve.memset(e_a[:, :, 0:1], 0.0))
            dve.memset(chain[:], 0.0).then_inc(S("experts_done"), 1)
            dve.wait_ge(S("experts_done"), 1)
            turns = early_value(dve, 1)
            with dve.Fori(0, turns) as i:
                own = Own(dve, S("vec_turn"), 0, i, VEC_TURN)
                acted = lambda n: dve.wait_ge(S("act_scan"), every(i, ACT_TURN, n))

                then(TS(ck[1][:], key_a[:, bass.ds(i * CW, CW)], CL_BASE, None, ALU.min))
                then(TS(same[:], ck[1][:, ::-1], const[:, C_SIGN + 1:C_SIGN + 2], None, ALU.mult))
                STT(ck[0][:], ck[1][:], const[:, C_SIGN:C_SIGN + 1], same[:], ALU.mult, ALU.add)\
                    .then_inc(S("to_columns"), 1)

                def steps_of(source, bits, target, last):
                    for j in range(bits - 1, -1, -1):
                        d = 1 << j
                        a, o = (v.rearrange("p (b w) -> p b w", w=2 * d) for v in (source, ck[target][:]))
                        hi = a[:, :, d:2 * d]
                        if j == bits - 1:
                            hi_sb = pen[:, 0:CW // 2].rearrange("p (b w) -> p b w", w=d)
                            then(dve.tensor_copy(hi_sb, hi))
                            hi = hi_sb
                        TT(o[:, :, 0:d], a[:, :, 0:d], hi, ALU.min)
                        ins = TT(o[:, :, d:2 * d], a[:, :, 0:d], hi, ALU.max)
                        if j == 0 and last:
                            ins.then_inc(S(last), 1)
                        else:
                            then(ins)
                        source, target = ck[target][:], 1 - target
                    return 1 - target

                for k in range(CHUNK_BITS + 1, ALL_BITS + 1):
                    n = k - CHUNK_BITS
                    dve.wait_ge(S("in_columns"), every(i, 7, n))
                    assert steps_of(ps[:, 0, 0:CW], n, 1, "to_rows") == n % 2
                    dve.wait_ge(S("in_rows"), every(i, 7, n))
                    assert steps_of(ps[:, 1, 0:CW], CHUNK_BITS, 0, None) == 1
                    if k < ALL_BITS:
                        TS(ck[0][:], ck[1][:], sign(k), None, ALU.mult).then_inc(S("to_columns"), 1)

                then(dve.tensor_copy(ki[:], ck[1][:]))
                TS(si[:], ki[:], N_TOK - 1, None, ALU.bitwise_and)
                then(TS(ti[:], ki[:], 12, None, ALU.logical_shift_right))
                then(dve.tensor_copy(dst_f[:], ti[:]))
                TS(i_first[:], dst_f[:, 0:1], LAST, None, ALU.min).then_inc(S("src_ready"), 1)
                node_of(ki, 12, 19)
                one_hots(0, "onehots2")
                dve.wait_ge(S("counted2"), every(i, 2, 1))
                one_hots(1, "onehots2")
                TT(same[:, 1:], dst_f[:, 1:], dst_f[:, :-1], ALU.is_equal)
                then(dve.memset(same[:, 0:1], 1.0))
                then(TS(pen[:], same[:], -LOW, LOW, ALU.mult, ALU.add))
                dve.wait_ge(S("counted2"), every(i, 2, 2))
                dve.tensor_copy(hist[:], ps[:, 2, 0:NT]).then_inc(S("hist_ready"), 1)
                dve.wait_ge(S("hist_ready"), every(i, 1, 1))
                then(TS(nonempty[:], hist[:], 0.0, None, ALU.is_gt))
                dve.wait_ge(S("cum_out"), every(i, 1, 1))
                then(dve.tensor_copy(pos[:, 0, :], ps[:, 2, 96:96 + NT]))
                then(dve.tensor_tensor_scan(pos[:, 1, :], ones[:, 0:NT], pos[:, 0, :], 0.0, ALU.mult, ALU.add))
                then(TT(pos[:, 1, :], pos[:, 1, :], pos[:, 0, :], ALU.subtract))
                then(TT(pos[:, 1, :], pos[:, 1, :], ps[:, 2, 64:64 + NT], ALU.add))
                TT(pos[:, 2, :], pos[:, 1, :], hist[:], ALU.subtract)
                then(TS(i_end[:], pos[:, 1, :], 1.0, 0.0, ALU.subtract, ALU.max))
                then(TS(pos[:, 3, :], nonempty[:], -OOB, OOB, ALU.mult, ALU.add))
                TT(i_start[:], pos[:, 2, :], pos[:, 3, :], ALU.add).then_inc(S("pos_ready"), 1)

                dve.wait_ge(S("ad_in"), every(i, 16, 16))
                dve.wait_ge(S("ad_first_in"), every(i, 16, 16))
                then(TS(e_new[:, 0, :], same[:], -1.0, 1.0, ALU.mult, ALU.add))
                then(TT(ad_at, ad_at, tall(e_new[:, 0, :], HEADS), ALU.mult))
                for h in range(HEADS):
                    ins = dve.tensor_tensor_scan(e_ad[:, h, :], same[:], ad_at[:, :, h], ad_first[:, h:h + 1], ALU.mult, ALU.add)
                then(ins)
                dve.wait_ge(S("rows_in"), every(i, 16 * CW, 16 * CW))
                turn_f = lambda v: v.rearrange("p f h -> p h f")
                m_run = turn_f(seg[:, :, 0:HEADS])
                then(TT(e_val, turn_f(rows[:, :, 0:HEADS]), e_ad, ALU.add))
                leaky(e_val)
                for h in range(HEADS):
                    ins = dve.tensor_tensor_scan(seg[:, :, h], pen[:], e_val[:, h, :], LOW, ALU.add, ALU.max)
                then(ins)
                TT(e_w, e_val, m_run, ALU.subtract)
                then(dve.memset(e_a[:, :, 0:1], 0.0))
                then(TT(e_a[:, :, 1:], m_run[:, :, 0:CW - 1], m_run[:, :, 1:], ALU.subtract))
                TS(e_a, e_a, 0.0, None, ALU.min).then_inc(S("shift_ready"), 1)
                acted(1)
                TT(e_a, e_a, same[:].unsqueeze(1).to_broadcast([P, HEADS, CW]), ALU.mult)
                h_of = rows[:, :, HEADS:ROW].rearrange("p f (h c) -> p f h c", h=HEADS)
                flat_w = e_w.rearrange("p h f -> p f h")
                then(TT(h_of, h_of, tall(flat_w, NE_EXP), ALU.mult))
                for h in range(HEADS):
                    for c in range(1 + NE_EXP):
                        x = e_w[:, h, :] if c == 0 else h_of[:, :, h, c - 1]
                        ins = dve.tensor_tensor_scan(seg[:, :, HEADS + h * 5 + c], e_a[:, h, :], x, 0.0, ALU.mult, ALU.add)
                then(ins)

                five = lambda v: v.rearrange("p (h c) -> p h c", h=HEADS)
                dve.tensor_copy(five(ends[:, 0, :]), tall(seg[:, CW - 1, 0:HEADS], 5))
                dve.tensor_copy(ends[:, 1, :], seg[:, CW - 1, HEADS:SROW])
                dve.tensor_copy(ends[:, 2, :], dst_f[:, 0:1].to_broadcast([P, NS]))
                dve.tensor_copy(ends[:, 3, :], dst_f[:, CW - 1:CW].to_broadcast([P, NS])).then_inc(S("ends_ready"), 1)
                dve.wait_ge(S("ends_turned"), every(i, 1, 1))
                e_m, e_s = ps[0:NS, 3, 0:P], ps[0:NS, 3, P:2 * P]
                c_ = lambda q: chain[0:NS, q, :]
                dve.tensor_copy(c_(0), ps[0:NS, 3, 2 * P:3 * P])
                then(dve.tensor_copy(c_(1), ps[0:NS, 3, 3 * P:4 * P]))
                then(TT(c_(2)[:, 1:], c_(1)[:, :-1], c_(0)[:, 1:], ALU.is_equal))
                then(TT(c_(3), c_(1), c_(0), ALU.is_equal))
                then(TT(c_(3), c_(3), c_(2), ALU.mult))
                then(TS(c_(5), c_(3), -LOW, LOW, ALU.mult, ALU.add))
                then(dve.tensor_tensor_scan(c_(6), c_(5), e_m, LOW, ALU.add, ALU.max))
                TT(c_(5), e_m, c_(6), ALU.subtract)
                then(TT(c_(4)[:, 1:], c_(6)[:, :-1], c_(6)[:, 1:], ALU.subtract))
                then(dve.memset(c_(4)[:, 0:1], 0.0))
                TS(c_(4), c_(4), 0.0, None, ALU.min).then_inc(S("chain_shift"), 1)
                acted(2)
                TT(c_(4), c_(4), c_(3), ALU.mult)
                then(TT(c_(5), c_(5), e_s, ALU.mult))
                then(dve.tensor_tensor_scan(c_(7), c_(4), c_(5), 0.0, ALU.mult, ALU.add))
                then(TS(c_(3), c_(2), -LOW, LOW, ALU.mult, ALU.add))
                dve.memset(c_(1)[:, 0:1], 0.0)
                dve.memset(c_(0)[:, 0:1], LOW)
                TT(c_(1)[:, 1:], c_(7)[:, :-1], c_(2)[:, 1:], ALU.mult)
                then(TT(c_(0)[:, 1:], c_(6)[:, :-1], c_(2)[:, 1:], ALU.mult))
                TT(c_(0)[:, 1:], c_(0)[:, 1:], c_(3)[:, 1:], ALU.add).then_inc(S("chain_ready"), 1)
                dve.wait_ge(S("carry_out"), every(i, 1, 1))
                dve.tensor_copy(carry[:, 0, :], ps[:, 5, 0:NS])
                dve.tensor_copy(carry[:, 1, :], ps[:, 5, P:P + NS])
                then(TS(pen[:], dst_f[:], dst_f[:, 0:1], 1.0, ALU.is_equal, ALU.subtract))
                then(TS(pen[:], pen[:], -LOW, None, ALU.mult))
                then(TT(e_ad, pen[:].unsqueeze(1).to_broadcast([P, HEADS, CW]), tall(five(carry[:, 0, :])[:, :, 0], CW), ALU.add))
                then(TT(e_new, e_ad, m_run, ALU.max))
                TT(e_w, e_ad, e_new, ALU.subtract)
                TT(e_a, m_run, e_new, ALU.subtract).then_inc(S("carry_shift"), 1)
                acted(3)
                dve.tensor_copy(m_run, e_new)
                s_run = seg[:, :, HEADS:SROW].rearrange("p f (h c) -> p f h c", h=HEADS)
                TT(s_run, s_run, tall(e_a.rearrange("p h f -> p f h"), 5), ALU.mult)
                t4 = tmp_s.rearrange("p f (h c) -> p f h c", h=HEADS)
                then(TT(t4, tall(flat_w, 5), five(carry[:, 1, :]).unsqueeze(1).to_broadcast([P, CW, HEADS, 5]), ALU.mult))
                TT(s_run, s_run, t4, ALU.add).then_inc(S("seg_ready"), 1)

                dve.wait_ge(S("pulled_in"), every(i, 16 * NT, 16 * NT))
                masked(nonempty[:])
                merge("x", "act_scan", every(i, ACT_TURN, 4))
                dve.memset(c_(2)[:, 0:1], 0.0).then_inc(S("turn_done"), 1)
                dve.wait_ge(S("turn_done"), every(i, 1, 1))
                assert own.n == VEC_TURN, own.n

            own = Own(dve, S("vec_end"))
            heads4 = lambda v: v.rearrange("p t (h c) -> p t h c", h=HEADS)
            then(TS(new_m[:], acc_s[:, :, :, 0], 1e-16, None, ALU.add))
            then(dve.reciprocal(new_m[:], new_m[:]))
            then(TT(heads4(agg), acc_s[:, :, :, 1:], tall(new_m[:], NE_EXP), ALU.mult))
            then(TT(agg, agg, across(B_GAT, 16, NT), ALU.add))
            then(dve.tensor_reduce(gate[:, 0, :], agg, X, ALU.add))
            then(TS(gate[:, 0, :], gate[:, 0, :], -1.0 / 16, None, ALU.mult))
            then(TT(agg2, agg, tall(gate[:, 0, :], 16), ALU.add))
            then(TT(agg, agg2, agg2, ALU.mult))
            then(dve.tensor_reduce(gate[:, 0, :], agg, X, ALU.add))
            TS(gate[:, 1, :], gate[:, 0, :], 1.0 / 16, LN_EPS, ALU.mult, ALU.add).then_inc(S("var_ready"), 1)
            dve.wait_ge(S("rstd_ready"), N_VAR)
            then(TT(agg, agg2, tall(gate[:, 2, :], 16), ALU.mult))
            then(TT(agg, agg, across(B_LG, 16, NT), ALU.mult))
            then(TT(agg, agg, across(B_LB, 16, NT), ALU.add))
            score = gate[:, 4:8, :]
            then(dve.tensor_reduce(score.rearrange("p e t -> p t e"), agg.rearrange("p t (h e) -> p t e h", h=HEADS), X, ALU.add))
            then(TS(score, score, 1.0 / HEADS, None, ALU.mult))
            rank = gate[:, 12:16, :]
            for x in range(NE_EXP):
                then(dve.memset(rank[:, x, :], float(x)))
            for a in range(NE_EXP):
                for b in range(a + 1, NE_EXP):
                    then(TT(gate[:, 0, :], score[:, b, :], score[:, a, :], ALU.is_gt))
                    then(TT(rank[:, a, :], rank[:, a, :], gate[:, 0, :], ALU.add))
                    then(TT(rank[:, b, :], rank[:, b, :], gate[:, 0, :], ALU.subtract))
            then(TS(rank, rank, 2.0, None, ALU.is_lt))
            then(dve.tensor_reduce(gate[:, 1, :], score.rearrange("p e t -> p t e"), X, ALU.max))
            soft = gate[:, 8:12, :]
            TT(soft, score, gate[:, 1, :].unsqueeze(1).to_broadcast([P, NE_EXP, NT]), ALU.subtract).then_inc(S("soft_shift"), 1)
            dve.wait_ge(S("soft_exp"), 1)
            then(TT(soft, soft, rank, ALU.mult))
            then(dve.tensor_reduce(gate[:, 1, :], soft.rearrange("p e t -> p t e"), X, ALU.add))
            then(dve.reciprocal(gate[:, 1, :], gate[:, 1, :]))
            then(TT(soft, soft, gate[:, 1, :].unsqueeze(1).to_broadcast([P, NE_EXP, NT]), ALU.mult))
            y4 = y_exp[:].rearrange("p t (e d) -> p t e d", e=NE_EXP)
            then(TT(y4, y4, tall(soft.rearrange("p e t -> p t e"), D), ALU.mult))
            for x in range(NE_EXP):
                ins = TT(h2[:], h2[:], y4[:, :, x, :], ALU.add)
                if x < NE_EXP - 1:
                    then(ins)
            ins.then_inc(S("result"), 1)


def kernel(**inputs):
    import numpy as np
    import concourse.bacc as bacc
    from concourse.bass_utils import run_bass_kernel_spmd as run

    v = {k: np.asarray(a) for k, a in inputs.items()}
    p = np.arange(P)
    const = np.zeros((P, C_WIDTH), np.float32)
    const[:, C_ID:C_ID + P] = np.eye(P)
    const[:, C_TRI:C_TRI + P] = p[:, None] <= p[None, :]
    const[:, C_ONE:C_ONE + P] = 1
    sgn = {k: 1 - 2 * ((p >> (k - CHUNK_BITS)) & 1) for k in range(CHUNK_BITS + 1, ALL_BITS + 1)}
    const[:, C_SIGN] = sgn[9] * (p % 2 == 0)
    const[:, C_SIGN + 1] = sgn[9] * (p % 2 == 1)
    for k in range(CHUNK_BITS + 1, ALL_BITS):
        const[:, C_SIGN + k - CHUNK_BITS + 1] = sgn[k] * sgn[k + 1]
    ffn = lambda n: v["L0_ffn_" + n]
    tok = lambda n: v["L0_tok_" + n]
    attn = lambda n: v["L0_attn_" + n]
    par = np.concatenate([a.ravel() for a in (
        tok("ln_g"), tok("ln_b"), ffn("att_src"), ffn("att_dst"), ffn("b_gat"), ffn("ln_gamma"), ffn("ln_beta"),
        ffn("b2"), tok("W_o"), tok("W_dt"))])[None, :]
    columns = lambda w: w.transpose(1, 0, 2).reshape(D, -1)
    arrays = {
        "idx": v["x"].T,
        "src": v["L0_ffn_edge_index"][0].reshape(P, EC),
        "dst": v["L0_ffn_edge_index"][1].reshape(P, EC),
        "const": const,
        "par": par,
        "outcomes": v["fside_BS_outcomes"],
        "times": v["fside_BS_timestamps"],
        "h_q": tok("h_q"),
        "w_tok": np.concatenate([tok("W_proj_w").T, tok("W_proj_b")[None, :]]),
        "w_kq": np.concatenate([columns(attn("Wks")), columns(attn("Wqs"))], axis=1),
        "w_vt": attn("Wvs").transpose(2, 0, 1).reshape(D, -1),
        "w_o": columns(attn("Wo")),
        "w_hid": np.concatenate([columns(ffn("W1")), ffn("b1").reshape(1, -1)]),
        "w_outp": ffn("W2").transpose(1, 0, 2).reshape(HID, -1),
        "w_gat": ffn("W_gat"),
        "zeros": np.zeros((1, CW * HEADS), np.float32),
    }
    arrays = {k: np.ascontiguousarray(a) for k, a in arrays.items()}
    nc = bacc.Bacc("TRN2", target_bir_lowering=False, num_devices=1)
    A = {k: nc.dram_tensor("in_" + k, a.shape, mybir.dt.from_np(a.dtype), kind="ExternalInput").ap()
         for k, a in arrays.items()}
    out = nc.dram_tensor("out", (NT, P, D), F32, kind="ExternalOutput").ap()
    build(nc, A, out)
    r = run(nc, [{"in_" + k: a for k, a in arrays.items()}], core_ids=[0])
    return r.results[0]["out"]
```

```python
from contextlib import ExitStack

import concourse.bass as bass
from concourse import mybir

P = 128
N_TOK, D, N_Q = 4096, 64, 25000
NT = N_TOK // P
TG = 4
NG = NT // TG
GW = TG * P
H, K = 8, 32
HF = H // 4
FEATS = D + 3
NE_EXP, HEADS, HID = 4, 4, 128
N_EDGES = 262144
EC = N_EDGES // P
CW = 256
SW = 144
PITCH = 2 * P * SW
GROUPS = 4
GC = SW // GROUPS
OH = 64
N_CHUNK = EC // CW
LOCAL_BITS = 11
CHUNK_BITS = 8
ALL_BITS = CHUNK_BITS + 7
CL_BASE = float(1 << 24)
BAD = float(1 << 25)
LAST = float(N_TOK - 1)
ROW = HEADS + HEADS * NE_EXP
NS = HEADS * (1 + NE_EXP)
SROW = HEADS + NS
LOW = -1e30
LN_EPS = 1e-5
ATT_EPS = 1e-9
OOB = 1e6
N_VAR = 3 * NG + 1
ACT_TURN = GROUPS + 3
EXPERTS_FIRST = 24
FILL = 2
VEC_HIST = 5
VEC_SORT = 92
VEC_TURN = 69

F32 = mybir.dt.float32
BF16 = mybir.dt.bfloat16
I32 = mybir.dt.int32
ALU = mybir.AluOpType
ACT = mybir.ActivationFunctionType
X = mybir.AxisListType.X

C_ID, C_TRI, C_ONE, C_ID1, C_TRI1, C_SIGN = (P * n for n in range(6))
C_WIDTH = 5 * P + 8
B_G, B_B, B_SRC, B_DST, B_GAT, B_LG, B_LB, B_B2 = 0, 64, 128, 144, 160, 176, 192, 208
B_WO, B_WDT = 464, 465
B_WIDTH = 466


class Own:

    def __init__(self, eng, sem, before=0, turn=None, per_turn=0):
        self.eng, self.sem, self.n, self.before, self.turn, self.per_turn = eng, sem, 0, before, turn, per_turn

    def did(self, ins):
        ins.then_inc(self.sem, 1)
        self.n += 1

    def settle(self):
        at = self.before + self.n
        self.eng.wait_ge(self.sem, at if self.turn is None else self.turn * self.per_turn + at)


def every(turn, per_turn, n):
    return turn * per_turn + n


def build(nc, A, out):
    with ExitStack() as ctx:
        def sb(name, shape, dt=F32):
            return ctx.enter_context(nc.sbuf_tensor(name, shape, dt))

        def sem(name):
            return ctx.enter_context(nc.semaphore(name))

        const = sb("const", [P, C_WIDTH])
        par = sb("par", [P, B_WIDTH])
        ident, tri, ones, ident1, tri1 = (const[:, c:c + P] for c in (C_ID, C_TRI, C_ONE, C_ID1, C_TRI1))
        key_a = sb("key_a", [P, EC])
        key_b = sb("key_b", [P, EC])
        h2 = sb("h2", [P, NT, D])
        tab = sb("tab", [P, NT, ROW])
        a_dst = sb("a_dst", [P, NT, HEADS])
        y_exp = sb("y_exp", [P, NT, NE_EXP * D])
        counts = sb("counts", [P, 4])
        n_turns = sb("n_turns", [1, 4], I32)
        n_clamped = sb("n_clamped", [P, NT])
        acc_m = sb("acc_m", [P, NT, HEADS])
        acc_s = sb("acc_s", [P, NT, HEADS, 1 + NE_EXP])
        last_row = sb("last_row", [P, ROW])
        w_hid = sb("w_hid", [D + 1, NE_EXP * HID])
        w_outp = sb("w_outp", [HID, NE_EXP * D])
        w_gat = sb("w_gat", [D, HEADS * NE_EXP])

        arena = sb("arena", [P, 28 * 1024])
        used = [0]

        def cut(shape, dt=F32, rows=P):
            n = 1
            for s in shape:
                n *= s
            words = n if dt != BF16 else n // 2
            v = arena[0:rows, used[0]:used[0] + words]
            used[0] += words
            assert used[0] <= 28 * 1024, used[0]
            if dt != F32:
                v = v.bitcast(dt)
            if len(shape) > 1:
                names = "abcd"[:len(shape)]
                v = v.rearrange(f"p ({' '.join(names)}) -> p {' '.join(names)}", **dict(zip(names, shape)))
            return v

        emb = cut([NT, D])
        cat_t = cut([N_TOK], rows=FEATS)
        h1 = cut([NT, D])
        exp_kq, relu_kq = cut([4, GW]), cut([4, GW])
        kq = cut([4, GW])
        vals = cut([2, H, D + 1])
        att = cut([2, 4, 2, P])
        w_tok = cut([D], rows=FEATS)
        w_kq = cut([4 * P], rows=D)
        w_vt, w_o, w_vo = (cut([H * D], rows=D) for _ in range(3))
        x_t = cut([GW], rows=D)
        ffn_at = used[0]
        src_i, dst_i, t_a, t_b = cut([EC], I32), cut([EC], I32), cut([EC]), cut([EC])
        used[0] = ffn_at
        x2_t = cut([N_TOK], rows=D + 1)
        hid = cut([NE_EXP, GW])
        pulled = cut([NT, SROW])
        gate = cut([16, NT])
        agg, agg2 = (cut([NT, HEADS * NE_EXP]) for _ in range(2))
        used[0] = 0
        oh_lo, oh_hi = cut([OH, CW], BF16), cut([OH, CW], BF16)
        after_hot = used[0]
        used[0] = 0
        seg = cut([SW, SROW])
        e_ad, e_val, e_new, e_w, e_a = (cut([HEADS, SW]) for _ in range(5))
        ad_at = cut([SW, HEADS])
        assert used[0] <= after_hot
        used[0] = after_hot
        rows = cut([SW, ROW])
        assert used[0] <= ffn_at
        tmp_s = rows

        cen = sb("cen", [P, TG, D])
        sq = sb("sq", [P, TG, D])
        x2 = sb("x2", [P, TG, D])
        stat = sb("stat", [P, 4, TG])
        half = sb("half", [P, NT])
        feats = sb("feats", [NT, 2, P])
        q_idx = sb("q_idx", [P, NT], I32)
        q_f = sb("q_f", [P, NT])
        nv = sb("nv", [P, 2, 4, D])
        att_den = sb("att_den", [P, 2, H])
        prod = sb("prod", [P, TG, HEADS * NE_EXP])

        ck = [sb("ck0", [P, CW]), sb("ck1", [P, CW])]
        wk = sb("wk", [P, SW])
        ki = sb("ki", [P, CW], I32)
        ti = sb("ti", [P, CW], I32)
        si = sb("si", [P, CW], I32)
        tb, lb = sb("tb", [P, CW], BF16), sb("lb", [P, CW], BF16)
        dst_f = sb("dst_f", [P, SW])
        same = sb("same", [P, SW])
        mirror = sb("mirror", [P, CW])
        pen = sb("pen", [P, SW])
        hist = sb("hist", [P, NT])
        hist64 = sb("hist64", [OH, OH])
        clamped64 = sb("clamped64", [OH, OH])
        pos = sb("pos", [P, 4, NT])
        i_start, i_end = sb("i_start", [P, NT], I32), sb("i_end", [P, NT], I32)
        nonempty = sb("nonempty", [P, NT])
        i_first = sb("i_first", [P, 1], I32)
        ad_first = sb("ad_first", [P, HEADS])
        ends = sb("ends", [P, 4, NS])
        chain = sb("chain", [P, 8, P])
        carry = sb("carry", [P, 2, NS])
        new_m = sb("new_m", [P, NT, HEADS])
        fade = sb("fade", [P, 2, NT, HEADS])

        ps = ctx.enter_context(nc.psum_tensor("ps", [P, 8, 512], F32))

        d_tab = nc.dram_tensor("d_tab", [N_TOK, ROW], F32).ap()
        d_keys = nc.dram_tensor("d_keys", [N_CHUNK * PITCH], F32).ap()
        d_ad = nc.dram_tensor("d_ad", [P * SW, HEADS], F32).ap()
        d_adrow = nc.dram_tensor("d_adrow", [N_TOK, HEADS], F32).ap()
        d_seg = nc.dram_tensor("d_seg", [P * SW, SROW], F32).ap()

        made = {}

        def S(name):
            if name not in made:
                made[name] = sem(name)
            return made[name]

        block = ctx.enter_context(nc.Block())
        tall = lambda ap, n: ap.unsqueeze(len(ap.shape)).to_broadcast(list(ap.shape) + [n])

        def sign(k):
            return const[:, C_SIGN + k - CHUNK_BITS + 1:C_SIGN + k - CHUNK_BITS + 2]

        def number(eng, which):
            eng.wait_ge(S("n_turns_set"), 3)
            return eng.value_load(n_turns[0:1, which:which + 1], min_val=1, max_val=(N_CHUNK, N_CHUNK, 2 * N_CHUNK)[which])

        def further(eng, which, body):
            turns = number(eng, which)
            with eng.If(turns > 1):
                with eng.Fori(1, turns) as i:
                    body(i)

        order = ["vo", ("turn", 0), ("token", 0)]
        for g in range(NG):
            order += [("x_t", g)] + [("kq", g, m) for m in range(4)] + [("values", TG * g + k) for k in range(TG)]
            if g < NG - 1:
                order += [("turn", g + 1), ("token", g + 1)]
            if g:
                order += [("x2_t", g - 1), ("nodes", g - 1)]
        order += [("x2_t", NG - 1), ("nodes", NG - 1)]
        order += [("hidden", g, x) for g in range(NG) for x in range(NE_EXP)]
        nth = {item: n + 1 for n, item in enumerate(order)}

        @block.sync
        def _(sp):
            sp.dma_start(q_idx[:], A["idx"]).then_inc(S("idx_in"), 16)
            sp.dma_start(src_i, A["src"]).then_inc(S("src_in"), 16)
            sp.dma_start(dst_i, A["dst"]).then_inc(S("dst_in"), 16)
            sp.dma_start(const[:], A["const"]).then_inc(S("const_in"), 16)
            sp.dma_start(par[:], A["par"].to_broadcast([P, B_WIDTH])).then_inc(S("par_in"), 16)
            sp.dma_start(feats[:, 0, :], A["outcomes"]).then_inc(S("feats_in"), 16)
            sp.dma_start(feats[:, 1, :], A["times"]).then_inc(S("feats_in"), 16)
            for dst, name in ((w_tok, "w_tok"), (w_kq, "w_kq"), (w_vt, "w_vt"), (w_o, "w_o"),
                              (w_hid[:], "w_hid"), (w_outp[:], "w_outp"), (w_gat[:], "w_gat")):
                sp.dma_start(dst, A[name]).then_inc(S("weights_in"), 16)
            sp.dma_start(d_ad.rearrange("(p f) h -> p (f h)", p=P), A["zeros"].to_broadcast([P, SW * HEADS]))\
              .then_inc(S("zero_written"), 16)
            sp.dma_start(d_keys.rearrange("(c n) -> c n", c=N_CHUNK)[:, P * CW:PITCH],
                         A["no_keys"].to_broadcast([N_CHUNK, PITCH - P * CW])).then_inc(S("no_keys_written"), 16)
            sp.wait_ge(S("feats_done"), 2)
            for r in range(2):
                sp.dma_start(cat_t[D + r:D + r + 1, :], feats[:, r, :]).then_inc(S("cat_rows"), 16)
            sp.wait_ge(S("tab_ready"), NG)
            sp.dma_start(d_tab.rearrange("(t p) r -> p t r", p=P), tab[:]).then_inc(S("tab_written"), 16)
            sp.dma_start(d_adrow.rearrange("(t p) r -> p t r", p=P), a_dst[:]).then_inc(S("adrow_written"), 16)

            def wait(name, value):
                sp.wait_ge(S(name), value)
                sp.sem_inc(S("sync_passed"), 1)

            def store_chunk(i):
                wait("chunk_sorted", every(i, 1, 1))
                sp.dma_start(d_keys[bass.ds(i * PITCH, P * CW)].rearrange("(p f) -> p f", p=P), ck[1][:])\
                  .then_inc(S("keys_stored"), 16)

            def window(i, later):
                if later:
                    wait("window_read", every(i, 1, 0))
                sp.dma_start(wk[:], d_keys[bass.ds(i * (P * SW), P * SW)].rearrange("(p f) -> p f", p=P))\
                  .then_inc(S("window_in"), 16)
                wait("hot_free", every(i, 1, 1))
                wait("ad_scattered", every(i, 16 * NT, 16 * NT))
                sp.dma_start(ad_at.rearrange("p f h -> p (f h)"), d_ad.rearrange("(p f) h -> p (f h)", p=P))\
                  .then_inc(S("ad_in"), 16)
                wait("seg_ready", every(i, 1, 1))
                sp.dma_start(d_seg.rearrange("(p f) s -> p (f s)", p=P), seg.rearrange("p f s -> p (f s)"))\
                  .then_inc(S("seg_written"), 16)

            store_chunk(0)
            further(sp, 1, store_chunk)
            sp.wait_ge(S("no_keys_written"), 16)
            sp.wait_ge(S("keys_stored"), 16)
            further(sp, 1, lambda i: wait("keys_stored", every(i, 16, 16)))
            sp.wait_ge(S("tab_written"), 16)
            sp.dma_start(last_row[:], d_tab[N_TOK - 1:N_TOK, :].to_broadcast([P, ROW])).then_inc(S("last_row_in"), 16)
            window(0, False)
            further(sp, 2, lambda i: window(i, True))
            sp.wait_ge(S("result"), 1)
            sp.dma_start(out.rearrange("b s d -> s b d"), h2[:]).then_inc(S("stored"), 16)
            sp.wait_ge(S("stored"), 16)

        @block.gpsimd
        def _(pool):
            pool.memset(half[:], -0.5).then_inc(S("half_set"), 1)
            pool.wait_ge(S("idx_ready"), 1)
            for t in range(NT):
                pool.indirect_dma_start(out=emb[:, t, :], out_offset=None, in_=A["h_q"],
                                        in_offset=bass.IndirectOffsetOnAxis(q_idx[:, t:t + 1], 0))\
                    .then_inc(S(f"emb_in{t // TG}"), 16)
            pool.wait_ge(S("half_set"), 1)
            n_pow = 0

            def rsqrt():
                nonlocal n_pow
                n_pow += 1
                pool.wait_ge(S("var_ready"), n_pow)
                pool.tensor_tensor(stat[:, 2, :], stat[:, 1, :], half[:, 0:TG], ALU.pow).then_inc(S("rstd_ready"), 1)

            def mask(b):
                pool.wait_ge(S("att_ready"), b + 1)
                v = att[:, b % 2].rearrange("p j m s -> p (j m) s")
                pool.affine_select(out=v, in_=v, compare_op=ALU.is_ge, fill=0.0, base=0,
                                   pattern=[[0, H], [1, P]], channel_multiplier=-1).then_inc(S("masked"), 1)

            rsqrt()
            rsqrt()
            for g in range(NG):
                if g:
                    rsqrt()
                for b in range(TG):
                    mask(TG * g + b)
                if g < NG - 1:
                    rsqrt()
                    rsqrt()
            rsqrt()

            pool.wait_ge(S("tab_written"), 16)
            pool.wait_ge(S("adrow_written"), 16)
            pool.wait_ge(S("zero_written"), 16)

            def window(i):
                def wait(name, value):
                    pool.wait_ge(S(name), value)
                    pool.sem_inc(S("pool_passed"), 1)

                wait("src_ready", every(i, 1, 1))
                pool.indirect_dma_start(out=ad_first[:], out_offset=None, in_=d_adrow,
                                        in_offset=bass.IndirectOffsetOnAxis(i_first[:, 0:1], 0))\
                    .then_inc(S("ad_first_in"), 16)
                for f in range(SW):
                    if f == 2 * GC:
                        wait("pos_ready", every(i, 1, 1))
                        for t in range(NT):
                            pool.indirect_dma_start(out=d_ad, in_=a_dst[:, t, :], in_offset=None,
                                                    out_offset=bass.IndirectOffsetOnAxis(i_start[:, t:t + 1], 0),
                                                    bounds_check=P * SW - 1, oob_is_err=False)\
                                .then_inc(S("ad_scattered"), 16)
                    pool.indirect_dma_start(out=rows[:, f, :], out_offset=None, in_=d_tab,
                                            in_offset=bass.IndirectOffsetOnAxis(si[:, f:f + 1], 0))\
                        .then_inc(S(f"rows_in{f // GC}"), 16)
                wait("seg_written", every(i, 16, 16))
                for t in range(NT):
                    pool.indirect_dma_start(out=pulled[:, t, :], out_offset=None, in_=d_seg,
                                            in_offset=bass.IndirectOffsetOnAxis(i_end[:, t:t + 1], 0))\
                        .then_inc(S("pulled_in"), 16)
                wait("turn_done", every(i, 1, 1))

            window(0)
            further(pool, 2, window)
            pool.wait_ge(S("var_ready"), N_VAR)
            pool.tensor_tensor(gate[:, 2, :], gate[:, 1, :], half[:], ALU.pow).then_inc(S("rstd_ready"), 1)

        @block.scalar
        def _(act):
            act.wait_ge(S("abs_ready"), 1)
            act.activation(feats[:, 1, :], feats[:, 1, :], ACT.Ln, bias=1.0).then_inc(S("logged"), 1)
            done = 0

            def evacuate(item, *jobs):
                nonlocal done
                done += 1
                assert nth[item] == done, item
                act.wait_ge(S("bank_filled"), done)
                for out_, func, view in jobs:
                    last = act.activation(out_, view(ps[:, (done - 1) % 2, :]), func)
                last.then_inc(S("bank_read"), 1)

            whole = lambda v: v
            lower = lambda v: v[0:D, :]

            def token_part(g):
                evacuate(("turn", g), (cat_t[0:D, g * GW:(g + 1) * GW], ACT.Copy, lower))
                evacuate(("token", g), (h1[:, TG * g:TG * g + TG, :], ACT.Copy,
                                        lambda v: v[:, 0:TG * D].rearrange("p (t d) -> p t d", t=TG)))

            def node_part(g):
                evacuate(("x2_t", g), (x2_t[0:D, g * GW:(g + 1) * GW], ACT.Copy, lower))
                evacuate(("nodes", g), (tab[:, TG * g:TG * g + TG, HEADS:ROW], ACT.Copy,
                                        lambda v: v[:, 0:64].rearrange("p (t c) -> p t c", t=TG)))

            evacuate("vo", (w_vo, ACT.Copy, lower))
            token_part(0)
            for g in range(NG):
                evacuate(("x_t", g), (x_t, ACT.Copy, lower))
                for m in range(4):
                    if g and m == 0:
                        act.wait_ge(S("kq_ready"), 4 * g)
                    evacuate(("kq", g, m), (relu_kq[:, m, :], ACT.Relu, whole), (exp_kq[:, m, :], ACT.Exp, whole))
                for b in range(TG * g, TG * g + TG):
                    act.wait_ge(S("att_out"), b + 1)
                    if b >= 2:
                        act.wait_ge(S("av_out"), b - 1)
                    act.activation(att[:, b % 2], ps[:, 4:8, 0:2 * P].rearrange("p j (m s) -> p j m s", m=2),
                                   ACT.Copy).then_inc(S("att_ready"), 1)
                    if b == 0:
                        act.wait_ge(S("ones_set"), 1)
                    evacuate(("values", b), (vals[:, b % 2, :, 0:D], ACT.Copy, lambda v: v.rearrange("p (h e) -> p h e", h=H)))
                if g < NG - 1:
                    token_part(g + 1)
                if g:
                    node_part(g - 1)
            node_part(NG - 1)
            def experts():
                for g in range(NG):
                    for x in range(NE_EXP):
                        if g and x == 0:
                            act.wait_ge(S("y_out"), 2 * g)
                        evacuate(("hidden", g, x), (hid[:, x, :], ACT.Gelu, whole))
                    for n in range(2 * g, 2 * g + 2):
                        act.wait_ge(S("y_out"), n + 1)
                        act.activation(y_exp[:, 2 * n:2 * n + 2, :], ps[:, 4 + n % 2, :].rearrange("p (t c) -> p t c", t=2),
                                       ACT.Copy).then_inc(S("y_read"), 1)

            def window(i):
                for q in range(GROUPS):
                    act.wait_ge(S("shift_ready"), every(i, GROUPS, q + 1))
                    c = slice(q * GC, (q + 1) * GC)
                    act.activation(e_a[:, :, c], e_a[:, :, c], ACT.Exp)
                    act.activation(e_w[:, :, c], e_w[:, :, c], ACT.Exp).then_inc(S("act_scan"), 1)
                act.wait_ge(S("chain_shift"), every(i, 1, 1))
                act.activation(chain[0:NS, 4:6, :], chain[0:NS, 4:6, :], ACT.Exp).then_inc(S("act_scan"), 1)
                act.wait_ge(S("carry_shift"), every(i, 1, 1))
                act.activation(e_a, e_a, ACT.Exp)
                act.activation(e_w, e_w, ACT.Exp).then_inc(S("act_scan"), 1)
                act.wait_ge(S("fade_shift"), every(i, 1, 2))
                act.activation(fade[:], fade[:], ACT.Exp).then_inc(S("act_scan"), 1)

            experts()
            act.wait_ge(S("fade_shift"), 1)
            act.activation(fade[:], fade[:], ACT.Exp).then_inc(S("faded"), 1)
            window(0)
            further(act, 2, window)
            act.wait_ge(S("soft_shift"), 1)
            act.activation(gate[:, 8:12, :], gate[:, 8:12, :], ACT.Exp).then_inc(S("soft_exp"), 1)

        @block.tensor
        def _(pe):
            pe.wait_ge(S("const_in"), 16)
            pe.wait_ge(S("weights_in"), 7 * 16)
            done = 0

            def bank(item):
                nonlocal done
                done += 1
                assert nth[item] == done, item
                if done > 2:
                    pe.wait_ge(S("bank_read"), done - 2)
                return ps[:, (done - 1) % 2, :]

            def copied(item):
                pe.wait_ge(S("bank_read"), nth[item])

            to = bank("vo")
            for h in range(H):
                last = pe.matmul(to[0:D, h * D:(h + 1) * D], w_vt[:, h * D:(h + 1) * D], w_o[:, h * D:(h + 1) * D],
                                 start=True, stop=True)
            last.then_inc(S("bank_filled"), 1)

            def turn(item, tile_of):
                to = bank(item)
                for k in range(TG):
                    last = pe.transpose(to[0:D, k * P:(k + 1) * P], tile_of(k), ident)
                last.then_inc(S("bank_filled"), 1)

            def token_part(g):
                pe.wait_ge(S(f"emb_in{g}"), 16 * TG)
                turn(("turn", g), lambda k: emb[:, TG * g + k, :])
                if g == 0:
                    pe.wait_ge(S("cat_rows"), 32)
                copied(("turn", g))
                to = bank(("token", g))
                for k in range(TG):
                    t = TG * g + k
                    last = pe.matmul(to[:, k * D:(k + 1) * D], cat_t[:, t * P:(t + 1) * P], w_tok, start=True, stop=True)
                last.then_inc(S("bank_filled"), 1)

            def node_part(g):
                pe.wait_ge(S("x2_ready"), g + 1)
                turn(("x2_t", g), lambda k: x2[:, k, :])
                copied(("x2_t", g))
                to = bank(("nodes", g))
                for k in range(TG):
                    t = TG * g + k
                    last = pe.matmul(to[:, 16 * k:16 * k + 16], x2_t[0:D, t * P:(t + 1) * P], w_gat[:], start=True, stop=True)
                last.then_inc(S("bank_filled"), 1)

            def weigh(b):
                pe.wait_ge(S("masked"), b + 1)
                copied(("values", b))
                if b:
                    pe.wait_ge(S("av_read"), b)
                for h in range(H):
                    j, m = h % 4, h // 4
                    last = pe.matmul(ps[:, 2 + m, j * (D + 1):(j + 1) * (D + 1)], att[:, b % 2, j, m, :],
                                     vals[:, b % 2, h, :], start=True, stop=True)
                last.then_inc(S("av_out"), 1)

            def chunk_turns(i):
                for n in range(1, ALL_BITS - CHUNK_BITS + 1):
                    for ready, done_, bank_, source in (("to_columns", "in_columns", 6, 0), ("to_rows", "in_rows", 7, n % 2)):
                        pe.wait_ge(S(ready), every(i, 7, n))
                        for q in range(2):
                            last = pe.transpose(ps[:, bank_, q * P:(q + 1) * P], ck[source][:, q * P:(q + 1) * P], ident)
                        last.then_inc(S(done_), 1)
                        yield

            token_part(0)
            for g in range(NG):
                pe.wait_ge(S("xa_ready"), g + 1)
                turn(("x_t", g), lambda k: h2[:, TG * g + k, :])
                copied(("x_t", g))
                for m in range(4):
                    pe.matmul(bank(("kq", g, m)), w_kq[:, m * P:(m + 1) * P], x_t, start=True, stop=True)\
                      .then_inc(S("bank_filled"), 1)
                pe.wait_ge(S("kq_ready"), 4 * (g + 1))
                for b in range(TG * g, TG * g + TG):
                    k = b - TG * g
                    if b:
                        pe.wait_ge(S("att_ready"), b)
                    for m in range(2):
                        for j in range(4):
                            last = pe.matmul(ps[:, 4 + j, m * P:(m + 1) * P], kq[32 * j:32 * j + 32, m, k * P:(k + 1) * P],
                                             kq[32 * j:32 * j + 32, 2 + m, k * P:(k + 1) * P], start=True, stop=True)
                    last.then_inc(S("att_out"), 1)
                    pe.matmul(bank(("values", b)), x_t[:, k * P:(k + 1) * P], w_vo, start=True, stop=True)\
                      .then_inc(S("bank_filled"), 1)
                    if k:
                        weigh(b - 1)
                if g < NG - 1:
                    token_part(g + 1)
                if g:
                    node_part(g - 1)
                weigh(TG * g + TG - 1)
            node_part(NG - 1)
            pe.wait_ge(S("av_read"), NT)
            pe.wait_ge(S("counts_ready"), 1)
            for q in range(2):
                last = pe.transpose(ps[0:1, 2, q * P:(q + 1) * P], counts[:, q:q + 1], ident)
            last.then_inc(S("counts_turned"), 1)

            def count(ready, columns, done_, value):
                pe.wait_ge(S(ready), value)
                for f in range(columns):
                    last = pe.matmul(ps[0:OH, 2, 0:OH], oh_lo[:, :, f], oh_hi[:, :, f], start=f == 0, stop=f == columns - 1)
                last.then_inc(S(done_), 1)

            def spread(source, c, low, high):
                v = source[:].rearrange("p (t b) -> p b t", b=2)
                pe.matmul(ps[:, 3, c:c + NT], low, v[:, 0, :], start=True, stop=False)
                return pe.matmul(ps[:, 3, c:c + NT], high, v[:, 1, :], start=False, stop=True)

            def experts():
                pe.wait_ge(S("x2_ones"), 1)
                for g in range(NG):
                    for x in range(NE_EXP):
                        pe.matmul(bank(("hidden", g, x)), w_hid[:, x * HID:(x + 1) * HID], x2_t[:, g * GW:(g + 1) * GW],
                                  start=True, stop=True).then_inc(S("bank_filled"), 1)
                        if x % 2:
                            yield
                    copied(("hidden", g, NE_EXP - 1))
                    for q in range(2):
                        n = 2 * g + q
                        if n >= 2:
                            pe.wait_ge(S("y_read"), n - 1)
                        for k in range(2):
                            for x in range(NE_EXP):
                                last = pe.matmul(ps[:, 4 + n % 2, k * 256 + x * D:k * 256 + (x + 1) * D],
                                                 hid[:, x, (2 * q + k) * P:(2 * q + k + 1) * P],
                                                 w_outp[:, x * D:(x + 1) * D], start=True, stop=True)
                        last.then_inc(S("y_out"), 1)
                        yield

            def window(i, between=None):
                count("onehots2", SW, "counted2", every(i, 1, 1))
                pe.wait_ge(S("hist_ready"), every(i, 1, 1))
                lows = slice(0, OH)
                spread(hist64, 0, ident[lows, :], ident1[lows, :])
                spread(hist64, 64, tri[lows, :], tri1[lows, :])
                spread(hist64, 96, ones[lows, :], ones[lows, :]).then_inc(S("cum_out"), 1)
                if between:
                    between()
                pe.wait_ge(S("ends_ready"), every(i, 1, 1))
                for q in range(4):
                    last = pe.transpose(ps[0:NS, 6, q * P:(q + 1) * P], ends[:, q, :], ident)
                last.then_inc(S("ends_turned"), 1)
                pe.wait_ge(S("chain_ready"), every(i, 1, 1))
                for q in range(2):
                    last = pe.transpose(ps[:, 7, q * P:(q + 1) * P], chain[:, q, :], ident)
                last.then_inc(S("carry_out"), 1)

            def between():
                turns = number(pe, 0)
                with pe.Fori(0, turns) as i:
                    count("onehots", CW, "counted", every(i, 1, 1))
                pe.wait_ge(S("clamped_ready"), 1)
                spread(clamped64, 128, ident[0:OH, :], ident1[0:OH, :]).then_inc(S("clamped_out"), 1)
                for _ in expert_work:
                    pass

            pe.wait_ge(S("att_ready"), NT)
            expert_work = experts()
            for _ in chunk_turns(0):
                next(expert_work)

            def more_turns(i):
                for _ in chunk_turns(i):
                    pass

            further(pe, 1, more_turns)

            for _ in range(EXPERTS_FIRST - 2 * (ALL_BITS - CHUNK_BITS)):
                next(expert_work)
            window(0, between)
            further(pe, 2, window)

        @block.vector
        def _(dve):
            own = Own(dve, S("vec_step"))

            def then(ins):
                own.did(ins)
                own.settle()

            TT, TS, STT = dve.tensor_tensor, dve.tensor_scalar, dve.scalar_tensor_tensor
            dve.memset(cat_t[D:FEATS, :], 1.0)
            dve.memset(counts[:], 0.0)
            dve.wait_ge(S("idx_in"), 16)
            then(dve.tensor_copy(q_f[:], q_idx[:]))
            then(TS(q_f[:], q_f[:], 0.0, float(N_Q - 1), ALU.max, ALU.min))
            dve.tensor_copy(q_idx[:], q_f[:]).then_inc(S("idx_ready"), 1)
            dve.wait_ge(S("feats_in"), 32)
            STT(feats[:, 1, :], feats[:, 1, :], -1.0, feats[:, 1, :], ALU.mult, ALU.max).then_inc(S("abs_ready"), 1)
            dve.wait_ge(S("par_in"), 16)
            then(TS(feats[:, 0, :], feats[:, 0, :], par[0:NT, B_WO:B_WO + 1], -5.0, ALU.mult, ALU.max))
            TS(feats[:, 0, :], feats[:, 0, :], 5.0, None, ALU.min).then_inc(S("feats_done"), 1)
            dve.wait_ge(S("logged"), 1)
            then(TS(feats[:, 1, :], feats[:, 1, :], par[0:NT, B_WDT:B_WDT + 1], -5.0, ALU.mult, ALU.max))
            TS(feats[:, 1, :], feats[:, 1, :], 5.0, None, ALU.min).then_inc(S("feats_done"), 1)
            dve.memset(vals[:, :, :, D:D + 1], 1.0).then_inc(S("ones_set"), 1)

            def edge_keys():
                own = Own(dve, S("key_step"))

                def then(ins):
                    own.did(ins)
                    own.settle()

                dve.wait_ge(S("src_in"), 16)
                dve.wait_ge(S("dst_in"), 16)
                dve.tensor_copy(key_b[:], src_i)
                then(dve.tensor_copy(t_a, dst_i))
                yield
                then(TS(t_b, key_b[:], 0.0, float(N_TOK), ALU.is_lt, ALU.mult))
                then(TT(key_b[:], key_b[:], t_b, ALU.add))
                yield
                then(TS(key_b[:], key_b[:], 0.0, LAST, ALU.max, ALU.min))
                TS(src_i, key_b[:], LAST, None, ALU.is_ge)
                TS(t_b, t_a, LAST, None, ALU.is_gt)
                yield
                then(STT(key_a[:], t_a, float(N_TOK), key_b[:], ALU.mult, ALU.add))
                then(STT(dst_i, t_a, 0.0, t_b, ALU.is_lt, ALU.max))
                yield
                then(TS(t_a, t_a, 2.0, CL_BASE, ALU.mult, ALU.add))
                then(dve.copy_predicated(key_a[:], src_i, t_a))
                yield
                then(dve.memset(t_b, BAD))
                then(dve.copy_predicated(key_a[:], dst_i, t_b))
                yield
                TS(t_a, key_a[:], BAD, None, ALU.is_lt)
                then(TS(t_b, key_a[:], CL_BASE, None, ALU.is_lt))
                yield
                then(dve.tensor_reduce(counts[:, 0:1], t_a, X, ALU.add))
                dve.tensor_reduce(counts[:, 1:2], t_b, X, ALU.add).then_inc(S("counts_ready"), 1)
                dve.wait_ge(S("counts_ready"), 1)
                dve.memset(x2_t[D:D + 1, :], 1.0).then_inc(S("x2_ones"), 1)

            def local_sort():
                sorting = Own(dve, S("sort_step"))
                src, dst = key_a, key_b
                for k in range(1, LOCAL_BITS + 1):
                    for j in range(k - 1, -1, -1):
                        d = 1 << j
                        a = src[:].rearrange("p (b w) -> p b w", w=2 * d)
                        o = dst[:].rearrange("p (b w) -> p b w", w=2 * d)
                        hi = a[:, :, 2 * d - 1:d - 1:-1] if j == k - 1 and d > 1 else a[:, :, d:2 * d]
                        if sorting.n:
                            sorting.settle()
                        TT(o[:, :, 0:d], a[:, :, 0:d], hi, ALU.min)
                        sorting.did(TT(o[:, :, d:2 * d], a[:, :, 0:d], hi, ALU.max))
                        src, dst = dst, src
                        yield
                assert src is key_a
                sorting.settle()

            making, sorting_steps = edge_keys(), local_sort()

            def fill(n):
                for _ in range(n):
                    if next(making, True) is True:
                        next(sorting_steps, None)

            n_var = 0

            def normalise(x, o, last=None):
                nonlocal n_var
                then(dve.tensor_reduce(stat[:, 0, :], x, X, ALU.add))
                then(TS(stat[:, 0, :], stat[:, 0, :], -1.0 / D, None, ALU.mult))
                then(TT(cen[:], x, tall(stat[:, 0, :], D), ALU.add))
                then(TT(sq[:], cen[:], cen[:], ALU.mult))
                then(dve.tensor_reduce(stat[:, 3, :], sq[:], X, ALU.add))
                TS(stat[:, 1, :], stat[:, 3, :], 1.0 / D, LN_EPS, ALU.mult, ALU.add).then_inc(S("var_ready"), 1)
                n_var += 1
                fill(1)
                dve.wait_ge(S("rstd_ready"), n_var)
                ins = TT(o, cen[:], tall(stat[:, 2, :], D), ALU.mult)
                if last:
                    ins.then_inc(S(last), 1)
                else:
                    then(ins)

            def across(c, n, mid):
                return par[:, c:c + n].unsqueeze(1).to_broadcast([P, mid, n])

            def token_part(g):
                dve.wait_ge(S("bank_read"), nth[("token", g)])
                t = slice(TG * g, TG * g + TG)
                normalise(h1[:, t, :], sq[:])
                then(TT(sq[:], sq[:], across(B_G, D, TG), ALU.mult))
                own.did(TT(h1[:, t, :], sq[:], across(B_B, D, TG), ALU.add))
                own.settle()
                normalise(h1[:, t, :], h2[:, t, :], "xa_ready")

            def features(g):
                for m in range(4):
                    dve.wait_ge(S("bank_read"), nth[("kq", g, m)])
                    STT(kq[:, m, :], exp_kq[:, m, :], 1.0, relu_kq[:, m, :], ALU.min, ALU.add).then_inc(S("kq_ready"), 1)

            def attended(b):
                dve.wait_ge(S("av_out"), b + 1)
                av = ps[:, 2:4, 0:4 * (D + 1)].rearrange("p m (j e) -> p m j e", j=4)
                d0, d1 = (att_den[:, q, :].rearrange("p (m j) -> p m j", m=2) for q in range(2))
                then(TS(d0, av[:, :, :, D], ATT_EPS, None, ALU.add))
                then(dve.reciprocal(d1, d0))
                dve.tensor_tensor(nv[:], av[:, :, :, 0:D], tall(d1, D), ALU.mult).then_inc(S("av_read"), 1)
                dve.wait_ge(S("av_read"), b + 1)
                then(dve.tensor_reduce(h2[:, b, :], nv[:].rearrange("p m j e -> p e (m j)"), X, ALU.add))
                own.did(TT(h2[:, b, :], h2[:, b, :], h1[:, b, :], ALU.add))

            def second_norm(g):
                own.settle()
                normalise(h2[:, TG * g:TG * g + TG, :], x2[:], "x2_ready")

            def node_part(g):
                t = slice(TG * g, TG * g + TG)
                dve.wait_ge(S("bank_read"), nth[("nodes", g)])
                for c, o in ((B_SRC, tab[:, t, 0:HEADS]), (B_DST, a_dst[:, t, :])):
                    then(TT(prod[:], tab[:, t, HEADS:ROW], across(c, 16, TG), ALU.mult))
                    ins = dve.tensor_reduce(o, prod[:].rearrange("p t (h e) -> p t h e", e=NE_EXP), X, ALU.add)
                    if c == B_DST:
                        ins.then_inc(S("tab_ready"), 1)
                    else:
                        then(ins)

            token_part(0)
            for g in range(NG):
                features(g)
                if g == 1:
                    for _ in making:
                        pass
                if g:
                    second_norm(g - 1)
                for b in range(TG * g, TG * g + 3):
                    fill(FILL)
                    attended(b)
                fill(FILL)
                if g < NG - 1:
                    token_part(g + 1)
                if g:
                    node_part(g - 1)
                attended(TG * g + 3)
            second_norm(NG - 1)
            node_part(NG - 1)
            fill(LOCAL_BITS * LOCAL_BITS)

            dve.wait_ge(S("counts_turned"), 1)
            few = lambda a, b: stat[0:1, 0, a:b]
            then(dve.tensor_reduce(few(0, 1), ps[0:1, 2, 0:P], X, ALU.max))
            then(dve.tensor_reduce(few(1, 2), ps[0:1, 2, P:2 * P], X, ALU.max))
            then(dve.tensor_reduce(few(2, 3), ps[0:1, 2, P:2 * P], X, ALU.add))
            then(TS(few(0, 2), few(0, 2), 1.0, float(CW - 1), ALU.max, ALU.add))
            then(dve.tensor_copy(n_turns[:, 0:2], few(0, 2)))
            TS(n_turns[:, 0:2], n_turns[:, 0:2], CHUNK_BITS, None, ALU.logical_shift_right).then_inc(S("n_turns_set"), 1)
            dve.wait_ge(S("n_turns_set"), 1)
            then(dve.tensor_copy(few(3, 4), n_turns[:, 1:2]))
            TS(few(2, 3), few(2, 3), float(P * SW), None, ALU.is_le).then_inc(S("n_turns_set"), 1)
            dve.wait_ge(S("n_turns_set"), 2)
            STT(n_turns[:, 2:3], few(3, 4), 2.0, few(2, 3), ALU.mult, ALU.subtract).then_inc(S("n_turns_set"), 1)

            def chunk_sort(i, later):
                nonlocal own
                own = Own(dve, S("vec_sort"), 0, i, VEC_SORT) if later else Own(dve, S("vec_sort"))
                if later:
                    dve.wait_ge(S("keys_stored"), every(i, 16, 0))
                keys = key_a[:, bass.ds(i * CW, CW)] if later else key_a[:, 0:CW]
                then(TS(ck[1][:], keys, CL_BASE, None, ALU.min))
                then(TS(mirror[:], ck[1][:, ::-1], const[:, C_SIGN + 1:C_SIGN + 2], None, ALU.mult))
                STT(ck[0][:], ck[1][:], const[:, C_SIGN:C_SIGN + 1], mirror[:], ALU.mult, ALU.add)\
                    .then_inc(S("to_columns"), 1)

                def steps_of(source, bits, target, last):
                    for j in range(bits - 1, -1, -1):
                        d = 1 << j
                        a, o = (v.rearrange("p (b w) -> p b w", w=2 * d) for v in (source, ck[target][:]))
                        hi = a[:, :, d:2 * d]
                        if j == bits - 1:
                            hi_sb = mirror[:, 0:CW // 2].rearrange("p (b w) -> p b w", w=d)
                            then(dve.tensor_copy(hi_sb, hi))
                            hi = hi_sb
                        TT(o[:, :, 0:d], a[:, :, 0:d], hi, ALU.min)
                        ins = TT(o[:, :, d:2 * d], a[:, :, 0:d], hi, ALU.max)
                        if j == 0 and last:
                            ins.then_inc(S(last), 1)
                        else:
                            then(ins)
                        source, target = ck[target][:], 1 - target
                    return 1 - target

                for k in range(CHUNK_BITS + 1, ALL_BITS + 1):
                    n = k - CHUNK_BITS
                    dve.wait_ge(S("in_columns"), every(i, 7, n))
                    assert steps_of(ps[:, 6, 0:CW], n, 1, "to_rows") == n % 2
                    dve.wait_ge(S("in_rows"), every(i, 7, n))
                    done_ = "chunk_sorted" if k == ALL_BITS else None
                    assert steps_of(ps[:, 7, 0:CW], CHUNK_BITS, 0, done_) == 1
                    if k < ALL_BITS:
                        TS(ck[0][:], ck[1][:], sign(k), None, ALU.mult).then_inc(S("to_columns"), 1)
                assert own.n == VEC_SORT, own.n

            chunk_sort(0, False)
            further(dve, 1, lambda i: chunk_sort(i, True))

            def node_of(ints, columns, low, high):
                c = slice(0, columns)
                then(TS(ti[:, c], ints[:, c], low, OH - 1, ALU.logical_shift_right, ALU.bitwise_and))
                then(dve.tensor_copy(lb[:, c], ti[:, c]))
                then(TS(ti[:, c], ints[:, c], high, None, ALU.arith_shift_right))
                then(dve.tensor_copy(tb[:, c], ti[:, c]))

            def one_hots(columns, ready):
                for bits, hot in ((lb, oh_lo), (tb, oh_hi)):
                    for j in range(OH):
                        last = TS(hot[:, j, 0:columns], bits[:, 0:columns], float(j), None, ALU.is_equal)
                last.then_inc(S(ready), 1)

            def leaky(o):
                then(STT(o, o, 0.2, o, ALU.mult, ALU.max))

            def masked(present):
                m, s_ = pulled[:, :, 0:HEADS], pulled[:, :, HEADS:SROW]
                then(TT(m, m, tall(present, HEADS), ALU.mult))
                then(TS(pos[:, 3, :], present, -LOW, LOW, ALU.mult, ALU.add))
                then(TT(m, m, tall(pos[:, 3, :], HEADS), ALU.add))
                then(TT(s_, s_, tall(present, NS), ALU.mult))

            s5 = lambda v: v.rearrange("p t (h c) -> p t h c", h=HEADS)

            def merge(sent, value):
                m, s_ = pulled[:, :, 0:HEADS], s5(pulled[:, :, HEADS:SROW])
                then(TT(new_m[:], acc_m[:], m, ALU.max))
                TT(fade[:, 0], acc_m[:], new_m[:], ALU.subtract)
                TT(fade[:, 1], m, new_m[:], ALU.subtract).then_inc(S("fade_shift"), 1)
                dve.wait_ge(S(sent), value)
                then(dve.tensor_copy(acc_m[:], new_m[:]))
                then(TT(acc_s[:], acc_s[:], tall(fade[:, 0], 1 + NE_EXP), ALU.mult))
                then(TT(s_, s_, tall(fade[:, 1], 1 + NE_EXP), ALU.mult))
                then(TT(acc_s[:], acc_s[:], s_, ALU.add))

            def clamped_part():
                nonlocal own
                before = own
                turns = number(dve, 0)
                with dve.Fori(0, turns) as i:
                    own = Own(dve, S("vec_hist"), 0, i, VEC_HIST)
                    then(TS(ki[:], key_a[:, bass.ds(i * CW, CW)], CL_BASE, 2.0 * N_TOK, ALU.subtract, ALU.min))
                    node_of(ki, CW, 1, 7)
                    one_hots(CW, "onehots")
                    dve.wait_ge(S("counted"), every(i, 1, 1))
                    TT(clamped64[:], clamped64[:], ps[0:OH, 2, 0:OH], ALU.add).then_inc(S("clamped_added"), 1)
                    dve.wait_ge(S("clamped_added"), every(i, 1, 1))
                    assert own.n == VEC_HIST, own.n
                own = Own(dve, S("vec_start"))
                dve.tensor_copy(ti[0:OH, 0:OH], clamped64[:]).then_inc(S("clamped_ready"), 1)
                dve.wait_ge(S("clamped_out"), 1)
                then(dve.tensor_copy(n_clamped[:], ps[:, 3, P:P + NT]))
                then(TT(acc_m[:], tab[:, :, 0:HEADS], a_dst[:], ALU.add))
                leaky(acc_m[:])
                then(dve.memset(acc_s[:], 1.0))
                then(dve.tensor_copy(acc_s[:, :, :, 1:], s5(tab[:, :, HEADS:ROW])))
                dve.wait_ge(S("last_row_in"), 16)
                lr = lambda a, b: last_row[:, a:b].unsqueeze(1).to_broadcast([P, NT, b - a])
                then(TT(pulled[:, :, 0:HEADS], a_dst[:], lr(0, HEADS), ALU.add))
                leaky(pulled[:, :, 0:HEADS])
                p5 = s5(pulled[:, :, HEADS:SROW])
                then(dve.memset(p5[:, :, :, 0:1], 1.0))
                then(dve.tensor_copy(p5[:, :, :, 1:], s5(lr(HEADS, ROW))))
                then(TT(pulled[:, :, HEADS:SROW], pulled[:, :, HEADS:SROW], tall(n_clamped[:], NS), ALU.mult))
                then(TS(hist[:], n_clamped[:], 0.0, None, ALU.is_gt))
                masked(hist[:])
                merge("faded", 1)
                dve.wait_ge(S("y_read"), 2 * NG)
                then(TT(y_exp[:], y_exp[:], across(B_B2, NE_EXP * D, NT), ALU.add))
                then(dve.memset(chain[:], 0.0))
                own = before

            def window(i, later, between=None):
                nonlocal own
                own = Own(dve, S("vec_turn"), 0, i, VEC_TURN) if later else Own(dve, S("vec_turn"))
                acted = lambda n: dve.wait_ge(S("act_scan"), every(i, ACT_TURN, n))

                dve.wait_ge(S("window_in"), every(i, 16, 16))
                w = slice(0, SW)
                dve.tensor_copy(ki[:, w], wk[:]).then_inc(S("window_read"), 1)
                dve.wait_ge(S("window_read"), every(i, 1, 1))
                TS(si[:, w], ki[:, w], N_TOK - 1, None, ALU.bitwise_and)
                then(TS(ti[:, w], ki[:, w], 12, None, ALU.logical_shift_right))
                then(dve.tensor_copy(dst_f[:], ti[:, w]))
                TS(i_first[:], dst_f[:, 0:1], LAST, None, ALU.min).then_inc(S("src_ready"), 1)
                node_of(ki, SW, 12, 18)
                one_hots(SW, "onehots2")
                TT(same[:, 1:], dst_f[:, 1:], dst_f[:, :-1], ALU.is_equal)
                then(dve.memset(same[:, 0:1], 1.0))
                then(TS(pen[:], same[:], -LOW, LOW, ALU.mult, ALU.add))
                dve.wait_ge(S("counted2"), every(i, 1, 1))
                dve.tensor_copy(hist64[:], ps[0:OH, 2, 0:OH]).then_inc(S("hist_ready"), 1)
                dve.wait_ge(S("cum_out"), every(i, 1, 1))
                then(TS(nonempty[:], ps[:, 3, 0:NT], 0.0, None, ALU.is_gt))
                then(dve.tensor_copy(hist[:], ps[:, 3, 0:NT]))
                then(dve.tensor_copy(pos[:, 0, :], ps[:, 3, 96:96 + NT]))
                then(dve.tensor_tensor_scan(pos[:, 1, :], ones[:, 0:NT], pos[:, 0, :], 0.0, ALU.mult, ALU.add))
                then(TT(pos[:, 1, :], pos[:, 1, :], pos[:, 0, :], ALU.subtract))
                then(TT(pos[:, 1, :], pos[:, 1, :], ps[:, 3, 64:64 + NT], ALU.add))
                TT(pos[:, 2, :], pos[:, 1, :], hist[:], ALU.subtract)
                then(TS(i_end[:], pos[:, 1, :], 1.0, 0.0, ALU.subtract, ALU.max))
                then(TS(pos[:, 3, :], nonempty[:], -OOB, OOB, ALU.mult, ALU.add))
                TT(i_start[:], pos[:, 2, :], pos[:, 3, :], ALU.add).then_inc(S("pos_ready"), 1)
                if between:
                    between()

                TS(e_new[:, 0, :], same[:], -1.0, 1.0, ALU.mult, ALU.add).then_inc(S("hot_free"), 1)
                dve.wait_ge(S("ad_in"), every(i, 16, 16))
                dve.wait_ge(S("ad_first_in"), every(i, 16, 16))
                then(TT(ad_at, ad_at, tall(e_new[:, 0, :], HEADS), ALU.mult))
                for h in range(HEADS):
                    ins = dve.tensor_tensor_scan(e_ad[:, h, :], same[:], ad_at[:, :, h], ad_first[:, h:h + 1], ALU.mult, ALU.add)
                then(ins)

                turn_f = lambda v: v.rearrange("p f h -> p h f")
                m_run = turn_f(seg[:, :, 0:HEADS])
                h_all = rows[:, :, HEADS:ROW].rearrange("p f (h c) -> p f h c", h=HEADS)
                flat_w = e_w.rearrange("p h f -> p f h")
                for q in range(GROUPS):
                    c = slice(q * GC, (q + 1) * GC)
                    before = q * GC - 1
                    dve.wait_ge(S(f"rows_in{q}"), every(i, 16 * GC, 16 * GC))
                    then(TT(e_val[:, :, c], turn_f(rows[:, c, 0:HEADS]), e_ad[:, :, c], ALU.add))
                    leaky(e_val[:, :, c])
                    for h in range(HEADS):
                        ins = dve.tensor_tensor_scan(seg[:, c, h], pen[:, c], e_val[:, h, c],
                                                     seg[:, before:before + 1, h] if q else LOW, ALU.add, ALU.max)
                    then(ins)
                    TT(e_w[:, :, c], e_val[:, :, c], m_run[:, :, c], ALU.subtract)
                    if q:
                        then(TT(e_a[:, :, c], m_run[:, :, before:before + GC], m_run[:, :, c], ALU.subtract))
                    else:
                        dve.memset(e_a[:, :, 0:1], 0.0)
                        then(TT(e_a[:, :, 1:GC], m_run[:, :, 0:GC - 1], m_run[:, :, 1:GC], ALU.subtract))
                    TS(e_a[:, :, c], e_a[:, :, c], 0.0, None, ALU.min).then_inc(S("shift_ready"), 1)
                    acted(q + 1)
                    TT(e_a[:, :, c], e_a[:, :, c], same[:, c].unsqueeze(1).to_broadcast([P, HEADS, GC]), ALU.mult)
                    h_of = h_all[:, c]
                    then(TT(h_of, h_of, tall(flat_w[:, c], NE_EXP), ALU.mult))
                    for h in range(HEADS):
                        for x in range(1 + NE_EXP):
                            v = e_w[:, h, c] if x == 0 else h_of[:, :, h, x - 1]
                            r = HEADS + h * (1 + NE_EXP) + x
                            ins = dve.tensor_tensor_scan(seg[:, c, r], e_a[:, h, c], v,
                                                         seg[:, before:before + 1, r] if q else 0.0, ALU.mult, ALU.add)
                    then(ins)

                five = lambda v: v.rearrange("p (h c) -> p h c", h=HEADS)
                dve.tensor_copy(five(ends[:, 0, :]), tall(seg[:, SW - 1, 0:HEADS], 5))
                dve.tensor_copy(ends[:, 1, :], seg[:, SW - 1, HEADS:SROW])
                dve.tensor_copy(ends[:, 2, :], dst_f[:, 0:1].to_broadcast([P, NS]))
                dve.tensor_copy(ends[:, 3, :], dst_f[:, SW - 1:SW].to_broadcast([P, NS])).then_inc(S("ends_ready"), 1)
                dve.wait_ge(S("ends_turned"), every(i, 1, 1))
                e_m, e_s = ps[0:NS, 6, 0:P], ps[0:NS, 6, P:2 * P]
                c_ = lambda q: chain[0:NS, q, :]
                dve.tensor_copy(c_(0), ps[0:NS, 6, 2 * P:3 * P])
                then(dve.tensor_copy(c_(1), ps[0:NS, 6, 3 * P:4 * P]))
                then(TT(c_(2)[:, 1:], c_(1)[:, :-1], c_(0)[:, 1:], ALU.is_equal))
                then(TT(c_(3), c_(1), c_(0), ALU.is_equal))
                then(TT(c_(3), c_(3), c_(2), ALU.mult))
                then(TS(c_(5), c_(3), -LOW, LOW, ALU.mult, ALU.add))
                then(dve.tensor_tensor_scan(c_(6), c_(5), e_m, LOW, ALU.add, ALU.max))
                TT(c_(5), e_m, c_(6), ALU.subtract)
                then(TT(c_(4)[:, 1:], c_(6)[:, :-1], c_(6)[:, 1:], ALU.subtract))
                then(dve.memset(c_(4)[:, 0:1], 0.0))
                TS(c_(4), c_(4), 0.0, None, ALU.min).then_inc(S("chain_shift"), 1)
                acted(GROUPS + 1)
                TT(c_(4), c_(4), c_(3), ALU.mult)
                then(TT(c_(5), c_(5), e_s, ALU.mult))
                then(dve.tensor_tensor_scan(c_(7), c_(4), c_(5), 0.0, ALU.mult, ALU.add))
                then(TS(c_(3), c_(2), -LOW, LOW, ALU.mult, ALU.add))
                dve.memset(c_(1)[:, 0:1], 0.0)
                dve.memset(c_(0)[:, 0:1], LOW)
                TT(c_(1)[:, 1:], c_(7)[:, :-1], c_(2)[:, 1:], ALU.mult)
                then(TT(c_(0)[:, 1:], c_(6)[:, :-1], c_(2)[:, 1:], ALU.mult))
                TT(c_(0)[:, 1:], c_(0)[:, 1:], c_(3)[:, 1:], ALU.add).then_inc(S("chain_ready"), 1)
                then(TS(pen[:], dst_f[:], dst_f[:, 0:1], 1.0, ALU.is_equal, ALU.subtract))
                then(TS(pen[:], pen[:], -LOW, None, ALU.mult))
                dve.wait_ge(S("carry_out"), every(i, 1, 1))
                dve.tensor_copy(carry[:, 0, :], ps[:, 7, 0:NS])
                then(dve.tensor_copy(carry[:, 1, :], ps[:, 7, P:P + NS]))
                then(TT(e_ad, pen[:].unsqueeze(1).to_broadcast([P, HEADS, SW]), tall(five(carry[:, 0, :])[:, :, 0], SW), ALU.add))
                then(TT(e_new, e_ad, m_run, ALU.max))
                TT(e_w, e_ad, e_new, ALU.subtract)
                TT(e_a, m_run, e_new, ALU.subtract).then_inc(S("carry_shift"), 1)
                acted(GROUPS + 2)
                dve.tensor_copy(m_run, e_new)
                s_run = seg[:, :, HEADS:SROW].rearrange("p f (h c) -> p f h c", h=HEADS)
                TT(s_run, s_run, tall(e_a.rearrange("p h f -> p f h"), 5), ALU.mult)
                t4 = tmp_s.rearrange("p f (h c) -> p f h c", h=HEADS)
                then(TT(t4, tall(flat_w, 5), five(carry[:, 1, :]).unsqueeze(1).to_broadcast([P, SW, HEADS, 5]), ALU.mult))
                TT(s_run, s_run, t4, ALU.add).then_inc(S("seg_ready"), 1)

                dve.wait_ge(S("pulled_in"), every(i, 16 * NT, 16 * NT))
                masked(nonempty[:])
                merge("act_scan", every(i, ACT_TURN, GROUPS + 3))
                dve.memset(c_(2)[:, 0:1], 0.0).then_inc(S("turn_done"), 1)
                dve.wait_ge(S("turn_done"), every(i, 1, 1))
                assert own.n == VEC_TURN, own.n

            own = Own(dve, S("vec_between"))
            then(dve.memset(clamped64[:], 0.0))
            window(0, False, clamped_part)
            further(dve, 2, lambda i: window(i, True))

            own = Own(dve, S("vec_end"))
            heads4 = lambda v: v.rearrange("p t (h c) -> p t h c", h=HEADS)
            then(TS(new_m[:], acc_s[:, :, :, 0], 1e-16, None, ALU.add))
            then(dve.reciprocal(new_m[:], new_m[:]))
            then(TT(heads4(agg), acc_s[:, :, :, 1:], tall(new_m[:], NE_EXP), ALU.mult))
            then(TT(agg, agg, across(B_GAT, 16, NT), ALU.add))
            then(dve.tensor_reduce(gate[:, 0, :], agg, X, ALU.add))
            then(TS(gate[:, 0, :], gate[:, 0, :], -1.0 / 16, None, ALU.mult))
            then(TT(agg2, agg, tall(gate[:, 0, :], 16), ALU.add))
            then(TT(agg, agg2, agg2, ALU.mult))
            then(dve.tensor_reduce(gate[:, 0, :], agg, X, ALU.add))
            TS(gate[:, 1, :], gate[:, 0, :], 1.0 / 16, LN_EPS, ALU.mult, ALU.add).then_inc(S("var_ready"), 1)
            dve.wait_ge(S("rstd_ready"), N_VAR)
            then(TT(agg, agg2, tall(gate[:, 2, :], 16), ALU.mult))
            then(TT(agg, agg, across(B_LG, 16, NT), ALU.mult))
            then(TT(agg, agg, across(B_LB, 16, NT), ALU.add))
            score = gate[:, 4:8, :]
            then(dve.tensor_reduce(score.rearrange("p e t -> p t e"), agg.rearrange("p t (h e) -> p t e h", h=HEADS), X, ALU.add))
            then(TS(score, score, 1.0 / HEADS, None, ALU.mult))
            rank = gate[:, 12:16, :]
            for x in range(NE_EXP):
                then(dve.memset(rank[:, x, :], float(x)))
            for a in range(NE_EXP):
                for b in range(a + 1, NE_EXP):
                    then(TT(gate[:, 0, :], score[:, b, :], score[:, a, :], ALU.is_gt))
                    then(TT(rank[:, a, :], rank[:, a, :], gate[:, 0, :], ALU.add))
                    then(TT(rank[:, b, :], rank[:, b, :], gate[:, 0, :], ALU.subtract))
            then(TS(rank, rank, 2.0, None, ALU.is_lt))
            then(dve.tensor_reduce(gate[:, 1, :], score.rearrange("p e t -> p t e"), X, ALU.max))
            soft = gate[:, 8:12, :]
            TT(soft, score, gate[:, 1, :].unsqueeze(1).to_broadcast([P, NE_EXP, NT]), ALU.subtract).then_inc(S("soft_shift"), 1)
            dve.wait_ge(S("soft_exp"), 1)
            then(TT(soft, soft, rank, ALU.mult))
            then(dve.tensor_reduce(gate[:, 1, :], soft.rearrange("p e t -> p t e"), X, ALU.add))
            then(dve.reciprocal(gate[:, 1, :], gate[:, 1, :]))
            then(TT(soft, soft, gate[:, 1, :].unsqueeze(1).to_broadcast([P, NE_EXP, NT]), ALU.mult))
            y4 = y_exp[:].rearrange("p t (e d) -> p t e d", e=NE_EXP)
            then(TT(y4, y4, tall(soft.rearrange("p e t -> p t e"), D), ALU.mult))
            for x in range(NE_EXP):
                ins = TT(h2[:], h2[:], y4[:, :, x, :], ALU.add)
                if x < NE_EXP - 1:
                    then(ins)
            ins.then_inc(S("result"), 1)


def kernel(**inputs):
    import numpy as np
    import concourse.bacc as bacc
    from concourse.bass_utils import run_bass_kernel_spmd as run

    v = {k: np.asarray(a) for k, a in inputs.items()}
    p = np.arange(P)
    const = np.zeros((P, C_WIDTH), np.float32)
    const[:, C_ID:C_ID + P] = np.eye(P)
    const[:, C_TRI:C_TRI + P] = p[:, None] <= p[None, :]
    const[:, C_ONE:C_ONE + P] = 1
    const[0:OH, C_ID1:C_ID1 + P] = const[OH:, C_ID:C_ID + P]
    const[0:OH, C_TRI1:C_TRI1 + P] = const[OH:, C_TRI:C_TRI + P]
    sgn = {k: 1 - 2 * ((p >> (k - CHUNK_BITS)) & 1) for k in range(CHUNK_BITS + 1, ALL_BITS + 1)}
    const[:, C_SIGN] = sgn[9] * (p % 2 == 0)
    const[:, C_SIGN + 1] = sgn[9] * (p % 2 == 1)
    for k in range(CHUNK_BITS + 1, ALL_BITS):
        const[:, C_SIGN + k - CHUNK_BITS + 1] = sgn[k] * sgn[k + 1]
    ffn = lambda n: v["L0_ffn_" + n]
    tok = lambda n: v["L0_tok_" + n]
    attn = lambda n: v["L0_attn_" + n]
    par = np.concatenate([a.ravel() for a in (
        tok("ln_g"), tok("ln_b"), ffn("att_src"), ffn("att_dst"), ffn("b_gat"), ffn("ln_gamma"), ffn("ln_beta"),
        ffn("b2"), tok("W_o"), tok("W_dt"))])[None, :]
    columns = lambda w: w.transpose(1, 0, 2).reshape(D, -1)
    arrays = {
        "idx": v["x"].T,
        "src": v["L0_ffn_edge_index"][0].reshape(P, EC),
        "dst": v["L0_ffn_edge_index"][1].reshape(P, EC),
        "const": const,
        "par": par,
        "outcomes": v["fside_BS_outcomes"],
        "times": v["fside_BS_timestamps"],
        "h_q": tok("h_q"),
        "w_tok": np.concatenate([tok("W_proj_w").T, tok("W_proj_b")[None, :]]),
        "w_kq": np.concatenate([columns(attn("Wks")), columns(attn("Wqs"))], axis=1),
        "w_vt": attn("Wvs").transpose(2, 0, 1).reshape(D, -1),
        "w_o": columns(attn("Wo")),
        "w_hid": np.concatenate([columns(ffn("W1")), ffn("b1").reshape(1, -1)]),
        "w_outp": ffn("W2").transpose(1, 0, 2).reshape(HID, -1),
        "w_gat": ffn("W_gat"),
        "zeros": np.zeros((1, SW * HEADS), np.float32),
        "no_keys": np.full((1, PITCH - P * CW), CL_BASE, np.float32),
    }
    arrays = {k: np.ascontiguousarray(a) for k, a in arrays.items()}
    nc = bacc.Bacc("TRN2", target_bir_lowering=False, num_devices=1)
    A = {k: nc.dram_tensor("in_" + k, a.shape, mybir.dt.from_np(a.dtype), kind="ExternalInput").ap()
         for k, a in arrays.items()}
    out = nc.dram_tensor("out", (NT, P, D), F32, kind="ExternalOutput").ap()
    build(nc, A, out)
    r = run(nc, [{"in_" + k: a for k, a in arrays.items()}], core_ids=[0])
    return r.results[0]["out"]
```

```python
from contextlib import ExitStack

import concourse.bass as bass
from concourse import mybir

P = 128
N_TOK, D, N_Q = 4096, 64, 25000
NT = N_TOK // P
TG = 4
NG = NT // TG
GW = TG * P
H, K = 8, 32
FEATS = D + 3
NE_EXP, HEADS, HID = 4, 4, 128
N_EDGES = 262144
EC = N_EDGES // P
CW = 256
SW = 132
PITCH = 2 * P * SW
GROUPS = 4
GC = SW // GROUPS
OH = 64
N_CHUNK = EC // CW
LOCAL_BITS = 11
BLOCK_BITS = 7
KEPT = EC // 2
CHUNK_BITS = 8
ALL_BITS = CHUNK_BITS + 7
CL_BASE = float(1 << 24)
BAD = float(1 << 25)
LAST = float(N_TOK - 1)
ROW = HEADS + HEADS * NE_EXP
NS = HEADS * (1 + NE_EXP)
SROW = HEADS + NS
LOW = -1e30
LN_EPS = 1e-5
ATT_EPS = 1e-9
OOB = 1e6
N_VAR = 3 * NG + 1
ACT_TURN = GROUPS + 3
EXPERTS_FIRST, EXPERTS_COUNTING, EXPERTS_SCANNING = 6, 5, 3
HIST_TURNS = 3
FIRST_PULLED = 24
TURNS = 2 * (ALL_BITS - CHUNK_BITS)
TURN_AT = {23: (1,), 24: (3,), 25: (4,), 26: (5,), 27: (6,), 28: (8,), 29: (9,), 30: (10,), 31: (11, 12, 13)}
TURN_AT_GROUP = {6: 2, 7: 7}
COUNTS_GROUP = 5
RESULT_VEC, RESULT_POOL = ((0, 14), (14, 23)), (23, 32)
SORTED_BATCH = 21
CHUNK_AT = {21: (0,), 22: (1,), 24: (4,), 25: (5,), 26: (6,), 28: (9,), 29: (10, 11), 30: (12,)}
CHUNK_AT_GROUP = {6: (2,), 7: (7, 8)}
FIRST_FILLS, FILLS = (1, 2), (1, 2, 2, 2, 4, 4, 0, 0)
VEC_HIST = 5
VEC_SORT = 92
VEC_TURN = 70

F32 = mybir.dt.float32
BF16 = mybir.dt.bfloat16
I32 = mybir.dt.int32
ALU = mybir.AluOpType
ACT = mybir.ActivationFunctionType
X = mybir.AxisListType.X

C_ID, C_TRI, C_ONE, C_ID1, C_TRI1, C_SIGN = (P * n for n in range(6))
C_WIDTH = 5 * P + 8
B_G, B_B, B_SRC, B_DST, B_GAT, B_LG, B_LB, B_B2 = 0, 64, 128, 144, 160, 176, 192, 208
B_WO, B_WDT = 464, 465
B_WIDTH = 466


class Own:

    def __init__(self, eng, sem, before=0, turn=None, per_turn=0):
        self.eng, self.sem, self.n, self.before, self.turn, self.per_turn = eng, sem, 0, before, turn, per_turn

    def did(self, ins):
        ins.then_inc(self.sem, 1)
        self.n += 1

    def settle(self):
        at = self.before + self.n
        self.eng.wait_ge(self.sem, at if self.turn is None else self.turn * self.per_turn + at)


def every(turn, per_turn, n):
    return turn * per_turn + n


def build(nc, A, out):
    with ExitStack() as ctx:
        def sb(name, shape, dt=F32):
            return ctx.enter_context(nc.sbuf_tensor(name, shape, dt))

        def sem(name):
            return ctx.enter_context(nc.semaphore(name))

        const = sb("const", [P, C_WIDTH])
        par = sb("par", [P, B_WIDTH])
        ident, tri, ones, ident1, tri1 = (const[:, c:c + P] for c in (C_ID, C_TRI, C_ONE, C_ID1, C_TRI1))
        key_a = sb("key_a", [P, EC])
        key_b = sb("key_b", [P, EC])
        h2 = sb("h2", [P, NT, D])
        tab = sb("tab", [P, NT, ROW])
        a_dst = sb("a_dst", [P, NT, HEADS])
        y_exp = sb("y_exp", [P, NT, NE_EXP * D])
        counts = sb("counts", [P, 4])
        counts_row = sb("counts_row", [1, 3 * P])
        n_turns = sb("n_turns", [1, 4], I32)
        n_clamped = sb("n_clamped", [P, NT])
        acc_m = sb("acc_m", [P, NT, HEADS])
        acc_s = sb("acc_s", [P, NT, HEADS, 1 + NE_EXP])
        last_row = sb("last_row", [P, ROW])
        w_hid = sb("w_hid", [D + 1, NE_EXP * HID])
        w_outp = sb("w_outp", [HID, NE_EXP * D])
        w_gat = sb("w_gat", [D, HEADS * NE_EXP])

        arena = sb("arena", [P, 28 * 1024])
        used = [0]

        def cut(shape, dt=F32, rows=P):
            n = 1
            for s in shape:
                n *= s
            words = n if dt != BF16 else n // 2
            v = arena[0:rows, used[0]:used[0] + words]
            used[0] += words
            assert used[0] <= 28 * 1024, used[0]
            if dt != F32:
                v = v.bitcast(dt)
            if len(shape) > 1:
                names = "abcd"[:len(shape)]
                v = v.rearrange(f"p ({' '.join(names)}) -> p {' '.join(names)}", **dict(zip(names, shape)))
            return v

        emb = cut([NT, D])
        cat_t = cut([N_TOK], rows=FEATS)
        h1 = cut([NT, D])
        exp_kq, relu_kq = cut([4, GW]), cut([4, GW])
        kq = cut([4, GW])
        vals = cut([2, H, D + 1])
        att = cut([2, 4, 2, P])
        w_tok = cut([D], rows=FEATS)
        w_kq = cut([4 * P], rows=D)
        w_vt, w_o, w_vo = (cut([H * D], rows=D) for _ in range(3))
        x_t = cut([GW], rows=D)
        ffn_at = used[0]
        src_i, dst_i, t_a, t_b = cut([EC], I32), cut([EC], I32), cut([EC]), cut([EC])
        used[0] = ffn_at
        x2_t = cut([N_TOK], rows=D + 1)
        hid = cut([NE_EXP, GW])
        pulled = cut([NT, SROW])
        gate = cut([16, NT])
        agg, agg2 = (cut([NT, HEADS * NE_EXP]) for _ in range(2))
        used[0] = 0
        oh_lo, oh_hi = cut([OH, CW], BF16), cut([OH, CW], BF16)
        after_hot = used[0]
        used[0] = 0
        seg = cut([SW, SROW])
        e_ad_at = used[0]
        e_ad, e_val, e_new, e_w, e_a = (cut([HEADS, SW]) for _ in range(5))
        ad_at = cut([SW, HEADS])
        assert used[0] <= after_hot
        used[0] = after_hot
        rows = cut([SW, ROW])
        assert used[0] <= ffn_at
        assert NT * SROW <= 2 * HEADS * SW
        carried = arena[:, e_ad_at:e_ad_at + NT * SROW].rearrange("p (t s) -> p t s", t=NT)
        clamped = rows.rearrange("p f r -> p (f r)")[:, 0:NT * SROW].rearrange("p (t s) -> p t s", t=NT)

        cen = sb("cen", [P, TG, D])
        sq = sb("sq", [P, TG, D])
        x2 = sb("x2", [P, TG, D])
        stat = sb("stat", [P, 4, TG])
        half = sb("half", [P, NT])
        feats = sb("feats", [NT, 2, P])
        q_idx = sb("q_idx", [P, NT], I32)
        q_f = sb("q_f", [P, NT])
        nv = sb("nv", [P, 2, 4, D])
        att_den = sb("att_den", [P, 2, H])
        prod = sb("prod", [P, TG, HEADS * NE_EXP])

        ck = [sb("ck0", [P, CW]), sb("ck1", [P, CW])]
        wk = sb("wk", [P, SW])
        ki = sb("ki", [P, CW], I32)
        ti = sb("ti", [P, CW], I32)
        si = sb("si", [P, CW], I32)
        tb, lb = sb("tb", [P, CW], BF16), sb("lb", [P, CW], BF16)
        dst_f = sb("dst_f", [P, SW])
        same = sb("same", [P, SW])
        mirror = sb("mirror", [P, CW])
        pen = sb("pen", [P, SW])
        hist = sb("hist", [P, NT])
        hist64 = sb("hist64", [OH, OH])
        clamped64 = sb("clamped64", [OH, OH])
        pos = sb("pos", [P, 4, NT])
        i_start, i_end = sb("i_start", [P, NT], I32), sb("i_end", [P, NT], I32)
        nonempty = sb("nonempty", [P, NT])
        i_first = sb("i_first", [P, 1], I32)
        ad_first = sb("ad_first", [P, HEADS])
        ends = sb("ends", [P, 4, NS])
        chain = sb("chain", [P, 9, P])
        carry = sb("carry", [P, SROW])
        i_carry = sb("i_carry", [P, 1], I32)
        new_m = sb("new_m", [P, NT, HEADS])
        fade = sb("fade", [P, 2, NT, HEADS])

        ps = ctx.enter_context(nc.psum_tensor("ps", [P, 8, 512], F32))

        d_tab = nc.dram_tensor("d_tab", [N_TOK, ROW], F32).ap()
        d_blocks = nc.dram_tensor("d_blocks", [P, EC], F32).ap()
        d_keys = nc.dram_tensor("d_keys", [N_CHUNK * PITCH], F32).ap()
        d_ad = nc.dram_tensor("d_ad", [P * SW, HEADS], F32).ap()
        d_adrow = nc.dram_tensor("d_adrow", [N_TOK, HEADS], F32).ap()
        d_carry = nc.dram_tensor("d_carry", [N_TOK, SROW], F32).ap()
        d_seg = nc.dram_tensor("d_seg", [P * SW, SROW], F32).ap()

        made = {}

        def S(name):
            if name not in made:
                made[name] = sem(name)
            return made[name]

        block = ctx.enter_context(nc.Block())
        tall = lambda ap, n: ap.unsqueeze(len(ap.shape)).to_broadcast(list(ap.shape) + [n])

        def sign(k):
            return const[:, C_SIGN + k - CHUNK_BITS + 1:C_SIGN + k - CHUNK_BITS + 2]

        def number(eng, which):
            eng.wait_ge(S("n_turns_set"), 4)
            return eng.value_load(n_turns[0:1, which:which + 1], min_val=1,
                                  max_val=(N_CHUNK, N_CHUNK, 2 * N_CHUNK, 2)[which])

        def further(eng, which, body, first=1):
            turns = number(eng, which)
            with eng.If(turns > first):
                with eng.Fori(first, turns) as i:
                    body(i)

        order = ["vo", ("turn", 0), ("token", 0)]
        for g in range(NG):
            order += [("x_t", g)] + [("kq", g, m) for m in range(4)]
            if g == COUNTS_GROUP:
                order += ["counts"]
            if g in TURN_AT_GROUP:
                order += [("chunk", TURN_AT_GROUP[g])]
            if g < NG - 1:
                order += [("turn", g + 1), ("token", g + 1)]
            for b in range(TG * g, TG * g + 2):
                order += [("values", b)] + [("chunk", m) for m in TURN_AT.get(b, ())]
            if g:
                order += [("x2_t", g - 1), ("nodes", g - 1)]
            for b in range(TG * g + 2, TG * g + TG):
                order += [("values", b)] + [("chunk", m) for m in TURN_AT.get(b, ())]
        order += [("x2_t", NG - 1), ("nodes", NG - 1)]
        order += [("chunk", 14)]
        order += [("hidden", g, x) for g in range(NG) for x in range(NE_EXP)]
        nth = {item: n + 1 for n, item in enumerate(order)}

        def gated(TT, tiles, own):
            t = slice(*tiles)
            y4 = y_exp[:, t].rearrange("p t (e d) -> p t e d", e=NE_EXP)
            own.did(TT(y4, y4, tall(gate[:, 8:12, t].rearrange("p e t -> p t e"), D), ALU.mult))
            for x in range(NE_EXP):
                own.settle()
                ins = TT(h2[:, t], h2[:, t], y4[:, :, x, :], ALU.add)
                if x < NE_EXP - 1:
                    own.did(ins)
            return ins

        @block.sync
        def _(sp):
            sp.dma_start(q_idx[:], A["idx"]).then_inc(S("idx_in"), 16)
            sp.dma_start(feats[:, 0, :], A["outcomes"]).then_inc(S("feats_in"), 16)
            sp.dma_start(feats[:, 1, :], A["times"]).then_inc(S("feats_in"), 16)
            sp.dma_start(const[:], A["const"]).then_inc(S("const_in"), 16)
            sp.dma_start(par[:], A["par"].to_broadcast([P, B_WIDTH])).then_inc(S("par_in"), 16)
            for dst, name in ((w_tok, "w_tok"), (w_kq, "w_kq"), (w_vt, "w_vt"), (w_o, "w_o"),
                              (w_hid[:], "w_hid"), (w_outp[:], "w_outp"), (w_gat[:], "w_gat")):
                sp.dma_start(dst, A[name]).then_inc(S("weights_in"), 16)
            sp.dma_start(src_i, A["src"]).then_inc(S("src_in"), 16)
            sp.dma_start(dst_i, A["dst"]).then_inc(S("dst_in"), 16)
            sp.dma_start(d_ad.rearrange("(p f) h -> p (f h)", p=P), A["zeros"].to_broadcast([P, SW * HEADS]))\
              .then_inc(S("zero_written"), 16)
            sp.dma_start(d_keys.rearrange("(c n) -> c n", c=N_CHUNK)[:, P * CW:PITCH],
                         A["no_keys"].to_broadcast([N_CHUNK, PITCH - P * CW])).then_inc(S("no_keys_written"), 16)
            sp.wait_ge(S("feats_done"), 2)
            for r in range(2):
                sp.dma_start(cat_t[D + r:D + r + 1, :], feats[:, r, :]).then_inc(S("cat_rows"), 16)
            sp.wait_ge(S("blocks_sorted"), 1)
            sp.dma_start(d_blocks, key_a[:]).then_inc(S("blocks_saved"), 16)
            again = number(sp, 3)
            with sp.If(again > 1):
                sp.wait_ge(S("blocks_saved"), 16)
                sp.dma_start(key_a[:], d_blocks).then_inc(S("blocks_back"), 16)
            sp.wait_ge(S("tab_ready"), NG)
            sp.dma_start(d_tab.rearrange("(t p) r -> p t r", p=P), tab[:]).then_inc(S("tab_written"), 16)
            sp.dma_start(d_adrow.rearrange("(t p) r -> p t r", p=P), a_dst[:]).then_inc(S("adrow_written"), 16)

            def wait(name, value):
                sp.wait_ge(S(name), value)
                sp.sem_inc(S("sync_passed"), 1)

            def store_chunk(i):
                wait("chunk_sorted", every(i, 1, 1))
                sp.dma_start(d_keys[bass.ds(i * PITCH, P * CW)].rearrange("(p f) -> p f", p=P), ck[1][:])\
                  .then_inc(S("keys_stored"), 16)

            def window(i, later):
                if later:
                    wait("window_read", every(i, 1, 0))
                sp.dma_start(wk[:], d_keys[bass.ds(i * (P * SW), P * SW)].rearrange("(p f) -> p f", p=P))\
                  .then_inc(S("window_in"), 16)
                if not later:
                    sp.wait_ge(S("tab_written"), 16)
                    sp.dma_start(last_row[:], d_tab[N_TOK - 1:N_TOK, :].to_broadcast([P, ROW])).then_inc(S("last_row_in"), 16)
                if later:
                    wait("carry_in", every(i, 16, 0))
                sp.dma_start(d_carry.rearrange("(p f) s -> p (f s)", p=P), A["no_carry"].to_broadcast([P, NT * SROW]))\
                  .then_inc(S("carry_reset"), 16)
                wait("hot_free", every(i, 1, 1))
                wait("ad_scattered", every(i, 16 * NT, 16 * NT))
                sp.dma_start(ad_at.rearrange("p f h -> p (f h)"), d_ad.rearrange("(p f) h -> p (f h)", p=P))\
                  .then_inc(S("ad_in"), 16)
                for q in range(GROUPS):
                    c = slice(q * GC, (q + 1) * GC)
                    wait("seg_ready", every(i, GROUPS, q + 1))
                    sp.dma_start(d_seg.rearrange("(p f) s -> p f s", p=P)[:, c], seg[:, c]).then_inc(S("seg_written"), 16)
                wait("carry_scattered", every(i, 16, 16))
                sp.dma_start(carried, d_carry.rearrange("(t p) s -> p t s", p=P)).then_inc(S("carry_in"), 16)

            store_chunk(0)
            further(sp, 1, store_chunk)
            sp.wait_ge(S("no_keys_written"), 16)
            sp.wait_ge(S("keys_stored"), 16)
            further(sp, 1, lambda i: wait("keys_stored", every(i, 16, 16)))
            window(0, False)
            further(sp, 2, lambda i: window(i, True))
            view = out.rearrange("b s d -> s b d")
            for n, (a, b) in enumerate(RESULT_VEC):
                sp.wait_ge(S("result"), n + 1)
                sp.dma_start(view[:, a:b], h2[:, a:b, :]).then_inc(S("stored"), 16)
            a, b = RESULT_POOL
            sp.wait_ge(S("result_pool"), 1)
            sp.dma_start(view[:, a:b], h2[:, a:b, :]).then_inc(S("stored"), 16)
            sp.wait_ge(S("stored"), 16 * (len(RESULT_VEC) + 1))

        @block.gpsimd
        def _(pool):
            pool.memset(half[:], -0.5).then_inc(S("half_set"), 1)
            pool.wait_ge(S("idx_ready"), 1)

            def embeddings(g):
                for t in range(TG * g, TG * g + TG):
                    pool.indirect_dma_start(out=emb[:, t, :], out_offset=None, in_=A["h_q"],
                                            in_offset=bass.IndirectOffsetOnAxis(q_idx[:, t:t + 1], 0))\
                        .then_inc(S(f"emb_in{g}"), 16)

            n_pow = 0

            def rsqrt():
                nonlocal n_pow
                n_pow += 1
                pool.wait_ge(S("var_ready"), n_pow)
                pool.tensor_tensor(stat[:, 2, :], stat[:, 1, :], half[:, 0:TG], ALU.pow).then_inc(S("rstd_ready"), 1)

            def mask(b):
                pool.wait_ge(S("att_ready"), b + 1)
                v = att[:, b % 2].rearrange("p j m s -> p (j m) s")
                pool.affine_select(out=v, in_=v, compare_op=ALU.is_ge, fill=0.0, base=0,
                                   pattern=[[0, H], [1, P]], channel_multiplier=-1).then_inc(S("masked"), 1)

            embeddings(0)
            embeddings(1)
            pool.wait_ge(S("half_set"), 1)
            rsqrt()
            rsqrt()
            embeddings(2)
            for g in range(NG):
                for _ in range((g > 0) + (g < NG - 1)):
                    rsqrt()
                mask(TG * g)
                if g < NG - 1:
                    rsqrt()
                for b in range(1, TG):
                    mask(TG * g + b)
                if g + 3 < NG:
                    embeddings(g + 3)
            rsqrt()

            pool.wait_ge(S("tab_written"), 16)
            pool.wait_ge(S("adrow_written"), 16)
            pool.wait_ge(S("zero_written"), 16)

            def window(i):
                def wait(name, value):
                    pool.wait_ge(S(name), value)
                    pool.sem_inc(S("pool_passed"), 1)

                wait("src_ready", every(i, 1, 1))
                pool.indirect_dma_start(out=ad_first[:], out_offset=None, in_=d_adrow,
                                        in_offset=bass.IndirectOffsetOnAxis(i_first[:, 0:1], 0))\
                    .then_inc(S("ad_first_in"), 16)
                for f in range(SW):
                    if f == 2 * GC:
                        wait("pos_ready", every(i, 1, 1))
                        for t in range(NT):
                            pool.indirect_dma_start(out=d_ad, in_=a_dst[:, t, :], in_offset=None,
                                                    out_offset=bass.IndirectOffsetOnAxis(i_start[:, t:t + 1], 0),
                                                    bounds_check=P * SW - 1, oob_is_err=False)\
                                .then_inc(S("ad_scattered"), 16)
                    pool.indirect_dma_start(out=rows[:, f, :], out_offset=None, in_=d_tab,
                                            in_offset=bass.IndirectOffsetOnAxis(si[:, f:f + 1], 0))\
                        .then_inc(S(f"rows_in{f // GC}"), 16)
                wait("seg_written", every(i, 16 * GROUPS, 16 * GROUPS))
                wait("carry_reset", every(i, 16, 16))
                for t in range(NT):
                    if t == NT // 4:
                        wait("carry_ready", every(i, 1, 1))
                        pool.indirect_dma_start(out=d_carry, in_=carry[:], in_offset=None,
                                                out_offset=bass.IndirectOffsetOnAxis(i_carry[:, 0:1], 0),
                                                bounds_check=N_TOK - 1, oob_is_err=False)\
                            .then_inc(S("carry_scattered"), 16)
                    pool.indirect_dma_start(out=pulled[:, t, :], out_offset=None, in_=d_seg,
                                            in_offset=bass.IndirectOffsetOnAxis(i_end[:, t:t + 1], 0))\
                        .then_inc(S(f"pulled_in{t // FIRST_PULLED}"), 16)
                wait("turn_done", every(i, 1, 1))

            window(0)
            further(pool, 2, window)
            pool.wait_ge(S("gates_ready"), 1)
            gated(pool.tensor_tensor, RESULT_POOL, Own(pool, S("pool_end"))).then_inc(S("result_pool"), 1)

        @block.scalar
        def _(act):
            act.wait_ge(S("abs_ready"), 1)
            act.activation(feats[:, 1, :], feats[:, 1, :], ACT.Ln, bias=1.0).then_inc(S("logged"), 1)
            done = 0

            def evacuate(item, *jobs):
                nonlocal done
                done += 1
                assert nth[item] == done, item
                act.wait_ge(S("bank_filled"), done)
                for out_, func, view in jobs:
                    last = act.activation(out_, view(ps[:, (done - 1) % 2, :]), func)
                last.then_inc(S("bank_read"), 1)

            whole = lambda v: v
            lower = lambda v: v[0:D, :]

            def token_part(g):
                evacuate(("turn", g), (cat_t[0:D, g * GW:(g + 1) * GW], ACT.Copy, lower))
                evacuate(("token", g), (h1[:, TG * g:TG * g + TG, :], ACT.Copy,
                                        lambda v: v[:, 0:TG * D].rearrange("p (t d) -> p t d", t=TG)))

            def node_part(g):
                evacuate(("x2_t", g), (x2_t[0:D, g * GW:(g + 1) * GW], ACT.Copy, lower))
                evacuate(("nodes", g), (tab[:, TG * g:TG * g + TG, HEADS:ROW], ACT.Copy,
                                        lambda v: v[:, 0:64].rearrange("p (t c) -> p t c", t=TG)))

            def turned(m):
                evacuate(("chunk", m), (mirror[:], ACT.Copy, lambda v: v[:, 0:CW]))

            evacuate("vo", (w_vo, ACT.Copy, lower))
            token_part(0)
            for g in range(NG):
                evacuate(("x_t", g), (x_t, ACT.Copy, lower))
                for m in range(4):
                    if g and m == 0:
                        act.wait_ge(S("kq_ready"), 4 * g)
                    evacuate(("kq", g, m), (relu_kq[:, m, :], ACT.Relu, whole), (exp_kq[:, m, :], ACT.Exp, whole))
                if g == COUNTS_GROUP:
                    evacuate("counts", (counts_row[:], ACT.Copy, lambda v: v[0:1, 0:3 * P]))
                if g in TURN_AT_GROUP:
                    turned(TURN_AT_GROUP[g])
                if g < NG - 1:
                    token_part(g + 1)
                for b in range(TG * g, TG * g + TG):
                    act.wait_ge(S("att_out"), b + 1)
                    if b >= 2:
                        act.wait_ge(S("av_out"), b - 1)
                    act.activation(att[:, b % 2], ps[:, 4:8, 0:2 * P].rearrange("p j (m s) -> p j m s", m=2),
                                   ACT.Copy).then_inc(S("att_ready"), 1)
                    if b == 0:
                        act.wait_ge(S("ones_set"), 1)
                    evacuate(("values", b), (vals[:, b % 2, :, 0:D], ACT.Copy, lambda v: v.rearrange("p (h e) -> p h e", h=H)))
                    for m in TURN_AT.get(b, ()):
                        turned(m)
                    if g and b == TG * g + 1:
                        node_part(g - 1)
            node_part(NG - 1)
            turned(14)

            def experts():
                for g in range(NG):
                    for x in range(NE_EXP):
                        if g and x == 0:
                            act.wait_ge(S("y_out"), 2 * g)
                        evacuate(("hidden", g, x), (hid[:, x, :], ACT.Gelu, whole))
                        if x % 2:
                            yield
                    for n in range(2 * g, 2 * g + 2):
                        act.wait_ge(S("y_out"), n + 1)
                        act.activation(y_exp[:, 2 * n:2 * n + 2, :], ps[:, 4 + n % 2, :].rearrange("p (t c) -> p t c", t=2),
                                       ACT.Copy).then_inc(S("y_read"), 1)
                        yield

            expert_work = experts()

            def window(i, first=False):
                for q in range(GROUPS):
                    if first and q:
                        for _ in range(EXPERTS_SCANNING if q < GROUPS - 1 else 4 * NG):
                            next(expert_work, None)
                    act.wait_ge(S("shift_ready"), every(i, GROUPS, q + 1))
                    c = slice(q * GC, (q + 1) * GC)
                    act.activation(e_a[:, :, c], e_a[:, :, c], ACT.Exp)
                    act.activation(e_w[:, :, c], e_w[:, :, c], ACT.Exp).then_inc(S("act_scan"), 1)
                act.wait_ge(S("chain_shift"), every(i, 1, 1))
                act.activation(chain[0:NS, 4:6, :], chain[0:NS, 4:6, :], ACT.Exp).then_inc(S("act_scan"), 1)
                if first:
                    act.wait_ge(S("fade_shift"), 1)
                    act.activation(fade[:], fade[:], ACT.Exp).then_inc(S("faded"), 1)
                for n in range(2):
                    act.wait_ge(S("fade_shift"), every(i, 2, 2 + n))
                    act.activation(fade[:], fade[:], ACT.Exp).then_inc(S("act_scan"), 1)

            for _ in range(EXPERTS_FIRST + HIST_TURNS * EXPERTS_COUNTING):
                next(expert_work)
            window(0, True)
            further(act, 2, window)
            act.wait_ge(S("var_ready"), N_VAR)
            act.activation(gate[:, 2, :], gate[:, 1, :], ACT.Sqrt).then_inc(S("root_ready"), 1)
            act.wait_ge(S("soft_shift"), 1)
            act.activation(gate[:, 8:12, :], gate[:, 8:12, :], ACT.Exp).then_inc(S("soft_exp"), 1)

        @block.tensor
        def _(pe):
            pe.wait_ge(S("const_in"), 16)
            pe.wait_ge(S("weights_in"), 7 * 16)
            done = 0

            def bank(item):
                nonlocal done
                done += 1
                assert nth[item] == done, item
                if done > 2:
                    pe.wait_ge(S("bank_read"), done - 2)
                return ps[:, (done - 1) % 2, :]

            def copied(item):
                pe.wait_ge(S("bank_read"), nth[item])

            to = bank("vo")
            for h in range(H):
                last = pe.matmul(to[0:D, h * D:(h + 1) * D], w_vt[:, h * D:(h + 1) * D], w_o[:, h * D:(h + 1) * D],
                                 start=True, stop=True)
            last.then_inc(S("bank_filled"), 1)

            def turn(item, tile_of):
                to = bank(item)
                for k in range(TG):
                    last = pe.transpose(to[0:D, k * P:(k + 1) * P], tile_of(k), ident)
                last.then_inc(S("bank_filled"), 1)

            def token_part(g, between=None):
                pe.wait_ge(S(f"emb_in{g}"), 16 * TG)
                turn(("turn", g), lambda k: emb[:, TG * g + k, :])
                if between is not None:
                    weigh(between)
                if g == 0:
                    pe.wait_ge(S("cat_rows"), 32)
                copied(("turn", g))
                to = bank(("token", g))
                for k in range(TG):
                    t = TG * g + k
                    last = pe.matmul(to[:, k * D:(k + 1) * D], cat_t[:, t * P:(t + 1) * P], w_tok, start=True, stop=True)
                last.then_inc(S("bank_filled"), 1)

            def node_part(g, between=None):
                pe.wait_ge(S("x2_ready"), g + 1)
                turn(("x2_t", g), lambda k: x2[:, k, :])
                if between is not None:
                    weigh(between)
                copied(("x2_t", g))
                to = bank(("nodes", g))
                for k in range(TG):
                    t = TG * g + k
                    last = pe.matmul(to[:, 16 * k:16 * k + 16], x2_t[0:D, t * P:(t + 1) * P], w_gat[:], start=True, stop=True)
                last.then_inc(S("bank_filled"), 1)

            def weigh(b):
                pe.wait_ge(S("masked"), b + 1)
                copied(("values", b))
                if b:
                    pe.wait_ge(S("av_read"), b)
                for h in range(H):
                    j, m = h % 4, h // 4
                    last = pe.matmul(ps[:, 2 + m, j * (D + 1):(j + 1) * (D + 1)], att[:, b % 2, j, m, :],
                                     vals[:, b % 2, h, :], start=True, stop=True)
                last.then_inc(S("av_out"), 1)

            def chunk_turn(m):
                n = (m + 1) // 2
                pe.wait_ge(S("to_columns" if m % 2 else "to_rows"), n)
                to = bank(("chunk", m))
                source = 0 if m % 2 else n % 2
                for q in range(2):
                    last = pe.transpose(to[:, q * P:(q + 1) * P], ck[source][:, q * P:(q + 1) * P], ident)
                last.then_inc(S("bank_filled"), 1)

            def chunk_turns(i):
                for n in range(1, ALL_BITS - CHUNK_BITS + 1):
                    for ready, done_, bank_, source in (("to_columns", "in_columns", 6, 0), ("to_rows", "in_rows", 7, n % 2)):
                        pe.wait_ge(S(ready), every(i, 7, n))
                        for q in range(2):
                            last = pe.transpose(ps[:, bank_, q * P:(q + 1) * P], ck[source][:, q * P:(q + 1) * P], ident)
                        last.then_inc(S(done_), 1)

            def features_turn(g):
                pe.wait_ge(S("xa_ready"), g + 1)
                turn(("x_t", g), lambda k: h2[:, TG * g + k, :])

            token_part(0)
            features_turn(0)
            for g in range(NG):
                copied(("x_t", g))
                for m in range(4):
                    pe.matmul(bank(("kq", g, m)), w_kq[:, m * P:(m + 1) * P], x_t, start=True, stop=True)\
                      .then_inc(S("bank_filled"), 1)
                if g == COUNTS_GROUP:
                    pe.wait_ge(S("counts_ready"), 1)
                    pe.wait_ge(S("blocks_sorted"), 1)
                    to = bank("counts")
                    for q in range(3):
                        last = pe.transpose(to[0:1, q * P:(q + 1) * P], counts[:, q:q + 1], ident)
                    last.then_inc(S("bank_filled"), 1)
                if g in TURN_AT_GROUP:
                    chunk_turn(TURN_AT_GROUP[g])
                if g < NG - 1:
                    token_part(g + 1, TG * g - 1 if g else None)
                else:
                    weigh(TG * g - 1)
                pe.wait_ge(S("kq_ready"), 4 * (g + 1))
                for b in range(TG * g, TG * g + TG):
                    k = b - TG * g
                    if b:
                        pe.wait_ge(S("att_ready"), b)
                    for m in range(2):
                        for j in range(4):
                            last = pe.matmul(ps[:, 4 + j, m * P:(m + 1) * P], kq[32 * j:32 * j + 32, m, k * P:(k + 1) * P],
                                             kq[32 * j:32 * j + 32, 2 + m, k * P:(k + 1) * P], start=True, stop=True)
                    last.then_inc(S("att_out"), 1)
                    pe.matmul(bank(("values", b)), x_t[:, k * P:(k + 1) * P], w_vo, start=True, stop=True)\
                      .then_inc(S("bank_filled"), 1)
                    if b in TURN_AT:
                        chunk_turn(TURN_AT[b][0])
                    if g and k == 1:
                        node_part(g - 1, b - 1)
                        continue
                    if k == TG - 1 and g < NG - 1:
                        features_turn(g + 1)
                    if k:
                        weigh(b - 1)
            chunk_turn(12)
            weigh(NT - 1)
            chunk_turn(13)
            node_part(NG - 1)
            chunk_turn(14)
            def count(ready, columns, done_, value):
                pe.wait_ge(S(ready), value)
                for f in range(columns):
                    last = pe.matmul(ps[0:OH, 2, 0:OH], oh_lo[:, :, f], oh_hi[:, :, f], start=f == 0, stop=f == columns - 1)
                last.then_inc(S(done_), 1)

            def spread(source, c, low, high):
                v = source[:].rearrange("p (t b) -> p b t", b=2)
                pe.matmul(ps[:, 3, c:c + NT], low, v[:, 0, :], start=True, stop=False)
                return pe.matmul(ps[:, 3, c:c + NT], high, v[:, 1, :], start=False, stop=True)

            def experts():
                pe.wait_ge(S("x2_ones"), 1)
                for g in range(NG):
                    for x in range(NE_EXP):
                        pe.matmul(bank(("hidden", g, x)), w_hid[:, x * HID:(x + 1) * HID], x2_t[:, g * GW:(g + 1) * GW],
                                  start=True, stop=True).then_inc(S("bank_filled"), 1)
                        if x % 2:
                            yield
                    copied(("hidden", g, NE_EXP - 1))
                    for q in range(2):
                        n = 2 * g + q
                        if n >= 2:
                            pe.wait_ge(S("y_read"), n - 1)
                        for k in range(2):
                            for x in range(NE_EXP):
                                last = pe.matmul(ps[:, 4 + n % 2, k * 256 + x * D:k * 256 + (x + 1) * D],
                                                 hid[:, x, (2 * q + k) * P:(2 * q + k + 1) * P],
                                                 w_outp[:, x * D:(x + 1) * D], start=True, stop=True)
                        last.then_inc(S("y_out"), 1)
                        yield

            def window(i, between=None):
                count("onehots2", SW, "counted2", every(i, 1, 1))
                pe.wait_ge(S("hist_ready"), every(i, 1, 1))
                lows = slice(0, OH)
                spread(hist64, 0, ident[lows, :], ident1[lows, :])
                spread(hist64, 64, tri[lows, :], tri1[lows, :])
                spread(hist64, 96, ones[lows, :], ones[lows, :]).then_inc(S("cum_out"), 1)
                if between:
                    between()
                pe.wait_ge(S("ends_ready"), every(i, 1, 1))
                for q in range(4):
                    last = pe.transpose(ps[0:NS, 6, q * P:(q + 1) * P], ends[:, q, :], ident)
                last.then_inc(S("ends_turned"), 1)
                pe.wait_ge(S("chain_ready"), every(i, 1, 1))
                for q, row in enumerate((0, 1, 8)):
                    last = pe.transpose(ps[:, 7, q * P:(q + 1) * P], chain[:, row, :], ident)
                last.then_inc(S("carry_out"), 1)

            def between():
                for i in range(HIST_TURNS):
                    for _ in range(EXPERTS_COUNTING):
                        next(expert_work)
                    count("onehots", CW, "counted", i + 1)
                further(pe, 0, lambda i: count("onehots", CW, "counted", every(i, 1, 1)), HIST_TURNS)
                pe.wait_ge(S("clamped_ready"), 1)
                spread(clamped64, 128, ident[0:OH, :], ident1[0:OH, :]).then_inc(S("clamped_out"), 1)
                for _ in expert_work:
                    pass

            pe.wait_ge(S("att_ready"), NT)
            expert_work = experts()
            further(pe, 1, chunk_turns)

            for _ in range(EXPERTS_FIRST):
                next(expert_work)
            window(0, between)
            further(pe, 2, window)

        @block.vector
        def _(dve):
            own = Own(dve, S("vec_step"))

            def then(ins):
                own.did(ins)
                own.settle()

            TT, TS, STT = dve.tensor_tensor, dve.tensor_scalar, dve.scalar_tensor_tensor
            dve.wait_ge(S("idx_in"), 16)
            then(dve.tensor_copy(q_f[:], q_idx[:]))
            then(TS(q_f[:], q_f[:], 0.0, float(N_Q - 1), ALU.max, ALU.min))
            dve.tensor_copy(q_idx[:], q_f[:]).then_inc(S("idx_ready"), 1)
            then(dve.memset(cat_t[D:FEATS, :], 1.0))
            dve.memset(counts[:], 0.0)
            dve.wait_ge(S("feats_in"), 32)
            STT(feats[:, 1, :], feats[:, 1, :], -1.0, feats[:, 1, :], ALU.mult, ALU.max).then_inc(S("abs_ready"), 1)
            dve.wait_ge(S("par_in"), 16)
            then(TS(feats[:, 0, :], feats[:, 0, :], par[0:NT, B_WO:B_WO + 1], -5.0, ALU.mult, ALU.max))
            TS(feats[:, 0, :], feats[:, 0, :], 5.0, None, ALU.min).then_inc(S("feats_done"), 1)
            dve.wait_ge(S("logged"), 1)
            then(TS(feats[:, 1, :], feats[:, 1, :], par[0:NT, B_WDT:B_WDT + 1], -5.0, ALU.mult, ALU.max))
            TS(feats[:, 1, :], feats[:, 1, :], 5.0, None, ALU.min).then_inc(S("feats_done"), 1)
            dve.memset(vals[:, :, :, D:D + 1], 1.0).then_inc(S("ones_set"), 1)

            def edge_keys():
                own = Own(dve, S("key_step"))

                def then(ins):
                    own.did(ins)
                    own.settle()

                dve.wait_ge(S("src_in"), 16)
                dve.wait_ge(S("dst_in"), 16)
                dve.tensor_copy(key_b[:], src_i)
                then(dve.tensor_copy(t_a, dst_i))
                yield
                then(TS(t_b, key_b[:], 0.0, float(N_TOK), ALU.is_lt, ALU.mult))
                then(TT(key_b[:], key_b[:], t_b, ALU.add))
                yield
                then(TS(key_b[:], key_b[:], 0.0, LAST, ALU.max, ALU.min))
                TS(src_i, key_b[:], LAST, None, ALU.is_ge)
                TS(t_b, t_a, LAST, None, ALU.is_gt)
                yield
                then(STT(key_a[:], t_a, float(N_TOK), key_b[:], ALU.mult, ALU.add))
                then(STT(dst_i, t_a, 0.0, t_b, ALU.is_lt, ALU.max))
                yield
                then(TS(t_a, t_a, 2.0, CL_BASE, ALU.mult, ALU.add))
                then(dve.copy_predicated(key_a[:], src_i, t_a))
                yield
                then(dve.memset(t_b, BAD))
                then(dve.copy_predicated(key_a[:], dst_i, t_b))
                yield
                TS(t_a, key_a[:], BAD, None, ALU.is_lt)
                then(TS(t_b, key_a[:], CL_BASE, None, ALU.is_lt))
                yield
                then(dve.tensor_reduce(counts[:, 0:1], t_a, X, ALU.add))
                dve.tensor_reduce(counts[:, 1:2], t_b, X, ALU.add).then_inc(S("counts_ready"), 1)
                dve.wait_ge(S("counts_ready"), 1)
                dve.memset(x2_t[D:D + 1, :], 1.0).then_inc(S("x2_ones"), 1)

            def step(source, target, w, mirrored, steps):
                d = w // 2
                hi = source[:, :, w - 1:d - 1:-1] if mirrored and d > 1 else source[:, :, d:w]
                if steps.n:
                    steps.settle()
                TT(target[:, :, 0:d], source[:, :, 0:d], hi, ALU.min)
                steps.did(TT(target[:, :, d:w], source[:, :, 0:d], hi, ALU.max))

            def merges(levels, width, start, steps):
                src, dst = (key_a, key_b) if start is key_a else (key_b, key_a)
                for k in levels:
                    for j in range(k - 1, -1, -1):
                        w = 2 << j
                        blocks = [v[:, 0:width].rearrange("p (b w) -> p b w", w=w) for v in (src, dst)]
                        step(*blocks, w, j == k - 1, steps)
                        src, dst = dst, src
                        yield
                assert src is key_a
                steps.settle()

            def local_sort():
                steps = Own(dve, S("sort_step"))
                yield from merges(range(1, BLOCK_BITS + 1), EC, key_a, steps)
                w = 1 << BLOCK_BITS
                dve.tensor_reduce(counts[:, 2:3], key_a[:].rearrange("p (b w) -> p b w", w=w)[:, :, w // 2:w // 2 + 1]
                                  .rearrange("p b w -> p w b"), X, ALU.min).then_inc(S("blocks_sorted"), 1)
                yield
                dve.wait_ge(S("blocks_saved"), 16)
                pairs = key_a[:].rearrange("p (b w) -> p b w", w=2 * w)
                steps.did(TT(pairs[:, :, 0:w], pairs[:, :, 0:w], pairs[:, :, 2 * w - 1:w - 1:-1], ALU.min))
                yield
                step(pairs[:, :, 0:w], key_b[:, 0:KEPT].rearrange("p (b w) -> p b w", w=w), w, False, steps)
                yield
                src, dst = key_b, key_a
                for j in range(BLOCK_BITS - 2, -1, -1):
                    blocks = [v[:, 0:KEPT].rearrange("p (b w) -> p b w", w=2 << j) for v in (src, dst)]
                    step(*blocks, 2 << j, False, steps)
                    src, dst = dst, src
                    yield
                assert src is key_b
                yield from merges(range(BLOCK_BITS + 1, LOCAL_BITS), KEPT, key_b, steps)

            making, sorting_steps = edge_keys(), local_sort()

            def fill(n):
                for _ in range(n):
                    if next(making, True) is True:
                        next(sorting_steps, None)

            n_var = 0

            def normalise(x, o, last=None):
                nonlocal n_var
                then(dve.tensor_reduce(stat[:, 0, :], x, X, ALU.add))
                then(TS(stat[:, 0, :], stat[:, 0, :], -1.0 / D, None, ALU.mult))
                then(TT(cen[:], x, tall(stat[:, 0, :], D), ALU.add))
                then(TT(sq[:], cen[:], cen[:], ALU.mult))
                then(dve.tensor_reduce(stat[:, 3, :], sq[:], X, ALU.add))
                TS(stat[:, 1, :], stat[:, 3, :], 1.0 / D, LN_EPS, ALU.mult, ALU.add).then_inc(S("var_ready"), 1)
                n_var += 1
                if n_var > 2:
                    fill(1)
                dve.wait_ge(S("rstd_ready"), n_var)
                ins = TT(o, cen[:], tall(stat[:, 2, :], D), ALU.mult)
                if last:
                    ins.then_inc(S(last), 1)
                else:
                    then(ins)

            def across(c, n, mid):
                return par[:, c:c + n].unsqueeze(1).to_broadcast([P, mid, n])

            def token_part(g):
                dve.wait_ge(S("bank_read"), nth[("token", g)])
                t = slice(TG * g, TG * g + TG)
                normalise(h1[:, t, :], sq[:])
                then(TT(sq[:], sq[:], across(B_G, D, TG), ALU.mult))
                own.did(TT(h1[:, t, :], sq[:], across(B_B, D, TG), ALU.add))
                own.settle()
                normalise(h1[:, t, :], h2[:, t, :], "xa_ready")

            def features(g):
                for m in range(4):
                    dve.wait_ge(S("bank_read"), nth[("kq", g, m)])
                    STT(kq[:, m, :], exp_kq[:, m, :], 1.0, relu_kq[:, m, :], ALU.min, ALU.add).then_inc(S("kq_ready"), 1)

            def attended(b):
                dve.wait_ge(S("av_out"), b + 1)
                av = ps[:, 2:4, 0:4 * (D + 1)].rearrange("p m (j e) -> p m j e", j=4)
                d0, d1 = (att_den[:, q, :].rearrange("p (m j) -> p m j", m=2) for q in range(2))
                then(TS(d0, av[:, :, :, D], ATT_EPS, None, ALU.add))
                then(dve.reciprocal(d1, d0))
                dve.tensor_tensor(nv[:], av[:, :, :, 0:D], tall(d1, D), ALU.mult).then_inc(S("av_read"), 1)
                dve.wait_ge(S("av_read"), b + 1)
                then(dve.tensor_reduce(h2[:, b, :], nv[:].rearrange("p m j e -> p e (m j)"), X, ALU.add))
                own.did(TT(h2[:, b, :], h2[:, b, :], h1[:, b, :], ALU.add))

            def second_norm(g):
                own.settle()
                normalise(h2[:, TG * g:TG * g + TG, :], x2[:], "x2_ready")

            def node_part(g):
                t = slice(TG * g, TG * g + TG)
                dve.wait_ge(S("bank_read"), nth[("nodes", g)])
                for c, o in ((B_SRC, tab[:, t, 0:HEADS]), (B_DST, a_dst[:, t, :])):
                    then(TT(prod[:], tab[:, t, HEADS:ROW], across(c, 16, TG), ALU.mult))
                    ins = dve.tensor_reduce(o, prod[:].rearrange("p t (h e) -> p t h e", e=NE_EXP), X, ALU.add)
                    if c == B_DST:
                        ins.then_inc(S("tab_ready"), 1)
                    else:
                        then(ins)

            def chunk_sort(i, later):
                own = Own(dve, S("vec_sort"), -TURNS, i, VEC_SORT) if later else Own(dve, S("vec_sort"))

                def then(ins):
                    own.did(ins)
                    own.settle()

                if later:
                    dve.wait_ge(S("keys_stored"), every(i, 16, 0))
                keys = key_a[:, bass.ds(i * CW, CW)] if later else key_a[:, 0:CW]
                then(TS(ck[1][:], keys, CL_BASE, None, ALU.min))
                then(TS(mirror[:], ck[1][:, ::-1], const[:, C_SIGN + 1:C_SIGN + 2], None, ALU.mult))
                STT(ck[0][:], ck[1][:], const[:, C_SIGN:C_SIGN + 1], mirror[:], ALU.mult, ALU.add)\
                    .then_inc(S("to_columns"), 1)
                yield

                def turned(m):
                    if later:
                        dve.wait_ge(S("in_columns" if m % 2 else "in_rows"), every(i - 1, 7, (m + 1) // 2))
                        then(dve.tensor_copy(mirror[:], ps[:, 7 - m % 2, 0:CW]))
                    else:
                        dve.wait_ge(S("bank_read"), nth[("chunk", m)])

                def steps_of(bits, target, last):
                    source = mirror[:]
                    for j in range(bits - 1, -1, -1):
                        d = 1 << j
                        a, o = (v.rearrange("p (b w) -> p b w", w=2 * d) for v in (source, ck[target][:]))
                        TT(o[:, :, 0:d], a[:, :, 0:d], a[:, :, d:2 * d], ALU.min)
                        ins = TT(o[:, :, d:2 * d], a[:, :, 0:d], a[:, :, d:2 * d], ALU.max)
                        if j == 0 and last:
                            ins.then_inc(S(last), 1)
                        else:
                            then(ins)
                        source, target = ck[target][:], 1 - target
                    return 1 - target

                for k in range(CHUNK_BITS + 1, ALL_BITS + 1):
                    n = k - CHUNK_BITS
                    turned(2 * n - 1)
                    assert steps_of(n, 1, "to_rows") == n % 2
                    yield
                    turned(2 * n)
                    done_ = "chunk_sorted" if k == ALL_BITS else None
                    assert steps_of(CHUNK_BITS, 0, done_) == 1
                    if k < ALL_BITS:
                        TS(ck[0][:], ck[1][:], sign(k), None, ALU.mult).then_inc(S("to_columns"), 1)
                    yield
                assert own.n == (VEC_SORT if later else VEC_SORT - TURNS), own.n

            def later_chunk(i):
                for _ in chunk_sort(i, True):
                    pass

            chunk_steps = chunk_sort(0, False)

            def chunk(*numbers):
                for m in numbers:
                    next(chunk_steps)

            def set_turns():
                dve.wait_ge(S("bank_read"), nth["counts"])
                few = lambda a, b: stat[0:1, 0, a:b]
                row = lambda q: counts_row[:, q * P:(q + 1) * P]
                then(dve.tensor_reduce(few(0, 1), row(0), X, ALU.max))
                then(dve.tensor_reduce(few(1, 2), row(1), X, ALU.max))
                then(dve.tensor_reduce(few(2, 3), row(1), X, ALU.add))
                then(TS(few(0, 2), few(0, 2), 1.0, float(CW - 1), ALU.max, ALU.add))
                then(dve.tensor_copy(n_turns[:, 0:2], few(0, 2)))
                TS(n_turns[:, 0:2], n_turns[:, 0:2], CHUNK_BITS, None, ALU.logical_shift_right).then_inc(S("n_turns_set"), 1)
                dve.wait_ge(S("n_turns_set"), 1)
                then(dve.tensor_copy(few(3, 4), n_turns[:, 1:2]))
                TS(few(2, 3), few(2, 3), float(P * SW), None, ALU.is_le).then_inc(S("n_turns_set"), 1)
                dve.wait_ge(S("n_turns_set"), 2)
                STT(n_turns[:, 2:3], few(3, 4), 2.0, few(2, 3), ALU.mult, ALU.subtract).then_inc(S("n_turns_set"), 1)
                dve.wait_ge(S("n_turns_set"), 3)
                then(dve.tensor_reduce(few(0, 1), row(2), X, ALU.min))
                TS(n_turns[:, 3:4], few(0, 1), BAD, 1.0, ALU.is_lt, ALU.add).then_inc(S("n_turns_set"), 1)
                again = number(dve, 3)
                with dve.If(again > 1):
                    dve.wait_ge(S("blocks_back"), 16)
                    for _ in merges(range(BLOCK_BITS + 1, LOCAL_BITS + 1), EC, key_a, Own(dve, S("again_step"))):
                        pass

            fill(FIRST_FILLS[0])
            token_part(0)
            fill(FIRST_FILLS[1])
            for g in range(NG):
                features(g)
                if g == 1:
                    for _ in making:
                        pass
                if g:
                    attended(TG * g - 1)
                    second_norm(g - 1)
                chunk(*CHUNK_AT_GROUP.get(g, ()))
                if g < NG - 1:
                    token_part(g + 1)
                if g == NG - 2:
                    chunk(3)
                for k in range(TG - 1):
                    b = TG * g + k
                    if b < SORTED_BATCH:
                        fill(FILLS[g])
                    elif b == SORTED_BATCH:
                        fill(LOCAL_BITS * LOCAL_BITS)
                        set_turns()
                    if g and k == 1:
                        node_part(g - 1)
                    attended(b)
                    chunk(*CHUNK_AT.get(b, ()))
                if g * TG + TG - 1 < SORTED_BATCH:
                    fill(FILLS[g])
            attended(NT - 1)
            second_norm(NG - 1)
            chunk(13)
            node_part(NG - 1)
            chunk(14)

            further(dve, 1, later_chunk)

            def node_of(ints, columns, low, high):
                c = slice(0, columns)
                then(TS(ti[:, c], ints[:, c], low, OH - 1, ALU.logical_shift_right, ALU.bitwise_and))
                then(dve.tensor_copy(lb[:, c], ti[:, c]))
                then(TS(ti[:, c], ints[:, c], high, None, ALU.arith_shift_right))
                then(dve.tensor_copy(tb[:, c], ti[:, c]))

            def one_hots(columns, ready):
                for bits, hot in ((lb, oh_lo), (tb, oh_hi)):
                    for j in range(OH):
                        last = TS(hot[:, j, 0:columns], bits[:, 0:columns], float(j), None, ALU.is_equal)
                last.then_inc(S(ready), 1)

            def leaky(o):
                then(STT(o, o, 0.2, o, ALU.mult, ALU.max))

            def masked(part, present, tiles):
                m, s_ = part[:, :, 0:HEADS], part[:, :, HEADS:SROW]
                then(TT(m, m, tall(present, HEADS), ALU.mult))
                then(TS(pos[:, 3, tiles], present, -LOW, LOW, ALU.mult, ALU.add))
                then(TT(m, m, tall(pos[:, 3, tiles], HEADS), ALU.add))
                then(TT(s_, s_, tall(present, NS), ALU.mult))

            s5 = lambda v: v.rearrange("p t (h c) -> p t h c", h=HEADS)

            def merge(part, sent, value):
                m, s_ = part[:, :, 0:HEADS], s5(part[:, :, HEADS:SROW])
                then(TT(new_m[:], acc_m[:], m, ALU.max))
                TT(fade[:, 0], acc_m[:], new_m[:], ALU.subtract)
                TT(fade[:, 1], m, new_m[:], ALU.subtract).then_inc(S("fade_shift"), 1)
                dve.wait_ge(S(sent), value)
                then(dve.tensor_copy(acc_m[:], new_m[:]))
                then(TT(acc_s[:], acc_s[:], tall(fade[:, 0], 1 + NE_EXP), ALU.mult))
                then(TT(s_, s_, tall(fade[:, 1], 1 + NE_EXP), ALU.mult))
                then(TT(acc_s[:], acc_s[:], s_, ALU.add))

            def clamped_counts():
                nonlocal own
                before = own

                def turn(i, later):
                    nonlocal own
                    own = Own(dve, S("vec_hist"), 0, i, VEC_HIST) if later else Own(dve, S("vec_hist"), i * VEC_HIST)
                    keys = key_a[:, bass.ds(i * CW, CW)] if later else key_a[:, i * CW:(i + 1) * CW]
                    then(TS(ki[:], keys, CL_BASE, 2.0 * N_TOK, ALU.subtract, ALU.min))
                    node_of(ki, CW, 1, 7)
                    one_hots(CW, "onehots")
                    dve.wait_ge(S("counted"), every(i, 1, 1))
                    TT(clamped64[:], clamped64[:], ps[0:OH, 2, 0:OH], ALU.add).then_inc(S("clamped_added"), 1)
                    dve.wait_ge(S("clamped_added"), every(i, 1, 1))
                    assert own.n == VEC_HIST, own.n

                for i in range(HIST_TURNS):
                    turn(i, False)
                further(dve, 0, lambda i: turn(i, True), HIST_TURNS)
                own = Own(dve, S("vec_start"))
                dve.tensor_copy(ti[0:OH, 0:OH], clamped64[:]).then_inc(S("clamped_ready"), 1)
                then(dve.memset(chain[:], 0.0))
                dve.wait_ge(S("clamped_out"), 1)
                then(dve.tensor_copy(n_clamped[:], ps[:, 3, P:P + NT]))
                own = before

            def clamped_part():
                nonlocal own
                before = own
                own = Own(dve, S("vec_clamped"))
                then(TT(acc_m[:], tab[:, :, 0:HEADS], a_dst[:], ALU.add))
                leaky(acc_m[:])
                then(dve.memset(acc_s[:], 1.0))
                then(dve.tensor_copy(acc_s[:, :, :, 1:], s5(tab[:, :, HEADS:ROW])))
                dve.wait_ge(S("last_row_in"), 16)
                lr = lambda a, b: last_row[:, a:b].unsqueeze(1).to_broadcast([P, NT, b - a])
                then(TT(clamped[:, :, 0:HEADS], a_dst[:], lr(0, HEADS), ALU.add))
                leaky(clamped[:, :, 0:HEADS])
                p5 = s5(clamped[:, :, HEADS:SROW])
                then(dve.memset(p5[:, :, :, 0:1], 1.0))
                then(dve.tensor_copy(p5[:, :, :, 1:], s5(lr(HEADS, ROW))))
                then(TT(clamped[:, :, HEADS:SROW], clamped[:, :, HEADS:SROW], tall(n_clamped[:], NS), ALU.mult))
                then(TS(hist[:], n_clamped[:], 0.0, None, ALU.is_gt))
                masked(clamped, hist[:], slice(0, NT))
                merge(clamped, "faded", 1)
                dve.wait_ge(S("y_read"), 2 * NG)
                then(TT(y_exp[:], y_exp[:], across(B_B2, NE_EXP * D, NT), ALU.add))
                own = before

            def window(i, later):
                nonlocal own
                own = Own(dve, S("vec_turn"), 0, i, VEC_TURN) if later else Own(dve, S("vec_turn"))
                acted = lambda n: dve.wait_ge(S("act_scan"), every(i, ACT_TURN, n))

                dve.wait_ge(S("window_in"), every(i, 16, 16))
                w = slice(0, SW)
                dve.tensor_copy(ki[:, w], wk[:]).then_inc(S("window_read"), 1)
                dve.wait_ge(S("window_read"), every(i, 1, 1))
                TS(si[:, w], ki[:, w], N_TOK - 1, None, ALU.bitwise_and)
                then(TS(ti[:, w], ki[:, w], 12, None, ALU.logical_shift_right))
                then(dve.tensor_copy(dst_f[:], ti[:, w]))
                TS(i_first[:], dst_f[:, 0:1], LAST, None, ALU.min).then_inc(S("src_ready"), 1)
                node_of(ki, SW, 12, 18)
                one_hots(SW, "onehots2")
                TT(same[:, 1:], dst_f[:, 1:], dst_f[:, :-1], ALU.is_equal)
                then(dve.memset(same[:, 0:1], 1.0))
                then(TS(pen[:], same[:], -LOW, LOW, ALU.mult, ALU.add))
                dve.wait_ge(S("counted2"), every(i, 1, 1))
                dve.tensor_copy(hist64[:], ps[0:OH, 2, 0:OH]).then_inc(S("hist_ready"), 1)
                dve.wait_ge(S("cum_out"), every(i, 1, 1))
                then(TS(nonempty[:], ps[:, 3, 0:NT], 0.0, None, ALU.is_gt))
                then(dve.tensor_copy(hist[:], ps[:, 3, 0:NT]))
                then(dve.tensor_copy(pos[:, 0, :], ps[:, 3, 96:96 + NT]))
                then(dve.tensor_tensor_scan(pos[:, 1, :], ones[:, 0:NT], pos[:, 0, :], 0.0, ALU.mult, ALU.add))
                then(TT(pos[:, 1, :], pos[:, 1, :], pos[:, 0, :], ALU.subtract))
                then(TT(pos[:, 1, :], pos[:, 1, :], ps[:, 3, 64:64 + NT], ALU.add))
                TT(pos[:, 2, :], pos[:, 1, :], hist[:], ALU.subtract)
                then(TS(i_end[:], pos[:, 1, :], 1.0, 0.0, ALU.subtract, ALU.max))
                then(TS(pos[:, 3, :], nonempty[:], -OOB, OOB, ALU.mult, ALU.add))
                TT(i_start[:], pos[:, 2, :], pos[:, 3, :], ALU.add).then_inc(S("pos_ready"), 1)
                if not later:
                    clamped_counts()

                TS(e_new[:, 0, :], same[:], -1.0, 1.0, ALU.mult, ALU.add).then_inc(S("hot_free"), 1)
                dve.wait_ge(S("ad_in"), every(i, 16, 16))
                dve.wait_ge(S("ad_first_in"), every(i, 16, 16))
                then(TT(ad_at, ad_at, tall(e_new[:, 0, :], HEADS), ALU.mult))
                for h in range(HEADS):
                    ins = dve.tensor_tensor_scan(e_ad[:, h, :], same[:], ad_at[:, :, h], ad_first[:, h:h + 1], ALU.mult, ALU.add)
                then(ins)

                turn_f = lambda v: v.rearrange("p f h -> p h f")
                m_run = turn_f(seg[:, :, 0:HEADS])
                h_all = rows[:, :, HEADS:ROW].rearrange("p f (h c) -> p f h c", h=HEADS)
                flat_w = e_w.rearrange("p h f -> p f h")
                for q in range(GROUPS):
                    c = slice(q * GC, (q + 1) * GC)
                    before = q * GC - 1
                    dve.wait_ge(S(f"rows_in{q}"), every(i, 16 * GC, 16 * GC))
                    then(TT(e_val[:, :, c], turn_f(rows[:, c, 0:HEADS]), e_ad[:, :, c], ALU.add))
                    leaky(e_val[:, :, c])
                    for h in range(HEADS):
                        ins = dve.tensor_tensor_scan(seg[:, c, h], pen[:, c], e_val[:, h, c],
                                                     seg[:, before:before + 1, h] if q else LOW, ALU.add, ALU.max)
                    then(ins)
                    TT(e_w[:, :, c], e_val[:, :, c], m_run[:, :, c], ALU.subtract)
                    if q:
                        then(TT(e_a[:, :, c], m_run[:, :, before:before + GC], m_run[:, :, c], ALU.subtract))
                    else:
                        dve.memset(e_a[:, :, 0:1], 0.0)
                        then(TT(e_a[:, :, 1:GC], m_run[:, :, 0:GC - 1], m_run[:, :, 1:GC], ALU.subtract))
                    TS(e_a[:, :, c], e_a[:, :, c], 0.0, None, ALU.min).then_inc(S("shift_ready"), 1)
                    acted(q + 1)
                    TT(e_a[:, :, c], e_a[:, :, c], same[:, c].unsqueeze(1).to_broadcast([P, HEADS, GC]), ALU.mult)
                    h_of = h_all[:, c]
                    then(TT(h_of, h_of, tall(flat_w[:, c], NE_EXP), ALU.mult))
                    for h in range(HEADS):
                        for x in range(1 + NE_EXP):
                            v = e_w[:, h, c] if x == 0 else h_of[:, :, h, x - 1]
                            r = HEADS + h * (1 + NE_EXP) + x
                            ins = dve.tensor_tensor_scan(seg[:, c, r], e_a[:, h, c], v,
                                                         seg[:, before:before + 1, r] if q else 0.0, ALU.mult, ALU.add)
                    ins.then_inc(S("seg_ready"), 1)
                    dve.wait_ge(S("seg_ready"), every(i, GROUPS, q + 1))

                five = lambda v: v.rearrange("p (h c) -> p h c", h=HEADS)
                dve.tensor_copy(five(ends[:, 0, :]), tall(seg[:, SW - 1, 0:HEADS], 5))
                dve.tensor_copy(ends[:, 1, :], seg[:, SW - 1, HEADS:SROW])
                dve.tensor_copy(ends[:, 2, :], dst_f[:, 0:1].to_broadcast([P, NS]))
                dve.tensor_copy(ends[:, 3, :], dst_f[:, SW - 1:SW].to_broadcast([P, NS])).then_inc(S("ends_ready"), 1)
                dve.wait_ge(S("ends_turned"), every(i, 1, 1))
                e_m, e_s = ps[0:NS, 6, 0:P], ps[0:NS, 6, P:2 * P]
                c_ = lambda q: chain[0:NS, q, :]
                dve.tensor_copy(c_(0), ps[0:NS, 6, 2 * P:3 * P])
                then(dve.tensor_copy(c_(1), ps[0:NS, 6, 3 * P:4 * P]))
                TT(c_(8)[:, :-1], c_(0)[:, :-1], c_(0)[:, 1:], ALU.is_equal)
                then(TT(c_(2)[:, 1:], c_(1)[:, :-1], c_(0)[:, 1:], ALU.is_equal))
                STT(c_(8)[:, :-1], c_(8)[:, :-1], OOB, c_(0)[:, :-1], ALU.mult, ALU.add)
                dve.tensor_copy(c_(8)[:, P - 1:P], c_(0)[:, P - 1:P])
                then(TT(c_(3), c_(1), c_(0), ALU.is_equal))
                then(TT(c_(3), c_(3), c_(2), ALU.mult))
                then(TS(c_(5), c_(3), -LOW, LOW, ALU.mult, ALU.add))
                then(dve.tensor_tensor_scan(c_(6), c_(5), e_m, LOW, ALU.add, ALU.max))
                TT(c_(5), e_m, c_(6), ALU.subtract)
                then(TT(c_(4)[:, 1:], c_(6)[:, :-1], c_(6)[:, 1:], ALU.subtract))
                then(dve.memset(c_(4)[:, 0:1], 0.0))
                TS(c_(4), c_(4), 0.0, None, ALU.min).then_inc(S("chain_shift"), 1)
                acted(GROUPS + 1)
                TT(c_(4), c_(4), c_(3), ALU.mult)
                then(TT(c_(5), c_(5), e_s, ALU.mult))
                then(dve.tensor_tensor_scan(c_(7), c_(4), c_(5), 0.0, ALU.mult, ALU.add))
                then(TS(c_(3), c_(2), -LOW, LOW, ALU.mult, ALU.add))
                dve.memset(c_(1)[:, 0:1], 0.0)
                dve.memset(c_(0)[:, 0:1], LOW)
                TT(c_(1)[:, 1:], c_(7)[:, :-1], c_(2)[:, 1:], ALU.mult)
                then(TT(c_(0)[:, 1:], c_(6)[:, :-1], c_(2)[:, 1:], ALU.mult))
                TT(c_(0)[:, 1:], c_(0)[:, 1:], c_(3)[:, 1:], ALU.add).then_inc(S("chain_ready"), 1)
                dve.wait_ge(S("carry_out"), every(i, 1, 1))
                then(dve.tensor_copy(carry[:, 0:HEADS], five(ps[:, 7, 0:NS])[:, :, 0]))
                then(dve.tensor_copy(carry[:, HEADS:SROW], ps[:, 7, P:P + NS]))
                dve.tensor_copy(i_carry[:], ps[:, 7, 2 * P:2 * P + 1]).then_inc(S("carry_ready"), 1)

                if not later:
                    clamped_part()
                dve.wait_ge(S("carry_in"), every(i, 16, 16))
                merge(carried, "act_scan", every(i, ACT_TURN, GROUPS + 2))
                for n, tiles in enumerate((slice(0, FIRST_PULLED), slice(FIRST_PULLED, NT))):
                    size = tiles.stop - tiles.start
                    dve.wait_ge(S(f"pulled_in{n}"), every(i, 16 * size, 16 * size))
                    masked(pulled[:, tiles], nonempty[:, tiles], tiles)
                merge(pulled, "act_scan", every(i, ACT_TURN, GROUPS + 3))
                dve.memset(c_(2)[:, 0:1], 0.0).then_inc(S("turn_done"), 1)
                dve.wait_ge(S("turn_done"), every(i, 1, 1))
                assert own.n == VEC_TURN, own.n

            own = Own(dve, S("vec_between"))
            then(dve.memset(clamped64[:], 0.0))
            window(0, False)
            further(dve, 2, lambda i: window(i, True))

            own = Own(dve, S("vec_end"))
            heads4 = lambda v: v.rearrange("p t (h c) -> p t h c", h=HEADS)
            then(TS(new_m[:], acc_s[:, :, :, 0], 1e-16, None, ALU.add))
            then(dve.reciprocal(new_m[:], new_m[:]))
            then(TT(heads4(agg), acc_s[:, :, :, 1:], tall(new_m[:], NE_EXP), ALU.mult))
            then(TT(agg, agg, across(B_GAT, 16, NT), ALU.add))
            then(dve.tensor_reduce(gate[:, 0, :], agg, X, ALU.add))
            then(TS(gate[:, 0, :], gate[:, 0, :], -1.0 / 16, None, ALU.mult))
            then(TT(agg2, agg, tall(gate[:, 0, :], 16), ALU.add))
            then(TT(agg, agg2, agg2, ALU.mult))
            then(dve.tensor_reduce(gate[:, 0, :], agg, X, ALU.add))
            TS(gate[:, 1, :], gate[:, 0, :], 1.0 / 16, LN_EPS, ALU.mult, ALU.add).then_inc(S("var_ready"), 1)
            rank = gate[:, 12:16, :]
            for x in range(NE_EXP):
                ins = dve.memset(rank[:, x, :], float(x))
            then(ins)
            dve.wait_ge(S("root_ready"), 1)
            then(dve.reciprocal(gate[:, 2, :], gate[:, 2, :]))
            then(TT(agg, agg2, tall(gate[:, 2, :], 16), ALU.mult))
            then(TT(agg, agg, across(B_LG, 16, NT), ALU.mult))
            then(TT(agg, agg, across(B_LB, 16, NT), ALU.add))
            score = gate[:, 4:8, :]
            then(dve.tensor_reduce(score.rearrange("p e t -> p t e"), agg.rearrange("p t (h e) -> p t e h", h=HEADS), X, ALU.add))
            then(TS(score, score, 1.0 / HEADS, None, ALU.mult))
            then(dve.tensor_reduce(gate[:, 1, :], score.rearrange("p e t -> p t e"), X, ALU.max))
            soft = gate[:, 8:12, :]
            TT(soft, score, gate[:, 1, :].unsqueeze(1).to_broadcast([P, NE_EXP, NT]), ALU.subtract).then_inc(S("soft_shift"), 1)
            ahead = agg2.rearrange("p t c -> p (t c)").rearrange("p (x t) -> p x t", t=NT)
            pairs = [(o, ahead[:, NE_EXP * (o - 1):NE_EXP * o - o, :]) for o in range(1, NE_EXP)]
            for o, higher in pairs:
                ins = TT(higher, score[:, o:, :], score[:, :NE_EXP - o, :], ALU.is_gt)
            then(ins)
            for o, higher in pairs:
                then(TT(rank[:, :NE_EXP - o, :], rank[:, :NE_EXP - o, :], higher, ALU.add))
                then(TT(rank[:, o:, :], rank[:, o:, :], higher, ALU.subtract))
            then(TS(rank, rank, 2.0, None, ALU.is_lt))
            dve.wait_ge(S("soft_exp"), 1)
            then(TT(soft, soft, rank, ALU.mult))
            then(dve.tensor_reduce(gate[:, 1, :], soft.rearrange("p e t -> p t e"), X, ALU.add))
            then(dve.reciprocal(gate[:, 1, :], gate[:, 1, :]))
            TT(soft, soft, gate[:, 1, :].unsqueeze(1).to_broadcast([P, NE_EXP, NT]), ALU.mult).then_inc(S("gates_ready"), 1)
            dve.wait_ge(S("gates_ready"), 1)
            for tiles in RESULT_VEC:
                gated(TT, tiles, own).then_inc(S("result"), 1)


def kernel(**inputs):
    import numpy as np
    import concourse.bacc as bacc
    from concourse.bass_utils import run_bass_kernel_spmd as run

    v = {k: np.asarray(a) for k, a in inputs.items()}
    p = np.arange(P)
    const = np.zeros((P, C_WIDTH), np.float32)
    const[:, C_ID:C_ID + P] = np.eye(P)
    const[:, C_TRI:C_TRI + P] = p[:, None] <= p[None, :]
    const[:, C_ONE:C_ONE + P] = 1
    const[0:OH, C_ID1:C_ID1 + P] = const[OH:, C_ID:C_ID + P]
    const[0:OH, C_TRI1:C_TRI1 + P] = const[OH:, C_TRI:C_TRI + P]
    sgn = {k: 1 - 2 * ((p >> (k - CHUNK_BITS)) & 1) for k in range(CHUNK_BITS + 1, ALL_BITS + 1)}
    const[:, C_SIGN] = sgn[9] * (p % 2 == 0)
    const[:, C_SIGN + 1] = sgn[9] * (p % 2 == 1)
    for k in range(CHUNK_BITS + 1, ALL_BITS):
        const[:, C_SIGN + k - CHUNK_BITS + 1] = sgn[k] * sgn[k + 1]
    ffn = lambda n: v["L0_ffn_" + n]
    tok = lambda n: v["L0_tok_" + n]
    attn = lambda n: v["L0_attn_" + n]
    par = np.concatenate([a.ravel() for a in (
        tok("ln_g"), tok("ln_b"), ffn("att_src"), ffn("att_dst"), ffn("b_gat"), ffn("ln_gamma"), ffn("ln_beta"),
        ffn("b2"), tok("W_o"), tok("W_dt"))])[None, :]
    columns = lambda w: w.transpose(1, 0, 2).reshape(D, -1)
    arrays = {
        "idx": v["x"].T,
        "src": v["L0_ffn_edge_index"][0].reshape(P, EC),
        "dst": v["L0_ffn_edge_index"][1].reshape(P, EC),
        "const": const,
        "par": par,
        "outcomes": v["fside_BS_outcomes"],
        "times": v["fside_BS_timestamps"],
        "h_q": tok("h_q"),
        "w_tok": np.concatenate([tok("W_proj_w").T, tok("W_proj_b")[None, :]]),
        "w_kq": np.concatenate([columns(attn("Wks")), columns(attn("Wqs"))], axis=1),
        "w_vt": attn("Wvs").transpose(2, 0, 1).reshape(D, -1),
        "w_o": columns(attn("Wo")),
        "w_hid": np.concatenate([columns(ffn("W1")), ffn("b1").reshape(1, -1)]),
        "w_outp": ffn("W2").transpose(1, 0, 2).reshape(HID, -1),
        "w_gat": ffn("W_gat"),
        "zeros": np.zeros((1, SW * HEADS), np.float32),
        "no_carry": np.tile(np.array([LOW] * HEADS + [0.0] * NS, np.float32), NT)[None, :],
        "no_keys": np.full((1, PITCH - P * CW), CL_BASE, np.float32),
    }
    arrays = {k: np.ascontiguousarray(a) for k, a in arrays.items()}
    nc = bacc.Bacc("TRN2", target_bir_lowering=False, num_devices=1)
    A = {k: nc.dram_tensor("in_" + k, a.shape, mybir.dt.from_np(a.dtype), kind="ExternalInput").ap()
         for k, a in arrays.items()}
    out = nc.dram_tensor("out", (NT, P, D), F32, kind="ExternalOutput").ap()
    build(nc, A, out)
    r = run(nc, [{"in_" + k: a for k, a in arrays.items()}], core_ids=[0])
    return r.results[0]["out"]
```
